# Optimizing a Trainium2 kernel written in Bass

```python
import numpy as np
import jax
import jax.numpy as jnp

def _softmax(x, axis=-1):
    return jax.nn.softmax(x, axis=axis)

def _gelu(x):
    return jax.nn.gelu(x, approximate=True)

def _silu(x):
    return jax.nn.silu(x)

def _sigmoid(x):
    return jax.nn.sigmoid(x)

def _layernorm(x, axis=-1, eps=1e-05):
    m = jnp.mean(x, axis=axis, keepdims=True)
    v = jnp.var(x, axis=axis, keepdims=True)
    return (x - m) / jnp.sqrt(v + eps)

def _scatter_add(tgt, idx, src, axis=0):
    return tgt.at[idx].add(src)

def _segment_sum(src, seg, n):
    return jax.ops.segment_sum(src, seg, n)
kernel_name = 'mk_hybrid_d1_jaxref_r8_adfbde'

def setup_inputs(seed: int=0):
    np.random.seed(seed)
    _w = jnp.asarray

    def _L0_attn_a_setup():
        import jax, jax.numpy as jnp
        import numpy as np
        HEADS = 8
        K_SIZE = 64
        key = jax.random.key(seed)
        k1, k2, k3, k4 = jax.random.split(key, 4)
        B, C, D = (4, 256, 128)
        return {'x': jax.random.normal(k1, (B, C, D), dtype=jnp.float32), 'Mq': jax.random.normal(k2, (D, HEADS * K_SIZE), dtype=jnp.float32) * 0.02, 'Mk': jax.random.normal(k3, (D, HEADS * K_SIZE), dtype=jnp.float32) * 0.02, 'Mv': jax.random.normal(k4, (D, 128), dtype=jnp.float32) * 0.02}
    _L0_attn_a_in = _L0_attn_a_setup()

    def _L0_attn_b_setup():
        import jax, jax.numpy as jnp
        import numpy as np
        N_HEAD = 16
        PAGE_SIZE = 32
        ROPE_THETA = 10000.0

        def _rope_tables(T, D, dtype):
            inv = 1.0 / ROPE_THETA ** (np.arange(0, D, 2, dtype=np.float32) / D)
            ang = np.outer(np.arange(T, dtype=np.float32), inv)
            return (jnp.asarray(np.cos(ang), dtype), jnp.asarray(np.sin(ang), dtype))

        def _apply_rope(x, cos, sin):
            x1 = x[..., 0::2]
            x2 = x[..., 1::2]
            c = cos[None, :, None, :]
            s = sin[None, :, None, :]
            out = jnp.stack([x1 * c - x2 * s, x1 * s + x2 * c], axis=-1)
            return out.reshape(x.shape)
        key = jax.random.key(seed)
        ks = jax.random.split(key, 6)
        B, T, E = (2, 256, 128)
        L = E // 2
        sc = lambda fan: 1.0 / np.sqrt(fan)
        return {'x': jax.random.normal(ks[0], (B, T, E), jnp.float32), 'wq': jax.random.normal(ks[1], (E, E), jnp.float32) * sc(E), 'w_down': jax.random.normal(ks[2], (E, L), jnp.float32) * sc(E), 'wk_up': jax.random.normal(ks[3], (L, E), jnp.float32) * sc(L), 'wv_up': jax.random.normal(ks[4], (L, E), jnp.float32) * sc(L), 'wo': jax.random.normal(ks[5], (E, E), jnp.float32) * sc(E)}
    _L0_attn_b_in = _L0_attn_b_setup()

    def _L0_ffn_setup():
        import jax, jax.numpy as jnp
        import numpy as np
        D_MODEL = 128
        MLP_DIM = 512
        N_EXPERTS = 8
        B, T = (4, 128)
        key = jax.random.key(seed)
        ks = jax.random.split(key, 7)
        scale_in = (1.0 / D_MODEL) ** 0.5
        scale_out = (1.0 / MLP_DIM) ** 0.5
        bound_g = (1.0 / D_MODEL) ** 0.5
        w_gate = jax.random.uniform(ks[0], (D_MODEL, N_EXPERTS), minval=-bound_g, maxval=bound_g, dtype=jnp.float32)
        b_gate = jax.random.uniform(ks[1], (N_EXPERTS,), minval=-bound_g, maxval=bound_g, dtype=jnp.float32)
        W1 = jax.random.uniform(ks[2], (N_EXPERTS, D_MODEL, MLP_DIM), minval=-scale_in, maxval=scale_in, dtype=jnp.float32)
        b1 = jnp.zeros((N_EXPERTS, MLP_DIM), dtype=jnp.float32)
        W2 = jax.random.uniform(ks[3], (N_EXPERTS, MLP_DIM, D_MODEL), minval=-scale_out, maxval=scale_out, dtype=jnp.float32)
        b2 = jnp.zeros((N_EXPERTS, D_MODEL), dtype=jnp.float32)
        x = jax.random.normal(ks[4], (B, T, D_MODEL), dtype=jnp.float32)
        return {'x': x, 'w_gate': w_gate, 'b_gate': b_gate, 'W1': W1, 'b1': b1, 'W2': W2, 'b2': b2}
    _L0_ffn_in = _L0_ffn_setup()
    _d = {'L0_attn_a_x': _L0_attn_a_in['x'], 'L0_attn_a_Mq': _L0_attn_a_in['Mq'], 'L0_attn_a_Mk': _L0_attn_a_in['Mk'], 'L0_attn_a_Mv': _L0_attn_a_in['Mv'], 'L0_attn_b_wq': _L0_attn_b_in['wq'], 'L0_attn_b_w_down': _L0_attn_b_in['w_down'], 'L0_attn_b_wk_up': _L0_attn_b_in['wk_up'], 'L0_attn_b_wv_up': _L0_attn_b_in['wv_up'], 'L0_attn_b_wo': _L0_attn_b_in['wo'], 'L0_ffn_w_gate': _L0_ffn_in['w_gate'], 'L0_ffn_b_gate': _L0_ffn_in['b_gate'], 'L0_ffn_W1': _L0_ffn_in['W1'], 'L0_ffn_b1': _L0_ffn_in['b1'], 'L0_ffn_W2': _L0_ffn_in['W2'], 'L0_ffn_b2': _L0_ffn_in['b2']}
    _x0 = _d['L0_attn_a_x']
    _d['L0_attn_a_x'] = jax.random.normal(jax.random.fold_in(jax.random.key(seed), 1), (8, 256, 128), dtype=_x0.dtype)
    del _x0
    return _d

def reference(L0_attn_a_x, L0_attn_a_Mq, L0_attn_a_Mk, L0_attn_a_Mv, L0_attn_b_wq, L0_attn_b_w_down, L0_attn_b_wk_up, L0_attn_b_wv_up, L0_attn_b_wo, L0_ffn_w_gate, L0_ffn_b_gate, L0_ffn_W1, L0_ffn_b1, L0_ffn_W2, L0_ffn_b2):

    def _L0_attn_a_ref(x, Mq, Mk, Mv):
        import jax, jax.numpy as jnp
        import numpy as np
        HEADS = 8
        K_SIZE = 64
        B, C, _ = x.shape
        H, K = (HEADS, K_SIZE)
        V = Mv.shape[1] // H
        q = (x @ Mq).reshape(B, H, C, K)
        k = (x @ Mk).reshape(B, H, C, K)
        v = (x @ Mv).reshape(B, H, C, V)
        scores = jnp.einsum('bhqk,bhck->bhqc', q, k).reshape(B * H, C, C)
        att = jax.nn.softmax(scores / jnp.sqrt(jnp.float32(K)), axis=1)
        att4 = att.reshape(B, C, H, C)
        out = jnp.einsum('bqhc,bhcd->bqhd', att4, v)
        return out.reshape(B, C, H * V)

    def _L0_attn_b_ref(x, wq, w_down, wk_up, wv_up, wo):
        import jax, jax.numpy as jnp
        import numpy as np
        N_HEAD = 16
        PAGE_SIZE = 32
        ROPE_THETA = 10000.0

        def _rope_tables(T, D, dtype):
            inv = 1.0 / ROPE_THETA ** (np.arange(0, D, 2, dtype=np.float32) / D)
            ang = np.outer(np.arange(T, dtype=np.float32), inv)
            return (jnp.asarray(np.cos(ang), dtype), jnp.asarray(np.sin(ang), dtype))

        def _apply_rope(x, cos, sin):
            x1 = x[..., 0::2]
            x2 = x[..., 1::2]
            c = cos[None, :, None, :]
            s = sin[None, :, None, :]
            out = jnp.stack([x1 * c - x2 * s, x1 * s + x2 * c], axis=-1)
            return out.reshape(x.shape)
        B, T, E = x.shape
        H = N_HEAD
        D = E // H
        q = (x @ wq).reshape(B, T, H, D)
        lat = x @ w_down
        k = (lat @ wk_up).reshape(B, T, H, D)
        v = (lat @ wv_up).reshape(B, T, H, D)
        cos, sin = _rope_tables(T, D, x.dtype)
        q = _apply_rope(q, cos, sin)
        k = _apply_rope(k, cos, sin)
        scale = 1.0 / jnp.sqrt(jnp.asarray(D, x.dtype))
        scores = jnp.einsum('bqhd,bkhd->bhqk', q, k) * scale
        pages = jnp.arange(T) // PAGE_SIZE
        allowed = pages[None, :] <= pages[:, None]
        scores = jnp.where(allowed[None, None], scores, jnp.finfo(scores.dtype).min)
        attn = jax.nn.softmax(scores, axis=-1)
        out = jnp.einsum('bhqk,bkhd->bqhd', attn, v).reshape(B, T, E)
        return out @ wo

    def _L0_ffn_ref(x, w_gate, b_gate, W1, b1, W2, b2):
        import jax, jax.numpy as jnp
        import numpy as np
        D_MODEL = 128
        MLP_DIM = 512
        N_EXPERTS = 8
        B, T = (4, 128)
        b, t, d = x.shape
        x_flat = x.reshape(b * t, d)
        logits = x_flat @ w_gate + b_gate
        probs = jax.nn.softmax(logits, axis=-1)
        route_p = jnp.max(probs, axis=-1)
        route_idx = jnp.argmax(probs, axis=-1)
        h = jnp.einsum('nd,edm->enm', x_flat, W1) + b1[:, None, :]
        h = jax.nn.relu(h)
        y = jnp.einsum('enm,emd->end', h, W2) + b2[:, None, :]
        n = b * t
        out = y[route_idx, jnp.arange(n)] * route_p[:, None]
        return out.reshape(b, t, d)
    x = L0_attn_a_x
    x = x + _L0_attn_a_ref(_layernorm(x, axis=-1), L0_attn_a_Mq, L0_attn_a_Mk, L0_attn_a_Mv)
    x = x + _L0_ffn_ref(_layernorm(x, axis=-1), L0_ffn_w_gate, L0_ffn_b_gate, L0_ffn_W1, L0_ffn_b1, L0_ffn_W2, L0_ffn_b2)
    x = x + _L0_attn_b_ref(_layernorm(x, axis=-1), L0_attn_b_wq, L0_attn_b_w_down, L0_attn_b_wk_up, L0_attn_b_wv_up, L0_attn_b_wo)
    x = x + _L0_ffn_ref(_layernorm(x, axis=-1), L0_ffn_w_gate, L0_ffn_b_gate, L0_ffn_W1, L0_ffn_b1, L0_ffn_W2, L0_ffn_b2)
    return x

_drawn_inputs = setup_inputs


def setup_inputs(seed=0):
    import zlib

    import numpy as np

    out = dict(_drawn_inputs(seed))
    spreads = {'L0_ffn_b1': (0.0, 0.379), 'L0_ffn_b2': (0.0, 0.1)}
    factors = {'L0_attn_a_Mq': 8.0, 'L0_attn_a_Mk': 8.0}
    for name, (base, spread) in spreads.items():
        noise = np.random.default_rng([zlib.crc32(name.encode()), seed]).standard_normal(out[name].shape)
        drawn = base * np.exp(spread * noise) if base else spread * noise
        out[name] = jnp.asarray(drawn.astype(out[name].dtype))
    for name, factor in factors.items():
        out[name] = (out[name] * factor).astype(out[name].dtype)
    return out
```

```python
from contextlib import ExitStack

import numpy as np

import concourse.bass as bass
from concourse import mybir

ALU = mybir.AluOpType
ACT = mybir.ActivationFunctionType
AX = mybir.AxisListType
F32 = mybir.dt.float32
BF16 = mybir.dt.bfloat16
I32 = mybir.dt.int32
U32 = mybir.dt.uint32

P = 128
D = 128
B = 8
T = 256
NT = B * T // P
EPS = 1e-5

HA = 8
KA = 64
VA = D // HA
RT = T // HA
SCALE_A = 1.0 / 8.0

NE = 8
MLP = 512
MC = MLP // P
SLOTS = NT + NE - 1

HB = 16
DB = D // HB
LAT = 64
PAGE = 32
NPG = T // PAGE
SCALE_B = float(1.0 / np.sqrt(np.float32(DB)))
MASKED = -1e30


class Chain:

    def __init__(self, eng, sem):
        self.eng, self.sem, self.base, self.k = eng, sem, 0, 0

    def inc(self, ins):
        ins.then_inc(self.sem, 1)
        self.k += 1

    def wait(self):
        self.eng.wait_ge(self.sem, self.base + self.k)

    def link(self, ins):
        self.inc(ins)
        self.wait()

    def restart(self, base):
        self.base, self.k = base, 0


def build(nc, x_in, Mq_in, Mk_in, Mv_in, wq_in, wdown_in, wkup_in, wvup_in, wo_in,
          wg_in, bg_in, W1_in, b1_in, W2_in, b2_in, cst_in, sel_in, out, xs_dram, ys_dram):
    with ExitStack() as ctx:
        def sb(name, shape, dt=F32):
            return ctx.enter_context(nc.sbuf_tensor(name, shape, dt))

        def sem(name):
            return ctx.enter_context(nc.semaphore(name))

        x = sb("x", [P, NT, D])
        xn = sb("xn", [P, NT, D])
        xnT = sb("xnT", [D, NT, P])
        cst = sb("cst", [P, NCST])
        def const(name):
            a, b = CST[name]
            return cst[:, a:b]
        ident = const("ident")
        stat = sb("stat", [P, NT, 6])
        mv = sb("mv", [P, NT, 2])
        rstd = sb("rstd", [P, 2, NT])
        Mq = sb("Mq", [D, HA * KA])
        Mk = sb("Mk", [D, HA * KA])
        Mv = sb("Mv", [D, HA * VA])
        xb = sb("xb", [D, 2, T])
        QT = sb("QT", [P, 2, HA, P])
        KT = sb("KT", [P, 2, 2, 4, HA, RT])
        Va = sb("Va", [P, 2, 2, HA * VA])
        E = sb("E", [P, 4, 2, 2, T])
        nmax = sb("nmax", [P, 4, 4])
        den = sb("den", [P, 4, 4])
        rden = sb("rden", [P, 4, 4])
        vs = sb("vs", [P, 4, 2, 2, HA * VA])
        OT = sb("OT", [P, 2, 2, 4, RT])

        W1 = sb("W1", [D, NE, MLP])
        W2 = sb("W2", [P, NE, MC, D])
        b1 = sb("b1", [P, NE, MLP])
        b2 = sb("b2", [P, NE, D])
        wg = sb("wg", [D, NE])
        bg = sb("bg", [P, NE])
        zeros = sb("zeros", [P, D])
        lg = sb("lg", [P, NT, NE])
        lmax = sb("lmax", [P, NT])
        lsub = sb("lsub", [P, NT, NE])
        lexp = sb("lexp", [P, NT, NE])
        route_p = sb("route_p", [P, 2, NT])
        cand = sb("cand", [P, NT, NE])
        cmax = sb("cmax", [P, NT])
        onehot = sb("onehot", [P, NE, NT])
        count = sb("count", [P, NE, NT])
        above = sb("above", [P, NE, NT])
        tiles = sb("tiles", [P, 4, NE])
        place = sb("place", [P, NE, NT])
        pos_f = sb("pos_f", [P, NT])
        pos = sb("pos", [P, NT], U32)
        past = sb("past", [P, SLOTS, NE])
        expert_f = sb("expert_f", [P, SLOTS])
        expert = sb("expert", [P, SLOTS], I32)
        xg = sb("xg", [P, 2, D])
        xgT = sb("xgT", [D, 2, P])
        hb = sb("hb", [P, 2, MLP])
        hT = sb("hT", [P, 2, MC, P])
        yo = sb("yo", [P, 2, D])
        yg = sb("yg", [P, NT, D])

        sel = sb("sel", [P, HB, P], BF16)
        identb = sb("identb", [P, P], BF16)
        wq = sb("wq", [D, HB * DB])
        wdown = sb("wdown", [D, LAT])
        wkv = sb("wkv", [LAT, 2 * D])
        wo = sb("wo", [D, D])
        latT = sb("latT", [LAT, T])
        turn = sb("turn", [P, 2, 2, 2, D])
        rest = sb("rest", [P, 2, 2, D])
        rest2 = sb("rest2", [P, 2, 2, D])
        qs = sb("qs", [P, 2, HB, 64], BF16)
        ks = sb("ks", [P, 2, HB, 64], BF16)
        vst = sb("vst", [P, 2, D])
        Vb = sb("Vb", [P, 2, 2, HB, 32])
        nm = sb("nm", [P, 2, HB])
        nmr = sb("nmr", [P, 2, HB])
        ms = sb("ms", [P, 2, P], BF16)
        mT = sb("mT", [P, 2, P], BF16)
        OTb = sb("OTb", [P, 2, 4, T])
        rsum = sb("rsum", [P, 2, HB])
        att = sb("att", [P, 2, D])
        attT = sb("attT", [D, 2, P])
        qT = QT[:, :, :, :].rearrange("p a j t -> p (a j t)").bitcast(BF16).rearrange(
            "p (a n t) -> p a n t", a=2, t=T)
        kT = KT[:, :, :, :, :, :].rearrange("p a h s j i -> p (a h s j i)").bitcast(BF16).rearrange(
            "p (a n h t) -> p a n h t", a=2, h=2, t=T)
        Eb = E[:, :, :, :, :].rearrange("p s h c q -> p (s h c q)")[:, 0:2 * 3 * 512].rearrange(
            "p (a k c) -> p a k c", a=2, c=512)

        pb = [ctx.enter_context(nc.psum_tensor(f"bank{i}", [P, 512], F32)) for i in range(4)]
        S4 = ctx.enter_context(nc.psum_tensor("S4", [P, 4, 512], F32))
        S = [S4[:, 0:2, :], S4[:, 2:4, :]]

        loaded = sem("loaded")
        x_loaded = sem("x_loaded")
        stored = sem("stored")

        norm = []
        for n in range(4):
            norm.append({k: sem(f"n{n}_{k}") for k in
                         ("stats", "mv", "vareps", "rstd", "xn", "xt", "xnT")})
        a_zero = sem("a_zero")
        a_xb = sem("a_xb")
        a_proj = sem("a_proj")
        a_evd = sem("a_evd")
        a_eva = sem("a_eva")
        a_scores = sem("a_scores")
        a_max = sem("a_max")
        a_exp = sem("a_exp")
        a_rden = sem("a_rden")
        a_vs = sem("a_vs")
        a_av = sem("a_av")
        a_ot = sem("a_ot")
        a_f = sem("a_f")
        a_x = sem("a_x")

        ffn = []
        for n in range(2):
            ffn.append({k: sem(f"f{n}_{k}") for k in
                        ("logits", "chain", "exp", "counts", "totals", "pos", "table", "scattered",
                         "in0", "in1", "xt", "xgT", "h", "hb", "ht", "hT", "y", "yo",
                         "out0", "out1", "back0", "back1", "back2", "back3", "x")})
        bs = {k: sem(f"b_{k}") for k in
              ("const", "zero", "xb", "p1", "latT", "turnq", "p2", "turnk", "v", "vb", "chain", "split", "tq", "qT", "tk",
               "kTlow", "kThigh", "s", "max", "mchain", "ms", "mt", "mT", "st", "exp", "pv", "ot", "on", "rsum", "att",
               "at", "attT", "y", "x")}
        b_loaded = sem("b_loaded")
        sel_loaded = sem("sel_loaded")
        w_loaded = sem("w_loaded")
        pool_const = sem("pool_const")
        slots_zero = sem("slots_zero")

        block = ctx.enter_context(nc.Block())

        def waits(eng, s, value):
            if not isinstance(value, int) or value > 0:
                eng.wait_ge(s, value)

        def live(tile):
            return not isinstance(tile, int) or 0 <= tile < SLOTS

        def there(b):
            return not isinstance(b, int) or 0 <= b < B

        def b_rounds(eng, round_):
            for b in (-1, 0):
                round_(b, b % 2)
            with eng.Fori(0, 2) as h:
                round_(h * 2 + 1, 1)
                round_(h * 2 + 2, 0)
            for b in range(5, B + 1):
                round_(b, b % 2)

        def slot_steps(eng, step, last):
            for s in range(-1, 3):
                step(s, s % 2)
            with eng.Fori(1, (SLOTS - 3) // 2) as k:
                step(k * 2 + 1, 1)
                step(k * 2 + 2, 0)
            for s in range(SLOTS - 2, last + 1):
                step(s, s % 2)

        x_view = x_in.rearrange("b (u p) d -> p (b u) d", p=P)
        out_view = out.rearrange("b (u p) d -> p (b u) d", p=P)

        @block.sync
        def _(sp):
            for g in range(4):
                sp.dma_start(x[:, 4 * g:4 * g + 4, :], x_view[:, 4 * g:4 * g + 4, :]).then_inc(x_loaded, 16)
                sp.wait_ge(x_loaded, 16 * g + 16)
            sp.dma_start(cst[:, :], cst_in).then_inc(loaded, 16)
            sp.dma_start(Mq[:, :], Mq_in).then_inc(loaded, 16)
            sp.dma_start(Mk[:, :], Mk_in).then_inc(loaded, 16)
            sp.dma_start(Mv[:, :], Mv_in).then_inc(loaded, 16)
            sp.dma_start(yg[:, :, :], sel_in.rearrange("p (h k) -> p h k", h=HB)).then_inc(sel_loaded, 16)
            sp.dma_start(wq[:, :], wq_in).then_inc(b_loaded, 16)
            sp.dma_start(wdown[:, :], wdown_in).then_inc(b_loaded, 16)
            sp.dma_start(wkv[:, 0:D], wkup_in).then_inc(b_loaded, 16)
            sp.dma_start(wkv[:, D:2 * D], wvup_in).then_inc(b_loaded, 16)
            sp.dma_start(wo[:, :], wo_in).then_inc(b_loaded, 16)
            sp.dma_start(wg[:, :], wg_in).then_inc(w_loaded, 16)
            sp.dma_start(bg[:, :], bg_in.unsqueeze(0).to_broadcast([P, NE])).then_inc(w_loaded, 16)
            sp.dma_start(W1[:, :, :], W1_in.rearrange("e d m -> d e m")).then_inc(w_loaded, 16)
            sp.dma_start(W2[:, :, :, :], W2_in.rearrange("e (c p) d -> p e c d", p=P)).then_inc(w_loaded, 16)
            sp.dma_start(b1[:, :, :], b1_in.unsqueeze(0).to_broadcast([P, NE, MLP])).then_inc(w_loaded, 16)
            sp.dma_start(b2[:, :, :], b2_in.unsqueeze(0).to_broadcast([P, NE, D])).then_inc(w_loaded, 16)
            sp.wait_ge(pool_const, 1)
            sp.dma_start(xs_dram.rearrange("(s p) d -> p s d", p=P),
                         zeros[:, :].unsqueeze(1).to_broadcast([P, SLOTS, D])).then_inc(slots_zero, 16)

            def ffn_loads(n):
                f = ffn[n]
                sp.wait_ge(f["scattered"], 16 * NT)

                def load(s, par):
                    waits(sp, f["xt"], s - 1)
                    sp.dma_start(xg[:, par, :], xs_dram[bass.ds(s * P, P), :]).then_inc(f[f"in{par}"], 16)

                load(0, 0)
                load(1, 1)
                with sp.Fori(1, SLOTS // 2) as k:
                    load(k * 2, 0)
                    load(k * 2 + 1, 1)
                load(SLOTS - 1, 0)

            ffn_loads(0)
            ffn_loads(1)
            sp.wait_ge(ffn[1]["x"], NT)
            sp.dma_start(out_view, x[:, :, :]).then_inc(stored, 16)
            sp.wait_ge(stored, 16)

        def evacuate_a(eng, p, i, bank):
            copy = eng.tensor_copy if eng.engine == mybir.EngineType.DVE else eng.copy
            j0 = 4 * bank
            if i == 0:
                src = pb[bank][:, :].rearrange("p (j t) -> p j t", j=4)
                if eng.engine == mybir.EngineType.DVE:
                    return eng.tensor_scalar(QT[:, p, j0:j0 + 4, :], src, SCALE_A, None, ALU.mult)
                return eng.mul(QT[:, p, j0:j0 + 4, :], src, SCALE_A)
            if i == 1:
                for jj in range(2):
                    for h in range(2):
                        src = pb[bank][64 * jj:64 * jj + 64, :].rearrange("p (m h t) -> p m h t", m=2, h=2)
                        dst = KT[64 * h:64 * h + 64, p, h, :, j0 + jj:j0 + 4:2, :].rearrange("p s m i -> p m s i")
                        last = copy(dst, src[:, :, h, :].rearrange("p m (s i) -> p m s i", s=4))
                return last
            src = pb[bank][:, 0:HA * 32].rearrange("p (j c d) -> p j c d", j=HA, c=2)
            last = copy(Va[:, p, :, :].rearrange("p c (j d) -> p j c d", d=VA), src)
            return last

        @block.vector
        def _(dve):
            def normalise(n, x_ready):
                s = norm[n]
                for t in range(NT):
                    x_ready(t)
                    dve.bn_stats(stat[:, t, :], x[:, t, :]).then_inc(s["stats"], 1)
                for t in range(NT):
                    dve.wait_ge(s["stats"], t + 1)
                    dve.bn_aggr(mv[:, t, :], stat[:, t, :]).then_inc(s["mv"], 1)
                dve.wait_ge(s["rstd"], 1)
                for t in range(NT):
                    dve.tensor_scalar(xn[:, t, :], x[:, t, :], mv[:, t, 0:1], rstd[:, 0, t:t + 1],
                                      ALU.subtract, ALU.mult).then_inc(s["xn"], 1)

            normalise(0, lambda t: dve.wait_ge(x_loaded, 16 * (t // 4) + 16))

            def a_evacuate(b, p, i):
                dve.wait_ge(a_proj, b * 5 + 2 * i + 1)
                evacuate_a(dve, p, i, 0).then_inc(a_evd, 1)

            def a_step(b, hp, p, lag, nxt):
                g = b * 4 + hp
                dve.wait_ge(a_scores, g + 1)
                dve.tensor_reduce(nmax[:, hp, :], S4[:, 2 * (hp % 2):2 * (hp % 2) + 2, :]
                                  .rearrange("p h (c q) -> p h c q", c=2), AX.X, ALU.max,
                                  negate=True).then_inc(a_max, 1)
                if nxt and hp < 3:
                    a_evacuate(b + 1, 1 - p, hp)
                if hp or lag:
                    a_recip(b * 4 + hp - 1, (hp + 3) % 4)
                if hp == 2 and lag:
                    a_add(b - 1)
                if hp >= 2 or lag:
                    a_outT(g - 2, (hp + 2) % 4)

            def a_recip(g, q):
                dve.wait_ge(a_exp, g + 1)
                dve.reciprocal(rden[:, q, :], den[:, q, :]).then_inc(a_rden, 1)

            def a_outT(g, q):
                dve.wait_ge(a_av, g + 1)
                dve.tensor_copy(OT[:, :, :, q, :], pb[2][:, 0:128].rearrange("p (h j i) -> p h j i", h=2, j=2)
                                ).then_inc(a_ot, 1)

            def a_add(b):
                dve.wait_ge(a_f, b + 1)
                xs = x[:, bass.ds(b * 2, 2), :]
                dve.tensor_tensor(xs, xs, pb[3][:, 0:256].rearrange("p (h c) -> p h c", h=2), ALU.add
                                  ).then_inc(a_x, 1)

            dve.wait_ge(a_zero, 1)
            for i in range(3):
                a_evacuate(0, 0, i)
            for hp in range(4):
                a_step(0, hp, 0, False, True)
            with dve.Fori(0, 3) as h:
                for hp in range(4):
                    a_step(h * 2 + 1, hp, 1, True, True)
                for hp in range(4):
                    a_step(h * 2 + 2, hp, 0, True, True)
            for hp in range(4):
                a_step(7, hp, 1, True, False)
            a_recip(31, 3)
            a_outT(30, 2)
            a_outT(31, 3)
            a_add(7)

            def ffn_route(n):
                f = ffn[n]
                chain = Chain(dve, f["chain"])
                link = chain.link
                dve.wait_ge(f["logits"], 1)
                bgb = bg[:, :].unsqueeze(1).to_broadcast([P, NT, NE])
                link(dve.tensor_tensor(lg[:, :, :], pb[2][:, 0:NT * NE].rearrange("p (t e) -> p t e", e=NE), bgb, ALU.add))
                link(dve.tensor_reduce(lmax[:, :], lg[:, :, :], AX.X, ALU.max))
                lmb = lmax[:, :].unsqueeze(2).to_broadcast([P, NT, NE])
                dve.tensor_tensor(lsub[:, :, :], lg[:, :, :], lmb, ALU.subtract).then_inc(f["exp"], 1)
                link(dve.tensor_tensor(cand[:, :, :], lg[:, :, :], lmb, ALU.is_equal))
                link(dve.tensor_tensor(cand[:, :, :], cand[:, :, :],
                                       const("order").unsqueeze(1).to_broadcast([P, NT, NE]), ALU.mult))
                link(dve.tensor_reduce(cmax[:, :], cand[:, :, :], AX.X, ALU.max))
                link(dve.tensor_tensor(onehot[:, :, :].rearrange("p e t -> p t e"), cand[:, :, :],
                                       cmax[:, :].unsqueeze(2).to_broadcast([P, NT, NE]), ALU.is_equal))
                dve.tensor_tensor_scan(count[:, :, :].rearrange("p e t -> p (e t)"), const("within"),
                                       onehot[:, :, :].rearrange("p e t -> p (e t)"), 0.0, ALU.mult, ALU.add
                                       ).then_inc(f["counts"], 1)
                dve.wait_ge(f["totals"], 1)
                earlier, total = pb[3][:, 0:NE], pb[3][:, NE:2 * NE]
                link(dve.tensor_tensor(above[:, :, :], total.unsqueeze(2).to_broadcast([P, NE, NT]),
                                       const("steps").unsqueeze(1).to_broadcast([P, NE, NT]), ALU.is_gt))
                link(dve.tensor_reduce(tiles[:, 0, :], above[:, :, :], AX.X, ALU.add))
                link(dve.tensor_tensor_scan(tiles[:, 1, :], const("ones")[:, 0:NE], tiles[:, 0, :], 0.0,
                                            ALU.mult, ALU.add))
                link(dve.tensor_tensor(tiles[:, 2, :], tiles[:, 1, :], tiles[:, 0, :], ALU.subtract))
                link(dve.scalar_tensor_tensor(out=tiles[:, 3, :], in0=tiles[:, 2, :], scalar=float(P),
                                              in1=earlier, op0=ALU.mult, op1=ALU.add))
                link(dve.tensor_tensor(place[:, :, :], count[:, :, :],
                                       tiles[:, 3, :].unsqueeze(2).to_broadcast([P, NE, NT]), ALU.add))
                link(dve.scalar_tensor_tensor(out=place[:, :, :], in0=place[:, :, :], scalar=-1.0,
                                              in1=onehot[:, :, :], op0=ALU.add, op1=ALU.mult))
                link(dve.tensor_reduce(pos_f[:, :], place[:, :, :].rearrange("p e t -> p t e"), AX.X, ALU.add))
                dve.tensor_copy(pos[:, :], pos_f[:, :]).then_inc(f["pos"], 1)
                link(dve.tensor_tensor(past[:, :, :],
                                       const("slots").unsqueeze(2).to_broadcast([P, SLOTS, NE]),
                                       tiles[:, 1, :].unsqueeze(1).to_broadcast([P, SLOTS, NE]), ALU.is_ge))
                link(dve.tensor_reduce(expert_f[:, :], past[:, :, :], AX.X, ALU.add))
                dve.tensor_scalar(expert[:, :], expert_f[:, :], float(NE - 1), None, ALU.min).then_inc(f["table"], 1)
                dve.wait_ge(f["exp"], 2)
                link(dve.tensor_reduce(route_p[:, 1, :], lexp[:, :, :], AX.X, ALU.add))
                link(dve.reciprocal(route_p[:, 0, :], route_p[:, 1, :]))

            def ffn_tiles(n):
                f = ffn[n]
                dve.wait_ge(f["table"], 1)

                def step(s, par):
                    if live(s + 1):
                        dve.wait_ge(f["xt"], s + 2)
                        waits(dve, f["h"], s)
                        dve.tensor_copy(xgT[:, 1 - par, :], pb[0][:, 0:P]).then_inc(f["xgT"], 1)
                    if live(s):
                        e = dve.value_load(expert[0:1, bass.ds(s, 1)], min_val=0, max_val=NE - 1)
                        dve.wait_ge(f["h"], s + 1)
                        waits(dve, f["ht"], s - 1)
                        dve.tensor_tensor(hb[:, par, :], S4[:, par, :], b1[:, bass.ds(e, 1), :].squeeze(1), ALU.add
                                          ).then_inc(f["hb"], 1)
                    if live(s - 2):
                        e2 = dve.value_load(expert[0:1, bass.ds(s - 2, 1)], min_val=0, max_val=NE - 1)
                        dve.wait_ge(f["y"], s - 1)
                        if isinstance(s, int):
                            waits(dve, f[f"out{par}"], 16 * ((s - 2) // 2))
                        else:
                            dve.wait_ge(f[f"out{par}"], (s - 2 - par) * 8)
                        dve.tensor_tensor(yo[:, par, :], pb[1 + par][:, 0:D], b2[:, bass.ds(e2, 1), :].squeeze(1),
                                          ALU.add).then_inc(f["yo"], 1)

                slot_steps(dve, step, SLOTS + 1)

            def ffn_add(n):
                f = ffn[n]
                for t in range(NT):
                    if t % 4 == 0:
                        dve.wait_ge(f[f"back{t // 4}"], 64)
                    dve.scalar_tensor_tensor(out=x[:, t, :], in0=yg[:, t, :], scalar=route_p[:, 0, t:t + 1],
                                             in1=x[:, t, :], op0=ALU.mult, op1=ALU.add).then_inc(f["x"], 1)

            normalise(1, lambda t: dve.wait_ge(a_x, t // 2 + 1))
            dve.wait_ge(w_loaded, 96)
            ffn_route(0)
            ffn_tiles(0)
            ffn_add(0)

            def b_turn(b, i, src, done):
                dve.wait_ge(bs["latT"] if i == 0 else bs["v"], b + 1)
                cos = const("cos").rearrange("p (u d) -> p u d", u=2)
                sin = const("sin").rearrange("p (u r) -> p u r", u=2)
                for u in range(2):
                    v = src(u).rearrange("p (h d) -> p h d", d=DB)
                    o = [turn[:, k, i, u, :].rearrange("p (h d) -> p h d", d=DB) for k in range(2)]
                    c = cos[:, u, :].unsqueeze(1).to_broadcast([P, HB, DB])
                    sn = sin[:, u, 0:DB].unsqueeze(1).to_broadcast([P, HB, DB])
                    dve.tensor_tensor(o[0], v, c, ALU.mult)
                    dve.tensor_tensor(o[1][:, :, 0:DB:2], v[:, :, 1:DB:2], sn[:, :, 0:DB:2], ALU.mult)
                    last = dve.tensor_tensor(o[1][:, :, 1:DB:2], v[:, :, 0:DB:2], sn[:, :, 1:DB:2], ALU.mult)
                last.then_inc(done, 1)

            def b_kT(b, p, i):
                dve.wait_ge(bs["tk"], b * 2 + i + 1)
                src = pb[0][0:64, :].bitcast(BF16).rearrange("p (n t) -> p n t", n=4)
                dve.tensor_copy(kT[0:64, p, 4 * i:4 * i + 4, 0, :], src).then_inc(bs["kTlow"], 1)

            def b_max(b, q):
                dve.wait_ge(bs["s"], b * 4 + q + 1)
                if q == 0:
                    waits(dve, bs["ms"], b)
                for d in range(2):
                    h0 = 4 * q + 2 * d
                    dve.tensor_reduce(nm[:, 1, h0:h0 + 2], pb[2 + d][:, :].rearrange("p (h k) -> p h k", h=2),
                                      AX.X, ALU.max, negate=True)
                dve.tensor_reduce(nm[:, 0, 4 * q:4 * q + 4], S4[:, 3, :].rearrange("p (h k) -> p h k", h=4),
                                  AX.X, ALU.max, negate=True).then_inc(bs["max"], 1)

            def b_normal(b, u):
                dve.wait_ge(bs["on"], b * 2 + u + 1)
                o = pb[1][:, :].rearrange("p (h r) -> p h r", r=32)
                dve.reciprocal(rsum[:, u, :], o[:, :, DB]).then_inc(bs["rsum"], 1)
                dve.wait_ge(bs["rsum"], b * 2 + u + 1)
                waits(dve, bs["at"], b)
                dve.tensor_tensor(att[:, u, :].rearrange("p (h d) -> p h d", d=DB), o[:, :, 0:DB],
                                  rsum[:, u, :].unsqueeze(2).to_broadcast([P, HB, DB]), ALU.mult
                                  ).then_inc(bs["att"], 1)

            def b_round(b, p):
                if there(b + 1):
                    b_kT(b + 1, 1 - p, 0)
                if there(b + 2):
                    dve.wait_ge(bs["p1"], b + 3)
                    waits(dve, bs["split"], b + 2)
                    b_turn(b + 2, 0, lambda u: pb[0][:, u * D:(u + 1) * D], bs["turnq"])
                if there(b + 1):
                    b_kT(b + 1, 1 - p, 1)
                if there(b + 2):
                    dve.wait_ge(bs["p2"], b + 3)
                    b_turn(b + 2, 1, lambda u: pb[0][:, 2 * u * D:(2 * u + 1) * D], bs["turnk"])
                if there(b + 1):
                    b_max(b + 1, 0)
                if there(b - 1):
                    b_normal(b - 1, 0)
                if there(b + 1):
                    b_max(b + 1, 1)
                if there(b - 1):
                    b_normal(b - 1, 1)
                if there(b + 1):
                    b_max(b + 1, 2)
                    b_max(b + 1, 3)
                if there(b - 1):
                    dve.wait_ge(bs["at"], b)
                    dve.tensor_copy(attT[:, :, :], pb[1][:, 0:T].rearrange("p (u t) -> p u t", u=2)
                                    ).then_inc(bs["attT"], 1)
                    dve.wait_ge(bs["y"], b)
                    xs = x[:, bass.ds((b - 1) * 2, 2), :]
                    dve.tensor_tensor(xs, xs, pb[1][:, 0:T].rearrange("p (u c) -> p u c", u=2), ALU.add
                                      ).then_inc(bs["x"], 1)

            def b_first():
                dve.wait_ge(bs["p1"], 1)
                b_turn(0, 0, lambda u: pb[0][:, u * D:(u + 1) * D], bs["turnq"])
                dve.wait_ge(bs["p2"], 1)
                b_turn(0, 1, lambda u: pb[0][:, 2 * u * D:(2 * u + 1) * D], bs["turnk"])

            normalise(2, lambda t: dve.wait_ge(ffn[0]["x"], t + 1))
            b_first()
            b_rounds(dve, b_round)
            normalise(3, lambda t: dve.wait_ge(bs["x"], t // 2 + 1))
            ffn_route(1)
            ffn_tiles(1)
            ffn_add(1)

        @block.scalar
        def _(act):
            def transposed(n):
                s = norm[n]
                for g in range(4):
                    act.wait_ge(s["xt"], 4 * g + 4)
                    act.copy(xnT[:, 4 * g:4 * g + 4, :], pb[g % 2][:, :].rearrange("p (t c) -> p t c", t=4)
                             ).then_inc(s["xnT"], 1)

            transposed(0)

            def a_evacuate(b, p, i):
                act.wait_ge(a_proj, b * 5 + 2 * i + 2)
                evacuate_a(act, p, i, 1).then_inc(a_eva, 1)

            def a_step(b, hp, p, lag, nxt):
                g = b * 4 + hp
                act.wait_ge(a_max, g + 1)
                if lag:
                    act.wait_ge(a_av, g - 3)
                    act.wait_ge(a_rden, g - 3)
                for h in range(2):
                    for c in range(2):
                        k = 2 * h + c
                        last = act.activation(E[:, hp, h, c, :], S[hp % 2][:, h, c * T:(c + 1) * T], ACT.Exp,
                                              bias=nmax[:, hp, k:k + 1], accum_out=den[:, hp, k:k + 1])
                last.then_inc(a_exp, 1)
                if nxt and hp < 2:
                    a_evacuate(b + 1, 1 - p, hp)

            act.wait_ge(a_zero, 1)
            for i in range(2):
                a_evacuate(0, 0, i)
            for hp in range(4):
                a_step(0, hp, 0, False, True)
            with act.Fori(0, 3) as h:
                for hp in range(4):
                    a_step(h * 2 + 1, hp, 1, True, True)
                for hp in range(4):
                    a_step(h * 2 + 2, hp, 0, True, True)
            for hp in range(4):
                a_step(7, hp, 1, True, False)

            def ffn_exp(n):
                f = ffn[n]
                act.wait_ge(f["exp"], 1)
                act.activation(lexp[:, :, :], lsub[:, :, :], ACT.Exp).then_inc(f["exp"], 1)

            def ffn_tiles(n):
                f = ffn[n]

                def step(s, par):
                    if live(s - 1):
                        act.wait_ge(f["ht"], s)
                        waits(act, f["y"], s - 2)
                        act.activation(hT[:, 1 - par, :, :], S4[:, 3 - par, :].rearrange("p (c t) -> p c t", c=MC),
                                       ACT.Relu).then_inc(f["hT"], 1)
                    if live(s - 3):
                        act.wait_ge(f["yo"], s - 2)
                        act.dma_start(ys_dram[bass.ds((s - 3) * P, P), :], yo[:, 1 - par, :]
                                      ).then_inc(f[f"out{1 - par}"], 16)

                slot_steps(act, step, SLOTS + 2)

            transposed(1)
            ffn_exp(0)
            ffn_tiles(0)

            def b_latent(b):
                act.wait_ge(bs["p1"], b + 1)
                waits(act, bs["p2"], b)
                act.copy(latT[:, :], pb[0][0:LAT, T:2 * T]).then_inc(bs["latT"], 1)

            def b_v(b):
                act.wait_ge(bs["p2"], b + 1)
                src = pb[0][:, :].rearrange("p (u i h d) -> p u i h d", u=2, i=2, d=DB)
                waits(act, bs["vb"], b)
                act.copy(vst[:, :, :].rearrange("p u (h d) -> p u h d", d=DB), src[:, :, 1, :, :]).then_inc(bs["v"], 1)

            def b_qT(b, p, i):
                act.wait_ge(bs["tq"], b * 2 + i + 1)
                src = pb[0][:, :].bitcast(BF16).rearrange("p (n t) -> p n t", n=4)
                act.copy(qT[:, p, 4 * i:4 * i + 4, :], src).then_inc(bs["qT"], 1)

            def b_kT(b, p, i):
                act.wait_ge(bs["tk"], b * 2 + i + 1)
                src = pb[0][64:P, :].bitcast(BF16).rearrange("p (n t) -> p n t", n=4)
                act.copy(kT[64:P, p, 4 * i:4 * i + 4, 1, :], src).then_inc(bs["kThigh"], 1)

            def b_exp(b, q):
                act.wait_ge(bs["st"], b * 4 + q + 1)
                waits(act, bs["pv"], b * 4 + q - 1)
                act.activation(Eb[:, q % 2, :, :], S4[:, 0:3, :], ACT.Exp, scale=SCALE_B).then_inc(bs["exp"], 1)

            def b_outT(b, p, q):
                act.wait_ge(bs["pv"], b * 4 + q + 1)
                act.copy(OTb[:, p, q, :], pb[1][:, 0:T]).then_inc(bs["ot"], 1)

            def b_round(b, p):
                n, nn, c, l = there(b + 1), there(b + 2), there(b), there(b - 1)
                if n: b_qT(b + 1, 1 - p, 0)
                if c: b_exp(b, 0)
                if n: b_kT(b + 1, 1 - p, 0)
                if nn: b_latent(b + 2)
                if l: b_outT(b - 1, 1 - p, 3)
                if n: b_qT(b + 1, 1 - p, 1)
                if c: b_exp(b, 1)
                if n: b_kT(b + 1, 1 - p, 1)
                if nn: b_v(b + 2)
                if c: b_outT(b, p, 0)
                if c: b_exp(b, 2)
                if c: b_outT(b, p, 1)
                if c: b_exp(b, 3)
                if c: b_outT(b, p, 2)
                if n:
                    act.wait_ge(bs["mt"], b + 2)
                    act.copy(mT[:, :, :], pb[0][:, 0:P].bitcast(BF16).rearrange("p (u t) -> p u t", u=2)
                             ).then_inc(bs["mT"], 1)

            transposed(2)
            b_latent(0)
            b_v(0)
            b_rounds(act, b_round)
            transposed(3)
            ffn_exp(1)
            ffn_tiles(1)

        @block.gpsimd
        def _(pool):
            pool.memset(KT[:, :, :, :, :, :], 0.0).then_inc(a_zero, 1)
            pool.memset(Vb[:, :, :, :, :], 0.0).then_inc(bs["const"], 1)
            pool.memset(ms[:, :, :], 0.0).then_inc(bs["const"], 1)
            pool.wait_ge(bs["const"], 1)
            pool.memset(Vb[:, :, :, :, DB:DB + 1], 1.0).then_inc(bs["const"], 1)

            pool.memset(zeros[:, :], 0.0).then_inc(pool_const, 1)
            pool.memset(rstd[:, 1, :], -0.5).then_inc(pool_const, 1)
            pool.wait_ge(pool_const, 2)

            def inverse_deviation(n):
                s = norm[n]
                pool.wait_ge(s["mv"], NT)
                pool.tensor_scalar(rstd[:, 0, :], mv[:, :, 1], EPS, None, ALU.add).then_inc(s["vareps"], 1)
                pool.wait_ge(s["vareps"], 1)
                pool.tensor_tensor(rstd[:, 0, :], rstd[:, 0, :], rstd[:, 1, :], ALU.pow).then_inc(s["rstd"], 1)

            inverse_deviation(0)

            def a_stage(b, p):
                pool.tensor_copy(xb[:, p, :].rearrange("p (u t) -> p u t", u=2),
                                 xnT[:, bass.ds(b * 2, 2), :]).then_inc(a_xb, 1)

            def a_values(g, q, p, reuse):
                pool.wait_ge(a_rden, g + 1)
                if reuse:
                    pool.wait_ge(a_av, g - 3)
                v = Va[:, p, :, :].unsqueeze(1).to_broadcast([P, 2, 2, HA * VA])
                r = rden[:, q, :].rearrange("p (h c) -> p h c", h=2).unsqueeze(3).to_broadcast([P, 2, 2, HA * VA])
                pool.tensor_tensor(vs[:, q, :, :, :], v, r, ALU.mult).then_inc(a_vs, 1)

            pool.wait_ge(norm[0]["xnT"], 4)
            a_stage(0, 0)
            a_stage(1, 1)
            pool.wait_ge(a_evd, 3)
            pool.wait_ge(a_eva, 2)

            def a_batch(b, p, lag, ahead):
                for hp in range(4):
                    if hp == 0:
                        pool.wait_ge(a_evd, b * 3 + 3)
                    if hp == 3 and ahead:
                        pool.wait_ge(a_proj, b * 5 + 5)
                        a_stage(b + 2, p)
                    a_values(b * 4 + hp, hp, p, lag)

            a_batch(0, 0, False, True)
            with pool.Fori(0, 2) as h:
                a_batch(h * 2 + 1, 1, True, True)
                a_batch(h * 2 + 2, 0, True, True)
            a_batch(5, 1, True, True)
            a_batch(6, 0, True, False)
            a_batch(7, 1, True, False)

            def ffn_scatter(n):
                f = ffn[n]
                pool.wait_ge(f["pos"], 1)
                for t in range(NT):
                    pool.indirect_dma_start(out=xs_dram, out_offset=bass.IndirectOffsetOnAxis(pos[:, t:t + 1], 0),
                                            in_=xn[:, t, :], in_offset=None).then_inc(f["scattered"], 16)

            def ffn_gather(n):
                f = ffn[n]
                pool.wait_ge(f["out0"], 16 * ((SLOTS + 1) // 2))
                pool.wait_ge(f["out1"], 16 * (SLOTS // 2))
                for t in range(NT):
                    pool.indirect_dma_start(out=yg[:, t, :], out_offset=None, in_=ys_dram,
                                            in_offset=bass.IndirectOffsetOnAxis(pos[:, t:t + 1], 0)
                                            ).then_inc(f[f"back{t // 4}"], 16)

            pool.wait_ge(a_scores, 4 * B)
            pool.memset(KT[:, :, :, :, :, :], 0.0).then_inc(bs["zero"], 1)
            pool.wait_ge(sel_loaded, 16)
            pool.tensor_copy(sel[:, :, :], yg[:, :, :]).then_inc(bs["const"], 1)
            pool.wait_ge(loaded, 64)
            pool.tensor_copy(identb[:, :], ident).then_inc(bs["const"], 1)
            for t, name in ((qs, "qmask"), (ks, "kmask")):
                for u in range(2):
                    pool.tensor_copy(t[:, u, :, 48:64], const(name)[:, 16 * u:16 * u + 16].unsqueeze(1)
                                     .to_broadcast([P, HB, 16])).then_inc(bs["const"], 1)
            inverse_deviation(1)
            pool.wait_ge(slots_zero, 16)
            ffn_scatter(0)
            pool.wait_ge(bs["const"], 5)
            ffn_gather(0)

            def b_stage(b, p):
                pool.tensor_copy(xb[:, p, :].rearrange("p (u t) -> p u t", u=2),
                                 xnT[:, bass.ds(b * 2, 2), :]).then_inc(bs["xb"], 1)

            def b_split(b):
                chain = Chain(pool, bs["chain"])
                chain.restart(b * 15)
                blocks = {"q": ((0, 1, 4), (2, 3), (5,)), "k": ((0, 2, 5), (1, 3), (4,))}

                def part(i, k):
                    dst = (qs, ks)[i]
                    n = blocks["qk"[i]][k]
                    return [dst[:, :, :, 8 * m:8 * m + 8].rearrange("p u h d -> p (u h) d") for m in n]

                def view(t, i):
                    return t[:, i, :, :].rearrange("p u (h d) -> p (u h) d", d=DB)

                pool.wait_ge(bs["turnq"], b + 1)
                pool.wait_ge(bs["turnk"], b + 1)
                flat = [turn[:, k, :, :, :].rearrange("p i u c -> p (i u c)") for k in range(2)]
                chain.inc(pool.tensor_tensor(rest[:, :, :, :].rearrange("p i u c -> p (i u c)"), flat[0], flat[1], ALU.add))
                waits(pool, bs["tq"], b * 2)
                waits(pool, bs["tk"], b * 2)
                for i in range(2):
                    chain.inc(pool.tensor_tensor(part(i, 0)[0], view(turn[:, 0, :, :, :], i), view(turn[:, 1, :, :, :], i),
                                                 ALU.add))
                chain.wait()
                for i in range(2):
                    hi = part(i, 0)
                    chain.inc(pool.tensor_tensor(part(i, 1)[0], view(rest, i), hi[0], ALU.subtract))
                    chain.inc(pool.tensor_tensor(view(rest2, i), view(rest, i), hi[0], ALU.subtract))
                    chain.inc(pool.tensor_copy(hi[1], hi[0]))
                    chain.inc(pool.tensor_copy(hi[2], hi[0]))
                chain.wait()
                for i in range(2):
                    mid = part(i, 1)
                    chain.inc(pool.tensor_tensor(part(i, 2)[0], view(rest2, i), mid[0], ALU.subtract))
                    chain.inc(pool.tensor_copy(mid[1], mid[0]))
                chain.wait()
                assert chain.k == 15
                pool.sem_inc(bs["split"], 1)

            def b_maxima(b):
                chain = Chain(pool, bs["mchain"])
                chain.restart(b * 4)
                pool.wait_ge(bs["max"], b * 4 + 4)
                waits(pool, bs["mt"], b)
                parts = ms[:, :, 0:3 * HB].rearrange("p u (h k) -> p u h k", k=3)
                chain.link(pool.tensor_tensor(
                    parts[:, :, :, 0], nm[:, :, :], zeros[:, 0:2 * HB].rearrange("p (u h) -> p u h", u=2), ALU.add))
                chain.inc(pool.tensor_tensor(nmr[:, :, :], nm[:, :, :], parts[:, :, :, 0], ALU.subtract))
                chain.link(pool.tensor_tensor(parts[:, :, :, 1], nm[:, :, :], parts[:, :, :, 0], ALU.subtract))
                chain.link(pool.tensor_tensor(parts[:, :, :, 2], nmr[:, :, :], parts[:, :, :, 1], ALU.subtract))
                pool.sem_inc(bs["ms"], 1)

            def b_place_v(b, p):
                pool.wait_ge(bs["v"], b + 1)
                waits(pool, bs["pv"], b * 4 - 4)
                z = zeros[:, :].rearrange("p (h d) -> p h d", d=DB)
                for u in range(2):
                    last = pool.tensor_tensor(Vb[:, p, u, :, 0:DB], vst[:, u, :].rearrange("p (h d) -> p h d", d=DB), z,
                                              ALU.add)
                last.then_inc(bs["vb"], 1)

            def b_round(b, p):
                if there(b + 1):
                    b_place_v(b + 1, 1 - p)
                if there(b + 2):
                    b_split(b + 2)
                if there(b + 3):
                    pool.wait_ge(bs["latT"], b + 2)
                    b_stage(b + 3, 1 - p)
                if there(b + 1):
                    b_maxima(b + 1)

            inverse_deviation(2)
            pool.wait_ge(norm[2]["xnT"], 4)
            b_stage(0, 0)
            b_stage(1, 1)
            b_split(0)
            for b in (-1, 0):
                b_round(b, b % 2)
            with pool.Fori(0, 2) as h:
                b_round(h * 2 + 1, 1)
                b_round(h * 2 + 2, 0)
            for b in range(5, B + 1):
                b_round(b, b % 2)
            inverse_deviation(3)
            ffn_scatter(1)
            ffn_gather(1)

        @block.tensor
        def _(pe):
            def transpose(n):
                s = norm[n]
                for t in range(NT):
                    pe.wait_ge(s["xn"], t + 1)
                    if t >= 8 and t % 4 == 0:
                        pe.wait_ge(s["xnT"], t // 4 - 1)
                    pe.transpose(pb[t // 4 % 2][:, (t % 4) * P:(t % 4 + 1) * P], xn[:, t, :], ident
                                 ).then_inc(s["xt"], 1)

            pe.wait_ge(loaded, 64)
            transpose(0)

            def a_project(b, p, i, free):
                if i == 0:
                    pe.wait_ge(a_xb, b + 1)
                for bank in range(2 if i < 2 else 1):
                    if free and bank == 0:
                        pe.wait_ge(a_evd, b * 3 + i)
                    if free and bank == 1:
                        pe.wait_ge(a_eva, b * 2 + i)
                    dst = pb[bank]
                    if i == 0:
                        for j in range(4):
                            for h in range(2):
                                jq = 4 * bank + j
                                last = pe.matmul(dst[64 * h:64 * h + 64, j * P:(j + 1) * P],
                                                 Mq[:, jq * KA:(jq + 1) * KA], xb[:, p, h * P:(h + 1) * P],
                                                 start=True, stop=True)
                    elif i == 1:
                        for m in range(2):
                            mq = 2 * bank + m
                            last = pe.matmul(dst[:, m * T:(m + 1) * T], Mk[:, mq * P:(mq + 1) * P],
                                             xb[:, p, :], start=True, stop=True)
                    else:
                        for j in range(HA):
                            for g in range(4):
                                last = pe.matmul(dst[32 * g:32 * g + 32, 32 * j:32 * j + 32],
                                                 xb[:, p, j * RT:(j + 1) * RT],
                                                 Mv[:, :].rearrange("p (c g d) -> p c g d", c=2, g=4)[:, :, g, :],
                                                 start=True, stop=True)
                    last.then_inc(a_proj, 1)

            def a_values_out(g, q):
                pe.wait_ge(a_vs, g + 1)
                for h in range(2):
                    for c in range(2):
                        for jp in range(4):
                            last = pe.matmul(pb[2][32 * jp:32 * jp + 32, 64 * h:64 * h + 64],
                                             vs[:, q, h, c, 32 * jp:32 * jp + 32],
                                             E[:, q, h, c, 64 * jp:64 * jp + 64], start=(c == 0), stop=(c == 1))
                last.then_inc(a_av, 1)

            def a_final(b):
                pe.wait_ge(a_ot, b * 4 + 4)
                for h in range(2):
                    for jj in range(2):
                        last = pe.matmul(pb[3][:, h * P:(h + 1) * P], OT[:, h, jj, :, :],
                                         const("pick")[:, jj * P:(jj + 1) * P], start=(jj == 0), stop=(jj == 1))
                last.then_inc(a_f, 1)

            def a_step(b, hp, p, lag, nxt):
                g = b * 4 + hp
                if hp >= 2 or lag:
                    pe.wait_ge(a_exp, g - 1)
                if hp == 0:
                    pe.wait_ge(a_evd, b * 3 + 3)
                    pe.wait_ge(a_eva, b * 2 + 2)
                for h in range(2):
                    for c in range(2):
                        last = pe.matmul(S[hp % 2][:, h, c * T:(c + 1) * T],
                                         KT[:, p, h, hp, 4 * c:4 * c + 4, :],
                                         QT[:, p, :, hp * RT:(hp + 1) * RT], start=True, stop=True)
                last.then_inc(a_scores, 1)
                if nxt and hp < 3:
                    a_project(b + 1, 1 - p, hp, True)
                if hp == 2 and lag:
                    a_final(b - 1)
                if hp >= 2 or lag:
                    if not (hp == 2 and not lag):
                        pe.wait_ge(a_ot, g - 2)
                    a_values_out(g - 2, (hp + 2) % 4)

            for i in range(3):
                if i == 0:
                    pe.wait_ge(norm[0]["xnT"], 4)
                a_project(0, 0, i, i > 0)
            for hp in range(4):
                a_step(0, hp, 0, False, True)
            with pe.Fori(0, 3) as h:
                for hp in range(4):
                    a_step(h * 2 + 1, hp, 1, True, True)
                for hp in range(4):
                    a_step(h * 2 + 2, hp, 0, True, True)
            for hp in range(4):
                a_step(7, hp, 1, True, False)
            for g in (30, 31):
                pe.wait_ge(a_ot, g)
                a_values_out(g, g % 4)
            a_final(7)

            def ffn_logits(n):
                f, s = ffn[n], norm[2 * n + 1]
                for t in range(NT):
                    pe.wait_ge(s["xnT"], t // 4 + 1)
                    last = pe.matmul(pb[2][:, t * NE:(t + 1) * NE], xnT[:, t, :], wg[:, :], start=True, stop=True)
                last.then_inc(f["logits"], 1)
                pe.wait_ge(f["counts"], 1)
                row = count[:, :, NT - 1]
                pe.matmul(pb[3][:, 0:NE], const("before"), row, start=True, stop=True)
                pe.matmul(pb[3][:, NE:2 * NE], const("ones"), row, start=True, stop=True).then_inc(f["totals"], 1)

            def ffn_tiles(n):
                f = ffn[n]
                pe.wait_ge(f["table"], 1)

                def step(s, par):
                    if live(s + 1):
                        if isinstance(s, int):
                            pe.wait_ge(f[f"in{1 - par}"], 16 * ((s + 1) // 2 + 1))
                        else:
                            pe.wait_ge(f[f"in{1 - par}"], (s + 1 - (1 - par)) * 8 + 16)
                        waits(pe, f["xgT"], s + 1)
                        pe.transpose(pb[0][:, 0:P], xg[:, 1 - par, :], ident).then_inc(f["xt"], 1)
                    if live(s):
                        e = pe.value_load(expert[0:1, bass.ds(s, 1)], min_val=0, max_val=NE - 1)
                        pe.wait_ge(f["xgT"], s + 1)
                        waits(pe, f["hb"], s - 1)
                        pe.matmul(S4[:, par, :], xgT[:, par, :], W1[:, bass.ds(e, 1), :].squeeze(1), start=True, stop=True
                                  ).then_inc(f["h"], 1)
                    if live(s - 1):
                        pe.wait_ge(f["hb"], s)
                        waits(pe, f["hT"], s - 2)
                        for c in range(MC):
                            last = pe.transpose(S4[:, 3 - par, c * P:(c + 1) * P],
                                                hb[:, 1 - par, c * P:(c + 1) * P], ident)
                        last.then_inc(f["ht"], 1)
                    if live(s - 2):
                        e2 = pe.value_load(expert[0:1, bass.ds(s - 2, 1)], min_val=0, max_val=NE - 1)
                        pe.wait_ge(f["hT"], s - 1)
                        waits(pe, f["yo"], s - 3)
                        for c in range(MC):
                            last = pe.matmul(pb[1 + par][:, 0:D], hT[:, par, c, :],
                                             W2[:, bass.ds(e2, 1), c, :].squeeze(1), start=(c == 0), stop=(c == MC - 1))
                        last.then_inc(f["y"], 1)

                slot_steps(pe, step, SLOTS + 1)

            transpose(1)
            pe.wait_ge(w_loaded, 96)
            ffn_logits(0)
            ffn_tiles(0)

            def b_q(b, p):
                pe.wait_ge(bs["xb"], b + 1)
                for u in range(2):
                    pe.matmul(pb[0][:, u * D:(u + 1) * D], xb[:, p, u * P:(u + 1) * P], wq[:, :], start=True, stop=True)
                pe.matmul(pb[0][0:LAT, T:2 * T], wdown[:, :], xb[:, p, :], start=True, stop=True).then_inc(bs["p1"], 1)

            def b_kv(b):
                pe.wait_ge(bs["latT"], b + 1)
                pe.wait_ge(bs["turnq"], b + 1)
                for u in range(2):
                    last = pe.matmul(pb[0][:, 2 * u * D:2 * (u + 1) * D], latT[:, u * P:(u + 1) * P], wkv[:, :],
                                     start=True, stop=True)
                last.then_inc(bs["p2"], 1)

            def b_transpose(src, i, done):
                dst = pb[0][:, :].bitcast(BF16)
                for n in range(4):
                    for u in range(2):
                        last = pe.transpose(dst[:, n * T + u * P:n * T + (u + 1) * P],
                                            src[:, u, 2 * (4 * i + n):2 * (4 * i + n) + 2, :]
                                            .rearrange("p h c -> p (h c)"), identb[:, :])
                last.then_inc(done, 1)

            def b_tq(b, i):
                pe.wait_ge(bs["split"], b + 1)
                b_transpose(qs, i, bs["tq"])

            def b_tk(b, i):
                pe.wait_ge(bs["qT"], b * 2 + i + 1)
                b_transpose(ks, i, bs["tk"])

            def b_scores(b, p, q):
                if q == 0:
                    pe.wait_ge(bs["qT"], b * 2 + 2)
                    pe.wait_ge(bs["kTlow"], b * 2 + 2)
                    pe.wait_ge(bs["kThigh"], b * 2 + 2)
                waits(pe, bs["max"], b * 4 + q)
                for d in range(2):
                    n = 2 * q + d
                    pe.matmul(pb[2 + d][:, :], qT[:, p, n, P:T], kT[:, p, n, :, :], start=True, stop=True)
                for d in range(2):
                    n = 2 * q + d
                    last = pe.matmul(S4[:, 3, d * T:(d + 1) * T], qT[:, p, n, 0:P], kT[:, p, n, :, 0:P],
                                     start=True, stop=True)
                last.then_inc(bs["s"], 1)

            def b_scoresT(b, p, q):
                if q == 0:
                    pe.wait_ge(bs["mT"], b + 1)
                waits(pe, bs["exp"], b * 4 + q)
                for d in range(2):
                    for h in range(2):
                        n, hh = 2 * q + d, 4 * q + 2 * d + h
                        dst = S4[:, d, h * T:(h + 1) * T]
                        pe.matmul(dst, kT[:, p, n, h, 0:P], qT[:, p, n, :], start=True, stop=False)
                        pe.matmul(dst, sel[:, hh, :], mT[:, :, :], start=False, stop=True)
                        dst = S4[:, 2, (2 * d + h) * P:(2 * d + h + 1) * P]
                        pe.matmul(dst, kT[:, p, n, h, P:T], qT[:, p, n, P:T], start=True, stop=False)
                        last = pe.matmul(dst, sel[:, hh, :], mT[:, 1, :], start=False, stop=True)
                last.then_inc(bs["st"], 1)

            def b_values(b, p, q):
                if q == 0:
                    pe.wait_ge(bs["vb"], b + 1)
                pe.wait_ge(bs["exp"], b * 4 + q + 1)
                for h in range(4):
                    pe.matmul(pb[1][32 * h:32 * h + 32, 0:T], Vb[:, p, 0, 4 * q + h, :],
                              Eb[:, q % 2, h // 2, (h % 2) * T:(h % 2 + 1) * T], start=True, stop=False)
                for h in range(4):
                    last = pe.matmul(pb[1][32 * h:32 * h + 32, P:T], Vb[:, p, 1, 4 * q + h, :],
                                     Eb[:, q % 2, 2, h * P:(h + 1) * P], start=False, stop=True)
                last.then_inc(bs["pv"], 1)

            def b_natural(b, p, u):
                if u == 0:
                    pe.wait_ge(bs["ot"], b * 4 + 4)
                for q in range(4):
                    last = pe.transpose(pb[1][:, q * P:(q + 1) * P], OTb[:, p, q, u * P:(u + 1) * P], ident)
                last.then_inc(bs["on"], 1)

            def b_round(b, p):
                n, nn, c, l = there(b + 1), there(b + 2), there(b), there(b - 1)
                if n:
                    waits(pe, bs["mT"], b + 1)
                    b_tq(b + 1, 0)
                if c: b_scoresT(b, p, 0)
                if n: b_tk(b + 1, 0)
                if nn:
                    pe.wait_ge(bs["kTlow"], b * 2 + 3)
                    pe.wait_ge(bs["kThigh"], b * 2 + 3)
                    b_q(b + 2, p)
                if l:
                    waits(pe, bs["x"], b - 1)
                    b_values(b - 1, 1 - p, 3)
                if n:
                    if nn:
                        pe.wait_ge(bs["turnq"], b + 3)
                        pe.wait_ge(bs["latT"], b + 3)
                    else:
                        pe.wait_ge(bs["kTlow"], b * 2 + 3)
                        pe.wait_ge(bs["kThigh"], b * 2 + 3)
                    b_tq(b + 1, 1)
                if c: b_scoresT(b, p, 1)
                if n: b_tk(b + 1, 1)
                if nn:
                    pe.wait_ge(bs["kTlow"], b * 2 + 4)
                    pe.wait_ge(bs["kThigh"], b * 2 + 4)
                    b_kv(b + 2)
                if n: b_scores(b + 1, 1 - p, 0)
                if l: b_natural(b - 1, 1 - p, 0)
                if c:
                    waits(pe, bs["att"], b * 2 - 1)
                    b_values(b, p, 0)
                if n: b_scores(b + 1, 1 - p, 1)
                if c: b_scoresT(b, p, 2)
                if l:
                    if c: pe.wait_ge(bs["ot"], b * 4 + 1)
                    else: pe.wait_ge(bs["att"], b * 2 - 1)
                    b_natural(b - 1, 1 - p, 1)
                if n: b_scores(b + 1, 1 - p, 2)
                if c:
                    if l: pe.wait_ge(bs["att"], b * 2)
                    else: pe.wait_ge(bs["ot"], b * 4 + 1)
                    b_values(b, p, 1)
                if n: b_scores(b + 1, 1 - p, 3)
                if c: b_scoresT(b, p, 3)
                if l:
                    pe.wait_ge(bs["att"], b * 2)
                    if c: pe.wait_ge(bs["ot"], b * 4 + 2)
                    for u in range(2):
                        last = pe.transpose(pb[1][:, u * P:(u + 1) * P], att[:, u, :], ident)
                    last.then_inc(bs["at"], 1)
                    pe.wait_ge(bs["attT"], b)
                if c:
                    pe.wait_ge(bs["ot"], b * 4 + 2)
                    b_values(b, p, 2)
                    pe.wait_ge(bs["ot"], b * 4 + 3)
                if l:
                    for u in range(2):
                        last = pe.matmul(pb[1][:, u * D:(u + 1) * D], attT[:, u, :], wo[:, :], start=True, stop=True)
                    last.then_inc(bs["y"], 1)
                if n:
                    pe.wait_ge(bs["ms"], b + 2)
                    if nn:
                        pe.wait_ge(bs["turnk"], b + 3)
                        pe.wait_ge(bs["v"], b + 3)
                    for u in range(2):
                        last = pe.transpose(pb[0][:, 0:P].bitcast(BF16)[:, u * P:(u + 1) * P], ms[:, u, :], identb[:, :])
                    last.then_inc(bs["mt"], 1)

            transpose(2)
            pe.wait_ge(b_loaded, 80)
            pe.wait_ge(bs["const"], 9)
            pe.wait_ge(bs["zero"], 1)
            b_q(0, 0)
            b_kv(0)
            pe.wait_ge(bs["turnk"], 1)
            pe.wait_ge(bs["v"], 1)
            b_rounds(pe, b_round)
            transpose(3)
            ffn_logits(1)
            ffn_tiles(1)


def _constants():
    i = np.arange(P)
    cols = {}
    cols["ident"] = np.eye(P)
    cols["pick"] = np.concatenate([np.eye(P) * ((i // VA) % 2 == jj)[:, None] for jj in range(2)], 1)
    inv = 1.0 / 10000.0 ** (np.arange(0, DB, 2, dtype=np.float32) / DB)
    ang = np.outer(np.arange(T, dtype=np.float32), inv)
    cos, sin = np.repeat(np.cos(ang), 2, 1), np.repeat(np.sin(ang), 2, 1)
    sin[:, 0::2] *= -1
    page = np.arange(T)[:, None] // PAGE
    pages = np.arange(NPG)[None, :]
    zero = np.zeros((T, 8))
    qmask = np.concatenate([np.where(page < pages, MASKED, 0.0), zero], 1)
    kmask = np.concatenate([page == pages, zero], 1)
    for name, c in (("cos", cos), ("sin", sin), ("qmask", qmask), ("kmask", kmask)):
        cols[name] = np.concatenate([c[:P], c[P:]], 1)
    cols["order"] = np.tile(NE - np.arange(NE), (P, 1))
    cols["within"] = np.tile((np.arange(NE * NT) % NT > 0), (P, 1))
    cols["steps"] = np.tile(P * np.arange(NT), (P, 1))
    cols["slots"] = np.tile(np.arange(SLOTS), (P, 1))
    cols["ones"] = np.ones((P, P))
    cols["before"] = np.triu(np.ones((P, P)), 1)
    return cols


def _select():
    s = np.zeros((P, HB, P), np.float32)
    for h in range(HB):
        s[3 * h:3 * h + 3, h, :] = 1.0
    return s.reshape(P, HB * P)


CST, NCST = {}, 0
for _name, _c in _constants().items():
    CST[_name] = (NCST, NCST + _c.shape[1])
    NCST += _c.shape[1]


_INS = ["L0_attn_a_x", "L0_attn_a_Mq", "L0_attn_a_Mk", "L0_attn_a_Mv", "L0_attn_b_wq", "L0_attn_b_w_down",
        "L0_attn_b_wk_up", "L0_attn_b_wv_up", "L0_attn_b_wo", "L0_ffn_w_gate", "L0_ffn_b_gate", "L0_ffn_W1",
        "L0_ffn_b1", "L0_ffn_W2", "L0_ffn_b2"]


def kernel(**inputs):
    import concourse.bacc as _bacc
    from concourse.bass_utils import run_bass_kernel_spmd as _run

    nc = _bacc.Bacc("TRN2", target_bir_lowering=False, num_devices=1)
    arrays = {f"in_{n}": np.ascontiguousarray(inputs[n]) for n in _INS}
    arrays["in_constants"] = np.concatenate(list(_constants().values()), 1).astype(np.float32)
    arrays["in_select"] = _select()
    args = [nc.dram_tensor(n, a.shape, mybir.dt.from_np(a.dtype), kind="ExternalInput").ap()
            for n, a in arrays.items()]
    out = nc.dram_tensor("out_0", (B, T, D), F32, kind="ExternalOutput").ap()
    xs = nc.dram_tensor("slots_in", (SLOTS * P, D), F32).ap()
    ys = nc.dram_tensor("slots_out", (SLOTS * P, D), F32).ap()
    build(nc, *args, out, xs, ys)
    r = _run(nc, [arrays], core_ids=[0])
    return r.results[0]["out_0"]
```

```python
from contextlib import ExitStack

import numpy as np

import concourse.bass as bass
from concourse import mybir

ALU = mybir.AluOpType
ACT = mybir.ActivationFunctionType
AX = mybir.AxisListType
F32 = mybir.dt.float32
BF16 = mybir.dt.bfloat16
I32 = mybir.dt.int32
U32 = mybir.dt.uint32

P = 128
D = 128
B = 8
T = 256
NT = B * T // P
EPS = 1e-5

HA = 8
KA = 64
VA = D // HA
RT = T // HA
SCALE_A = 1.0 / 8.0

NE = 8
MLP = 512
MC = MLP // P
SLOTS = NT + NE - 1

HB = 16
DB = D // HB
LAT = 64
PAGE = 32
NPG = T // PAGE
SCALE_B = float(1.0 / np.sqrt(np.float32(DB)))
MASKED = -1e30


class Chain:

    def __init__(self, eng, sem):
        self.eng, self.sem, self.base, self.k = eng, sem, 0, 0

    def inc(self, ins):
        ins.then_inc(self.sem, 1)
        self.k += 1

    def wait(self):
        self.eng.wait_ge(self.sem, self.base + self.k)

    def link(self, ins):
        self.inc(ins)
        self.wait()

    def restart(self, base):
        self.base, self.k = base, 0


def build(nc, x_in, Mq_in, Mk_in, Mv_in, wq_in, wdown_in, wkup_in, wvup_in, wo_in,
          wg_in, bg_in, W1_in, b1_in, W2_in, b2_in, cst_in, sel_in, out, xs_dram, ys_dram):
    with ExitStack() as ctx:
        def sb(name, shape, dt=F32):
            return ctx.enter_context(nc.sbuf_tensor(name, shape, dt))

        def sem(name):
            return ctx.enter_context(nc.semaphore(name))

        x = sb("x", [P, NT, D])
        xn = sb("xn", [P, NT, D])
        xnT = sb("xnT", [D, NT, P])
        cst = sb("cst", [P, NCST])
        def const(name):
            a, b = CST[name]
            return cst[:, a:b]
        ident = const("ident")
        stat = sb("stat", [P, NT, 6])
        mv = sb("mv", [P, NT, 2])
        rstd = sb("rstd", [P, 2, NT])
        Mq = sb("Mq", [D, HA * KA])
        Mk = sb("Mk", [D, HA * KA])
        Mv = sb("Mv", [D, HA * VA])
        xb = sb("xb", [D, 2, T])
        QT = sb("QT", [P, 2, HA, P])
        KT = sb("KT", [P, 2, 2, 4, HA, RT])
        Va = sb("Va", [P, 2, 2, HA * VA])
        E = sb("E", [P, 4, 2, 2, T])
        nmax = sb("nmax", [P, 4, 4])
        den = sb("den", [P, 4, 4])
        rden = sb("rden", [P, 4, 4])
        vs = sb("vs", [P, 4, 2, 2, HA * VA])
        OT = sb("OT", [P, 2, 2, 4, RT])

        W1 = sb("W1", [D, NE, MLP])
        W2 = sb("W2", [P, NE, MC, D])
        b1 = sb("b1", [P, NE, MLP])
        b2 = sb("b2", [P, NE, D])
        wg = sb("wg", [D, NE])
        bg = sb("bg", [P, NE])
        zeros = sb("zeros", [P, D])
        lg = sb("lg", [P, NT, NE])
        lmax = sb("lmax", [P, NT])
        lsub = sb("lsub", [P, NT, NE])
        lexp = sb("lexp", [P, NT, NE])
        route_p = sb("route_p", [P, 2, NT])
        cand = sb("cand", [P, NT, NE])
        cmax = sb("cmax", [P, NT])
        onehot = sb("onehot", [P, NE, NT])
        count = sb("count", [P, NE, NT])
        above = sb("above", [P, NE, NT])
        tiles = sb("tiles", [P, 4, NE])
        place = sb("place", [P, NE, NT])
        pos_f = sb("pos_f", [P, NT])
        pos = sb("pos", [P, NT], U32)
        past = sb("past", [P, SLOTS, NE])
        expert_f = sb("expert_f", [P, SLOTS])
        expert = sb("expert", [P, SLOTS], I32)
        xg = sb("xg", [P, 2, D])
        xgT = sb("xgT", [D, 2, P])
        hb = sb("hb", [P, 2, MLP])
        hT = sb("hT", [P, 2, MC, P])
        yo = sb("yo", [P, 2, D])
        yg = sb("yg", [P, NT, D])

        sel = sb("sel", [P, HB, P], BF16)
        identb = sb("identb", [P, P], BF16)
        wq = sb("wq", [D, HB * DB])
        wdown = sb("wdown", [D, LAT])
        wkv = sb("wkv", [LAT, 2 * D])
        wo = sb("wo", [D, D])
        latT = sb("latT", [LAT, T])
        turn = sb("turn", [P, 2, 2, 2, D])
        rest = sb("rest", [P, 2, 2, D])
        rest2 = sb("rest2", [P, 2, 2, D])
        qs = sb("qs", [P, 2, 2, HB, 64], BF16)
        ks = sb("ks", [P, 2, 2, HB, 64], BF16)
        vst = sb("vst", [P, 2, 2, D])
        Vb = sb("Vb", [P, 2, 2, HB, 32])
        nm = sb("nm", [P, 2, HB])
        nmr = sb("nmr", [P, 2, HB])
        ms = sb("ms", [P, 2, P], BF16)
        mT = sb("mT", [P, 2, P], BF16)
        rsum = sb("rsum", [P, 2, HB])
        OTb = vs[:, :, :, :, :].rearrange("p s h c n -> p (s h c n)").rearrange(
            "p (a q t) -> p a q t", a=2, t=T)
        spare = OT[:, :, :, :, :].rearrange("p h j s i -> p (h j s i)").rearrange("p (k u c) -> p k u c", k=2, u=2)
        att, attT = spare[:, 0, :, :], spare[:, 1, :, :]
        qT = QT[:, :, :, :].rearrange("p a j t -> p (a j t)").bitcast(BF16).rearrange(
            "p (a n t) -> p a n t", a=2, t=T)
        kT = KT[:, :, :, :, :, :].rearrange("p a h s j i -> p (a h s j i)").bitcast(BF16).rearrange(
            "p (a n h t) -> p a n h t", a=2, h=2, t=T)
        Eb = E[:, :, :, :, :].rearrange("p s h c q -> p (s h c q)")[:, 0:2 * 3 * 512].rearrange(
            "p (a k c) -> p a k c", a=2, c=512)

        pb = [ctx.enter_context(nc.psum_tensor(f"bank{i}", [P, 512], F32)) for i in range(4)]
        S4 = ctx.enter_context(nc.psum_tensor("S4", [P, 4, 512], F32))
        S = [S4[:, 0:2, :], S4[:, 2:4, :]]

        loaded = sem("loaded")
        x_loaded = sem("x_loaded")
        stored = sem("stored")

        norm = []
        for n in range(4):
            norm.append({k: sem(f"n{n}_{k}") for k in
                         ("stats", "mv", "vareps", "rstd", "xn", "xt", "xnT")})
        a_zero = sem("a_zero")
        a_xb = sem("a_xb")
        a_proj = sem("a_proj")
        a_evd = sem("a_evd")
        a_eva = sem("a_eva")
        a_scores = sem("a_scores")
        a_max = sem("a_max")
        a_exp = sem("a_exp")
        a_rden = sem("a_rden")
        a_vs = sem("a_vs")
        a_av = sem("a_av")
        a_ot = sem("a_ot")
        a_f = sem("a_f")
        a_x = sem("a_x")

        ffn = []
        for n in range(2):
            ffn.append({k: sem(f"f{n}_{k}") for k in
                        ("logits", "chain", "exp", "counts", "totals", "pos", "table", "scattered",
                         "in0", "in1", "xt", "xgT", "h", "hb", "ht", "hT", "y", "yo",
                         "out0", "out1", "back0", "back1", "back2", "back3", "x")})
        bs = {k: sem(f"b_{k}") for k in
              ("const", "zero", "xb", "p1", "latT", "turnq", "p2", "turnk", "v", "vb", "chain", "split", "rep", "tq", "qT", "tk",
               "kT", "s", "max", "mchain", "ms", "mt", "mT", "st", "exp", "pv", "ot", "on", "rsum", "att",
               "at", "attT", "y", "x")}
        b_loaded = sem("b_loaded")
        sel_loaded = sem("sel_loaded")
        w_loaded = sem("w_loaded")
        pool_const = sem("pool_const")
        slots_zero = sem("slots_zero")

        block = ctx.enter_context(nc.Block())

        def waits(eng, s, value):
            if not isinstance(value, int) or value > 0:
                eng.wait_ge(s, value)

        def live(tile):
            return not isinstance(tile, int) or 0 <= tile < SLOTS

        def there(b):
            return not isinstance(b, int) or 0 <= b < B

        def b_rounds(eng, round_):
            for b in (-1, 0):
                round_(b, b % 2)
            with eng.Fori(0, 2) as h:
                round_(h * 2 + 1, 1)
                round_(h * 2 + 2, 0)
            for b in range(5, B + 1):
                round_(b, b % 2)

        def slot_steps(eng, step, last):
            for s in range(-1, 3):
                step(s, s % 2)
            with eng.Fori(1, (SLOTS - 3) // 2) as k:
                step(k * 2 + 1, 1)
                step(k * 2 + 2, 0)
            for s in range(SLOTS - 2, last + 1):
                step(s, s % 2)

        x_view = x_in.rearrange("b (u p) d -> p (b u) d", p=P)
        out_view = out.rearrange("b (u p) d -> p (b u) d", p=P)

        @block.sync
        def _(sp):
            for g in range(4):
                sp.dma_start(x[:, 4 * g:4 * g + 4, :], x_view[:, 4 * g:4 * g + 4, :]).then_inc(x_loaded, 16)
                sp.wait_ge(x_loaded, 16 * g + 16)
            sp.dma_start(cst[:, :], cst_in).then_inc(loaded, 16)
            sp.dma_start(Mq[:, :], Mq_in).then_inc(loaded, 16)
            sp.dma_start(Mk[:, :], Mk_in).then_inc(loaded, 16)
            sp.dma_start(Mv[:, :], Mv_in).then_inc(loaded, 16)
            sp.dma_start(yg[:, :, :], sel_in.rearrange("p (h k) -> p h k", h=HB)).then_inc(sel_loaded, 16)
            sp.dma_start(wq[:, :], wq_in).then_inc(b_loaded, 16)
            sp.dma_start(wdown[:, :], wdown_in).then_inc(b_loaded, 16)
            sp.dma_start(wkv[:, 0:D], wkup_in).then_inc(b_loaded, 16)
            sp.dma_start(wkv[:, D:2 * D], wvup_in).then_inc(b_loaded, 16)
            sp.dma_start(wo[:, :], wo_in).then_inc(b_loaded, 16)
            sp.dma_start(wg[:, :], wg_in).then_inc(w_loaded, 16)
            sp.dma_start(bg[:, :], bg_in.unsqueeze(0).to_broadcast([P, NE])).then_inc(w_loaded, 16)
            sp.dma_start(W1[:, :, :], W1_in.rearrange("e d m -> d e m")).then_inc(w_loaded, 16)
            sp.dma_start(W2[:, :, :, :], W2_in.rearrange("e (c p) d -> p e c d", p=P)).then_inc(w_loaded, 16)
            sp.dma_start(b1[:, :, :], b1_in.unsqueeze(0).to_broadcast([P, NE, MLP])).then_inc(w_loaded, 16)
            sp.dma_start(b2[:, :, :], b2_in.unsqueeze(0).to_broadcast([P, NE, D])).then_inc(w_loaded, 16)
            sp.wait_ge(pool_const, 1)
            sp.dma_start(xs_dram.rearrange("(s p) d -> p s d", p=P),
                         zeros[:, :].unsqueeze(1).to_broadcast([P, SLOTS, D])).then_inc(slots_zero, 16)

            def ffn_loads(n):
                f = ffn[n]
                sp.wait_ge(f["scattered"], 16 * NT)

                def load(s, par):
                    waits(sp, f["xt"], s - 1)
                    sp.dma_start(xg[:, par, :], xs_dram[bass.ds(s * P, P), :]).then_inc(f[f"in{par}"], 16)

                load(0, 0)
                load(1, 1)
                with sp.Fori(1, SLOTS // 2) as k:
                    load(k * 2, 0)
                    load(k * 2 + 1, 1)
                load(SLOTS - 1, 0)

            ffn_loads(0)
            ffn_loads(1)
            sp.wait_ge(ffn[1]["x"], NT)
            sp.dma_start(out_view, x[:, :, :]).then_inc(stored, 16)
            sp.wait_ge(stored, 16)

        def evacuate_a(eng, p, i, bank):
            copy = eng.tensor_copy if eng.engine == mybir.EngineType.DVE else eng.copy
            j0 = 4 * bank
            if i == 0:
                src = pb[bank][:, :].rearrange("p (j t) -> p j t", j=4)
                if eng.engine == mybir.EngineType.DVE:
                    return eng.tensor_scalar(QT[:, p, j0:j0 + 4, :], src, SCALE_A, None, ALU.mult)
                return eng.mul(QT[:, p, j0:j0 + 4, :], src, SCALE_A)
            if i == 1:
                for jj in range(2):
                    for h in range(2):
                        src = pb[bank][64 * jj:64 * jj + 64, :].rearrange("p (m h t) -> p m h t", m=2, h=2)
                        dst = KT[64 * h:64 * h + 64, p, h, :, j0 + jj:j0 + 4:2, :].rearrange("p s m i -> p m s i")
                        last = copy(dst, src[:, :, h, :].rearrange("p m (s i) -> p m s i", s=4))
                return last
            src = pb[bank][:, 0:HA * 32].rearrange("p (j c d) -> p j c d", j=HA, c=2)
            last = copy(Va[:, p, :, :].rearrange("p c (j d) -> p j c d", d=VA), src)
            return last

        @block.vector
        def _(dve):
            def normalise(n, x_ready):
                s = norm[n]
                for t in range(NT):
                    x_ready(t)
                    dve.bn_stats(stat[:, t, :], x[:, t, :]).then_inc(s["stats"], 1)
                for t in range(NT):
                    dve.wait_ge(s["stats"], t + 1)
                    dve.bn_aggr(mv[:, t, :], stat[:, t, :]).then_inc(s["mv"], 1)
                dve.wait_ge(s["rstd"], 1)
                for t in range(NT):
                    dve.tensor_scalar(xn[:, t, :], x[:, t, :], mv[:, t, 0:1], rstd[:, 0, t:t + 1],
                                      ALU.subtract, ALU.mult).then_inc(s["xn"], 1)

            normalise(0, lambda t: dve.wait_ge(x_loaded, 16 * (t // 4) + 16))

            def a_evacuate(b, p, i):
                dve.wait_ge(a_proj, b * 5 + 2 * i + 1)
                evacuate_a(dve, p, i, 0).then_inc(a_evd, 1)

            def a_step(b, hp, p, lag, nxt):
                g = b * 4 + hp
                dve.wait_ge(a_scores, g + 1)
                dve.tensor_reduce(nmax[:, hp, :], S4[:, 2 * (hp % 2):2 * (hp % 2) + 2, :]
                                  .rearrange("p h (c q) -> p h c q", c=2), AX.X, ALU.max,
                                  negate=True).then_inc(a_max, 1)
                if nxt and hp < 3:
                    a_evacuate(b + 1, 1 - p, hp)
                if hp or lag:
                    a_recip(b * 4 + hp - 1, (hp + 3) % 4)
                if hp == 2 and lag:
                    a_add(b - 1)
                if hp >= 2 or lag:
                    a_outT(g - 2, (hp + 2) % 4)

            def a_recip(g, q):
                dve.wait_ge(a_exp, g + 1)
                dve.reciprocal(rden[:, q, :], den[:, q, :]).then_inc(a_rden, 1)

            def a_outT(g, q):
                dve.wait_ge(a_av, g + 1)
                dve.tensor_copy(OT[:, :, :, q, :], pb[2][:, 0:128].rearrange("p (h j i) -> p h j i", h=2, j=2)
                                ).then_inc(a_ot, 1)

            def a_add(b):
                dve.wait_ge(a_f, b + 1)
                xs = x[:, bass.ds(b * 2, 2), :]
                dve.tensor_tensor(xs, xs, pb[3][:, 0:256].rearrange("p (h c) -> p h c", h=2), ALU.add
                                  ).then_inc(a_x, 1)

            dve.wait_ge(a_zero, 1)
            for i in range(3):
                a_evacuate(0, 0, i)
            for hp in range(4):
                a_step(0, hp, 0, False, True)
            with dve.Fori(0, 3) as h:
                for hp in range(4):
                    a_step(h * 2 + 1, hp, 1, True, True)
                for hp in range(4):
                    a_step(h * 2 + 2, hp, 0, True, True)
            for hp in range(4):
                a_step(7, hp, 1, True, False)
            a_recip(31, 3)
            a_outT(30, 2)
            a_outT(31, 3)
            a_add(7)

            def ffn_route(n):
                f = ffn[n]
                chain = Chain(dve, f["chain"])
                link = chain.link
                dve.wait_ge(f["logits"], 1)
                bgb = bg[:, :].unsqueeze(1).to_broadcast([P, NT, NE])
                link(dve.tensor_tensor(lg[:, :, :], pb[2][:, 0:NT * NE].rearrange("p (t e) -> p t e", e=NE), bgb, ALU.add))
                link(dve.tensor_reduce(lmax[:, :], lg[:, :, :], AX.X, ALU.max))
                lmb = lmax[:, :].unsqueeze(2).to_broadcast([P, NT, NE])
                dve.tensor_tensor(lsub[:, :, :], lg[:, :, :], lmb, ALU.subtract).then_inc(f["exp"], 1)
                link(dve.tensor_tensor(cand[:, :, :], lg[:, :, :], lmb, ALU.is_equal))
                link(dve.tensor_tensor(cand[:, :, :], cand[:, :, :],
                                       const("order").unsqueeze(1).to_broadcast([P, NT, NE]), ALU.mult))
                link(dve.tensor_reduce(cmax[:, :], cand[:, :, :], AX.X, ALU.max))
                link(dve.tensor_tensor(onehot[:, :, :].rearrange("p e t -> p t e"), cand[:, :, :],
                                       cmax[:, :].unsqueeze(2).to_broadcast([P, NT, NE]), ALU.is_equal))
                dve.tensor_tensor_scan(count[:, :, :].rearrange("p e t -> p (e t)"), const("within"),
                                       onehot[:, :, :].rearrange("p e t -> p (e t)"), 0.0, ALU.mult, ALU.add
                                       ).then_inc(f["counts"], 1)
                dve.wait_ge(f["totals"], 1)
                earlier, total = pb[3][:, 0:NE], pb[3][:, NE:2 * NE]
                link(dve.tensor_tensor(above[:, :, :], total.unsqueeze(2).to_broadcast([P, NE, NT]),
                                       const("steps").unsqueeze(1).to_broadcast([P, NE, NT]), ALU.is_gt))
                link(dve.tensor_reduce(tiles[:, 0, :], above[:, :, :], AX.X, ALU.add))
                link(dve.tensor_tensor_scan(tiles[:, 1, :], const("ones")[:, 0:NE], tiles[:, 0, :], 0.0,
                                            ALU.mult, ALU.add))
                link(dve.tensor_tensor(tiles[:, 2, :], tiles[:, 1, :], tiles[:, 0, :], ALU.subtract))
                link(dve.scalar_tensor_tensor(out=tiles[:, 3, :], in0=tiles[:, 2, :], scalar=float(P),
                                              in1=earlier, op0=ALU.mult, op1=ALU.add))
                link(dve.tensor_tensor(place[:, :, :], count[:, :, :],
                                       tiles[:, 3, :].unsqueeze(2).to_broadcast([P, NE, NT]), ALU.add))
                link(dve.scalar_tensor_tensor(out=place[:, :, :], in0=place[:, :, :], scalar=-1.0,
                                              in1=onehot[:, :, :], op0=ALU.add, op1=ALU.mult))
                link(dve.tensor_reduce(pos_f[:, :], place[:, :, :].rearrange("p e t -> p t e"), AX.X, ALU.add))
                dve.tensor_copy(pos[:, :], pos_f[:, :]).then_inc(f["pos"], 1)
                link(dve.tensor_tensor(past[:, :, :],
                                       const("slots").unsqueeze(2).to_broadcast([P, SLOTS, NE]),
                                       tiles[:, 1, :].unsqueeze(1).to_broadcast([P, SLOTS, NE]), ALU.is_ge))
                link(dve.tensor_reduce(expert_f[:, :], past[:, :, :], AX.X, ALU.add))
                dve.tensor_scalar(expert[:, :], expert_f[:, :], float(NE - 1), None, ALU.min).then_inc(f["table"], 1)
                dve.wait_ge(f["exp"], 2)
                link(dve.tensor_reduce(route_p[:, 1, :], lexp[:, :, :], AX.X, ALU.add))
                link(dve.reciprocal(route_p[:, 0, :], route_p[:, 1, :]))

            def ffn_tiles(n):
                f = ffn[n]
                dve.wait_ge(f["table"], 1)

                def step(s, par):
                    if live(s + 1):
                        dve.wait_ge(f["xt"], s + 2)
                        waits(dve, f["h"], s)
                        dve.tensor_copy(xgT[:, 1 - par, :], pb[0][:, 0:P]).then_inc(f["xgT"], 1)
                    if live(s):
                        e = dve.value_load(expert[0:1, bass.ds(s, 1)], min_val=0, max_val=NE - 1)
                        dve.wait_ge(f["h"], s + 1)
                        waits(dve, f["ht"], s - 1)
                        dve.tensor_tensor(hb[:, par, :], S4[:, par, :], b1[:, bass.ds(e, 1), :].squeeze(1), ALU.add
                                          ).then_inc(f["hb"], 1)
                    if live(s - 2):
                        e2 = dve.value_load(expert[0:1, bass.ds(s - 2, 1)], min_val=0, max_val=NE - 1)
                        dve.wait_ge(f["y"], s - 1)
                        if isinstance(s, int):
                            waits(dve, f[f"out{par}"], 16 * ((s - 2) // 2))
                        else:
                            dve.wait_ge(f[f"out{par}"], (s - 2 - par) * 8)
                        dve.tensor_tensor(yo[:, par, :], pb[1 + par][:, 0:D], b2[:, bass.ds(e2, 1), :].squeeze(1),
                                          ALU.add).then_inc(f["yo"], 1)

                slot_steps(dve, step, SLOTS + 1)

            def ffn_add(n):
                f = ffn[n]
                for t in range(NT):
                    if t % 4 == 0:
                        dve.wait_ge(f[f"back{t // 4}"], 64)
                    dve.scalar_tensor_tensor(out=x[:, t, :], in0=yg[:, t, :], scalar=route_p[:, 0, t:t + 1],
                                             in1=x[:, t, :], op0=ALU.mult, op1=ALU.add).then_inc(f["x"], 1)

            normalise(1, lambda t: dve.wait_ge(a_x, t // 2 + 1))
            dve.wait_ge(w_loaded, 96)
            ffn_route(0)
            ffn_tiles(0)
            ffn_add(0)

            def b_turn(b, i, src, done):
                dve.wait_ge(bs["latT"] if i == 0 else bs["v"], b + 1)
                cos = const("cos").rearrange("p (u d) -> p u d", u=2)
                sin = const("sin").rearrange("p (u r) -> p u r", u=2)
                for u in range(2):
                    v = src(u).rearrange("p (h d) -> p h d", d=DB)
                    o = [turn[:, k, i, u, :].rearrange("p (h d) -> p h d", d=DB) for k in range(2)]
                    c = cos[:, u, :].unsqueeze(1).to_broadcast([P, HB, DB])
                    sn = sin[:, u, 0:DB].unsqueeze(1).to_broadcast([P, HB, DB])
                    dve.tensor_tensor(o[0], v, c, ALU.mult)
                    dve.tensor_tensor(o[1][:, :, 0:DB:2], v[:, :, 1:DB:2], sn[:, :, 0:DB:2], ALU.mult)
                    last = dve.tensor_tensor(o[1][:, :, 1:DB:2], v[:, :, 0:DB:2], sn[:, :, 1:DB:2], ALU.mult)
                last.then_inc(done, 1)

            def b_kT(b, p, i):
                dve.wait_ge(bs["tk"], b * 2 + i + 1)
                for h in range(2):
                    rows = slice(64 * h, 64 * h + 64)
                    src = pb[0][rows, :].bitcast(BF16).rearrange("p (n t) -> p n t", n=4)
                    last = dve.tensor_copy(kT[rows, p, 4 * i:4 * i + 4, h, :], src)
                last.then_inc(bs["kT"], 1)

            def b_repeat(b, p):
                dve.wait_ge(bs["split"], b + 1)
                waits(dve, bs["tk"], b * 2 - 2)
                for t, hi, mid in ((qs, (0, 1), (2, 3)), (ks, (0, 2), (1, 3))):
                    v = t[:, p, :, :, :].rearrange("p u h c -> p (u h) c")
                    dst = v[:, :, 8 * hi[1]:64].rearrange("p n c -> p n c")
                    dst = v[:, :, 8 * hi[1]:8 * hi[1] + 32].rearrange("p n (m d) -> p n m d", d=8)[:, :, 0:4:3, :]
                    dve.tensor_copy(dst, v[:, :, 0:8].unsqueeze(2).to_broadcast([P, 2 * HB, 2, 8]))
                    last = dve.tensor_copy(v[:, :, 8 * mid[1]:8 * mid[1] + 8], v[:, :, 8 * mid[0]:8 * mid[0] + 8])
                last.then_inc(bs["rep"], 1)

            def b_max(b, q):
                dve.wait_ge(bs["s"], b * 4 + q + 1)
                if q == 0:
                    waits(dve, bs["ms"], b)
                for d in range(2):
                    h0 = 4 * q + 2 * d
                    dve.tensor_reduce(nm[:, 1, h0:h0 + 2], pb[2 + d][:, :].rearrange("p (h k) -> p h k", h=2),
                                      AX.X, ALU.max, negate=True)
                dve.tensor_reduce(nm[:, 0, 4 * q:4 * q + 4], S4[:, 3, :].rearrange("p (h k) -> p h k", h=4),
                                  AX.X, ALU.max, negate=True).then_inc(bs["max"], 1)

            def b_normal(b, u):
                dve.wait_ge(bs["on"], b * 2 + u + 1)
                o = pb[1][:, :].rearrange("p (h r) -> p h r", r=32)
                dve.reciprocal(rsum[:, u, :], o[:, :, DB]).then_inc(bs["rsum"], 1)
                dve.wait_ge(bs["rsum"], b * 2 + u + 1)
                waits(dve, bs["at"], b)
                dve.tensor_tensor(att[:, u, :].rearrange("p (h d) -> p h d", d=DB), o[:, :, 0:DB],
                                  rsum[:, u, :].unsqueeze(2).to_broadcast([P, HB, DB]), ALU.mult
                                  ).then_inc(bs["att"], 1)

            def b_turn_q(b):
                dve.wait_ge(bs["p1"], b + 1)
                waits(dve, bs["split"], b)
                b_turn(b, 0, lambda u: pb[0][:, u * D:(u + 1) * D], bs["turnq"])

            def b_turn_k(b):
                dve.wait_ge(bs["p2"], b + 1)
                b_turn(b, 1, lambda u: pb[0][:, 2 * u * D:(2 * u + 1) * D], bs["turnk"])

            def b_round(b, p):
                n, nn, nnn, l = there(b + 1), there(b + 2), there(b + 3), there(b - 1)
                if n: b_kT(b + 1, 1 - p, 0)
                if l: b_normal(b - 1, 0)
                if n: b_max(b + 1, 0)
                if n: b_kT(b + 1, 1 - p, 1)
                if l: b_normal(b - 1, 1)
                if n: b_max(b + 1, 1)
                if nnn: b_turn_q(b + 3)
                if n: b_max(b + 1, 2)
                if l:
                    dve.wait_ge(bs["at"], b)
                    dve.tensor_copy(attT[:, :, :], pb[1][:, 0:T].rearrange("p (u t) -> p u t", u=2)
                                    ).then_inc(bs["attT"], 1)
                if n: b_max(b + 1, 3)
                if nnn: b_turn_k(b + 3)
                if l:
                    dve.wait_ge(bs["y"], b)
                    xs = x[:, bass.ds((b - 1) * 2, 2), :]
                    dve.tensor_tensor(xs, xs, pb[1][:, 0:T].rearrange("p (u c) -> p u c", u=2), ALU.add
                                      ).then_inc(bs["x"], 1)
                if nn: b_repeat(b + 2, p)

            normalise(2, lambda t: dve.wait_ge(ffn[0]["x"], t + 1))
            for b in range(2):
                b_turn_q(b)
                b_turn_k(b)
                if b == 0:
                    b_repeat(0, 0)
            b_rounds(dve, b_round)
            normalise(3, lambda t: dve.wait_ge(bs["x"], t // 2 + 1))
            ffn_route(1)
            ffn_tiles(1)
            ffn_add(1)

        @block.scalar
        def _(act):
            def transposed(n):
                s = norm[n]
                for g in range(4):
                    act.wait_ge(s["xt"], 4 * g + 4)
                    act.copy(xnT[:, 4 * g:4 * g + 4, :], pb[g % 2][:, :].rearrange("p (t c) -> p t c", t=4)
                             ).then_inc(s["xnT"], 1)

            transposed(0)

            def a_evacuate(b, p, i):
                act.wait_ge(a_proj, b * 5 + 2 * i + 2)
                evacuate_a(act, p, i, 1).then_inc(a_eva, 1)

            def a_step(b, hp, p, lag, nxt):
                g = b * 4 + hp
                act.wait_ge(a_max, g + 1)
                if lag:
                    act.wait_ge(a_av, g - 3)
                    act.wait_ge(a_rden, g - 3)
                for h in range(2):
                    for c in range(2):
                        k = 2 * h + c
                        last = act.activation(E[:, hp, h, c, :], S[hp % 2][:, h, c * T:(c + 1) * T], ACT.Exp,
                                              bias=nmax[:, hp, k:k + 1], accum_out=den[:, hp, k:k + 1])
                last.then_inc(a_exp, 1)
                if nxt and hp < 2:
                    a_evacuate(b + 1, 1 - p, hp)

            act.wait_ge(a_zero, 1)
            for i in range(2):
                a_evacuate(0, 0, i)
            for hp in range(4):
                a_step(0, hp, 0, False, True)
            with act.Fori(0, 3) as h:
                for hp in range(4):
                    a_step(h * 2 + 1, hp, 1, True, True)
                for hp in range(4):
                    a_step(h * 2 + 2, hp, 0, True, True)
            for hp in range(4):
                a_step(7, hp, 1, True, False)

            def ffn_exp(n):
                f = ffn[n]
                act.wait_ge(f["exp"], 1)
                act.activation(lexp[:, :, :], lsub[:, :, :], ACT.Exp).then_inc(f["exp"], 1)

            def ffn_tiles(n):
                f = ffn[n]

                def step(s, par):
                    if live(s - 1):
                        act.wait_ge(f["ht"], s)
                        waits(act, f["y"], s - 2)
                        act.activation(hT[:, 1 - par, :, :], S4[:, 3 - par, :].rearrange("p (c t) -> p c t", c=MC),
                                       ACT.Relu).then_inc(f["hT"], 1)
                    if live(s - 3):
                        act.wait_ge(f["yo"], s - 2)
                        act.dma_start(ys_dram[bass.ds((s - 3) * P, P), :], yo[:, 1 - par, :]
                                      ).then_inc(f[f"out{1 - par}"], 16)

                slot_steps(act, step, SLOTS + 2)

            transposed(1)
            ffn_exp(0)
            ffn_tiles(0)

            def b_latent(b):
                act.wait_ge(bs["p1"], b + 1)
                waits(act, bs["p2"], b)
                act.copy(latT[:, :], pb[0][0:LAT, T:2 * T]).then_inc(bs["latT"], 1)

            def b_v(b, p):
                act.wait_ge(bs["p2"], b + 1)
                src = pb[0][:, :].rearrange("p (u i h d) -> p u i h d", u=2, i=2, d=DB)
                waits(act, bs["vb"], b - 1)
                act.copy(vst[:, p, :, :].rearrange("p u (h d) -> p u h d", d=DB), src[:, :, 1, :, :]).then_inc(bs["v"], 1)

            def b_qT(b, p, i):
                act.wait_ge(bs["tq"], b * 2 + i + 1)
                src = pb[0][:, :].bitcast(BF16).rearrange("p (n t) -> p n t", n=4)
                act.copy(qT[:, p, 4 * i:4 * i + 4, :], src).then_inc(bs["qT"], 1)

            def b_exp(b, q):
                act.wait_ge(bs["st"], b * 4 + q + 1)
                waits(act, bs["pv"], b * 4 + q - 1)
                act.activation(Eb[:, q % 2, :, :], S4[:, 0:3, :], ACT.Exp, scale=SCALE_B).then_inc(bs["exp"], 1)

            def b_outT(b, p, q):
                act.wait_ge(bs["pv"], b * 4 + q + 1)
                act.copy(OTb[:, p, q, :], pb[1][:, 0:T]).then_inc(bs["ot"], 1)

            def b_round(b, p):
                n, nnn, c, l = there(b + 1), there(b + 3), there(b), there(b - 1)
                if n: b_qT(b + 1, 1 - p, 0)
                if l: b_outT(b - 1, 1 - p, 3)
                if c: b_exp(b, 0)
                if n: b_qT(b + 1, 1 - p, 1)
                if c: b_exp(b, 1)
                if c: b_outT(b, p, 0)
                if c: b_exp(b, 2)
                if nnn: b_latent(b + 3)
                if c: b_outT(b, p, 1)
                if c: b_exp(b, 3)
                if nnn: b_v(b + 3, 1 - p)
                if c: b_outT(b, p, 2)
                if n:
                    act.wait_ge(bs["mt"], b + 2)
                    act.copy(mT[:, :, :], pb[0][:, 0:P].bitcast(BF16).rearrange("p (u t) -> p u t", u=2)
                             ).then_inc(bs["mT"], 1)

            transposed(2)
            for b in range(2):
                b_latent(b)
                b_v(b, b)
            b_rounds(act, b_round)
            transposed(3)
            ffn_exp(1)
            ffn_tiles(1)

        @block.gpsimd
        def _(pool):
            pool.memset(KT[:, :, :, :, :, :], 0.0).then_inc(a_zero, 1)
            pool.memset(Vb[:, :, :, :, :], 0.0).then_inc(bs["const"], 1)
            pool.memset(ms[:, :, :], 0.0).then_inc(bs["const"], 1)
            pool.wait_ge(bs["const"], 1)
            pool.memset(Vb[:, :, :, :, DB:DB + 1], 1.0).then_inc(bs["const"], 1)

            pool.memset(zeros[:, :], 0.0).then_inc(pool_const, 1)
            pool.memset(rstd[:, 1, :], -0.5).then_inc(pool_const, 1)
            pool.wait_ge(pool_const, 2)

            def inverse_deviation(n):
                s = norm[n]
                pool.wait_ge(s["mv"], NT)
                pool.tensor_scalar(rstd[:, 0, :], mv[:, :, 1], EPS, None, ALU.add).then_inc(s["vareps"], 1)
                pool.wait_ge(s["vareps"], 1)
                pool.tensor_tensor(rstd[:, 0, :], rstd[:, 0, :], rstd[:, 1, :], ALU.pow).then_inc(s["rstd"], 1)

            inverse_deviation(0)

            def a_stage(b, p):
                pool.tensor_copy(xb[:, p, :].rearrange("p (u t) -> p u t", u=2),
                                 xnT[:, bass.ds(b * 2, 2), :]).then_inc(a_xb, 1)

            def a_values(g, q, p, reuse):
                pool.wait_ge(a_rden, g + 1)
                if reuse:
                    pool.wait_ge(a_av, g - 3)
                v = Va[:, p, :, :].unsqueeze(1).to_broadcast([P, 2, 2, HA * VA])
                r = rden[:, q, :].rearrange("p (h c) -> p h c", h=2).unsqueeze(3).to_broadcast([P, 2, 2, HA * VA])
                pool.tensor_tensor(vs[:, q, :, :, :], v, r, ALU.mult).then_inc(a_vs, 1)

            pool.wait_ge(norm[0]["xnT"], 4)
            a_stage(0, 0)
            a_stage(1, 1)
            pool.wait_ge(a_evd, 3)
            pool.wait_ge(a_eva, 2)

            def a_batch(b, p, lag, ahead):
                for hp in range(4):
                    if hp == 0:
                        pool.wait_ge(a_evd, b * 3 + 3)
                    if hp == 3 and ahead:
                        pool.wait_ge(a_proj, b * 5 + 5)
                        a_stage(b + 2, p)
                    a_values(b * 4 + hp, hp, p, lag)

            a_batch(0, 0, False, True)
            with pool.Fori(0, 2) as h:
                a_batch(h * 2 + 1, 1, True, True)
                a_batch(h * 2 + 2, 0, True, True)
            a_batch(5, 1, True, True)
            a_batch(6, 0, True, False)
            a_batch(7, 1, True, False)

            def ffn_scatter(n):
                f = ffn[n]
                pool.wait_ge(f["pos"], 1)
                for t in range(NT):
                    pool.indirect_dma_start(out=xs_dram, out_offset=bass.IndirectOffsetOnAxis(pos[:, t:t + 1], 0),
                                            in_=xn[:, t, :], in_offset=None).then_inc(f["scattered"], 16)

            def ffn_gather(n):
                f = ffn[n]
                pool.wait_ge(f["out0"], 16 * ((SLOTS + 1) // 2))
                pool.wait_ge(f["out1"], 16 * (SLOTS // 2))
                for t in range(NT):
                    pool.indirect_dma_start(out=yg[:, t, :], out_offset=None, in_=ys_dram,
                                            in_offset=bass.IndirectOffsetOnAxis(pos[:, t:t + 1], 0)
                                            ).then_inc(f[f"back{t // 4}"], 16)

            pool.wait_ge(a_scores, 4 * B)
            pool.memset(KT[:, :, :, :, :, :], 0.0).then_inc(bs["zero"], 1)
            pool.wait_ge(sel_loaded, 16)
            pool.tensor_copy(sel[:, :, :], yg[:, :, :]).then_inc(bs["const"], 1)
            pool.wait_ge(loaded, 64)
            pool.tensor_copy(identb[:, :], ident).then_inc(bs["const"], 1)
            for t, name in ((qs, "qmask"), (ks, "kmask")):
                for u in range(2):
                    for a in range(2):
                        pool.tensor_copy(t[:, a, u, :, 48:64], const(name)[:, 16 * u:16 * u + 16].unsqueeze(1)
                                         .to_broadcast([P, HB, 16])).then_inc(bs["const"], 1)
            inverse_deviation(1)
            pool.wait_ge(slots_zero, 16)
            ffn_scatter(0)
            pool.wait_ge(bs["const"], 5)
            ffn_gather(0)

            def b_stage(b, p):
                pool.tensor_copy(xb[:, p, :].rearrange("p (u t) -> p u t", u=2),
                                 xnT[:, bass.ds(b * 2, 2), :]).then_inc(bs["xb"], 1)

            def b_split(b, p):
                chain = Chain(pool, bs["chain"])
                chain.restart(b * 9)
                blocks = {"q": (0, 2, 5), "k": (0, 1, 4)}

                def part(i, k):
                    dst = (qs, ks)[i][:, p, :, :, :]
                    m = blocks["qk"[i]][k]
                    return dst[:, :, :, 8 * m:8 * m + 8].rearrange("p u h d -> p (u h) d")

                def view(t, i):
                    return t[:, i, :, :].rearrange("p u (h d) -> p (u h) d", d=DB)

                pool.wait_ge(bs["turnq"], b + 1)
                pool.wait_ge(bs["turnk"], b + 1)
                flat = [turn[:, k, :, :, :].rearrange("p i u c -> p (i u c)") for k in range(2)]
                chain.inc(pool.tensor_tensor(rest[:, :, :, :].rearrange("p i u c -> p (i u c)"), flat[0], flat[1], ALU.add))
                waits(pool, bs["tk"], b * 2 - 2)
                for i in range(2):
                    chain.inc(pool.tensor_tensor(part(i, 0), view(turn[:, 0, :, :, :], i), view(turn[:, 1, :, :, :], i),
                                                 ALU.add))
                chain.wait()
                for i in range(2):
                    hi = part(i, 0)
                    chain.inc(pool.tensor_tensor(part(i, 1), view(rest, i), hi, ALU.subtract))
                    chain.inc(pool.tensor_tensor(view(rest2, i), view(rest, i), hi, ALU.subtract))
                chain.wait()
                for i in range(2):
                    mid = part(i, 1)
                    chain.inc(pool.tensor_tensor(part(i, 2), view(rest2, i), mid, ALU.subtract))
                chain.wait()
                assert chain.k == 9
                pool.sem_inc(bs["split"], 1)

            def b_maxima(b):
                chain = Chain(pool, bs["mchain"])
                chain.restart(b * 4)
                pool.wait_ge(bs["max"], b * 4 + 4)
                waits(pool, bs["mt"], b)
                parts = ms[:, :, 0:3 * HB].rearrange("p u (h k) -> p u h k", k=3)
                chain.link(pool.tensor_tensor(
                    parts[:, :, :, 0], nm[:, :, :], zeros[:, 0:2 * HB].rearrange("p (u h) -> p u h", u=2), ALU.add))
                chain.inc(pool.tensor_tensor(nmr[:, :, :], nm[:, :, :], parts[:, :, :, 0], ALU.subtract))
                chain.link(pool.tensor_tensor(parts[:, :, :, 1], nm[:, :, :], parts[:, :, :, 0], ALU.subtract))
                chain.link(pool.tensor_tensor(parts[:, :, :, 2], nmr[:, :, :], parts[:, :, :, 1], ALU.subtract))
                pool.sem_inc(bs["ms"], 1)

            def b_place_v(b, p):
                pool.wait_ge(bs["v"], b + 1)
                waits(pool, bs["pv"], b * 4 - 4)
                z = zeros[:, :].rearrange("p (h d) -> p h d", d=DB)
                for u in range(2):
                    last = pool.tensor_tensor(Vb[:, p, u, :, 0:DB], vst[:, p, u, :].rearrange("p (h d) -> p h d", d=DB), z,
                                              ALU.add)
                last.then_inc(bs["vb"], 1)

            def b_round(b, p):
                if there(b + 1):
                    b_place_v(b + 1, 1 - p)
                if there(b + 2):
                    b_split(b + 2, p)
                if there(b + 4):
                    pool.wait_ge(bs["latT"], b + 3)
                    b_stage(b + 4, p)
                if there(b + 1):
                    b_maxima(b + 1)

            inverse_deviation(2)
            pool.wait_ge(norm[2]["xnT"], 4)
            b_stage(0, 0)
            b_stage(1, 1)
            b_split(0, 0)
            pool.wait_ge(bs["latT"], 1)
            b_stage(2, 0)
            for b in (-1, 0):
                b_round(b, b % 2)
            with pool.Fori(0, 1) as h:
                b_round(h * 2 + 1, 1)
                b_round(h * 2 + 2, 0)
            for b in range(3, B + 1):
                b_round(b, b % 2)
            inverse_deviation(3)
            ffn_scatter(1)
            ffn_gather(1)

        @block.tensor
        def _(pe):
            def transpose(n):
                s = norm[n]
                for t in range(NT):
                    pe.wait_ge(s["xn"], t + 1)
                    if t >= 8 and t % 4 == 0:
                        pe.wait_ge(s["xnT"], t // 4 - 1)
                    pe.transpose(pb[t // 4 % 2][:, (t % 4) * P:(t % 4 + 1) * P], xn[:, t, :], ident
                                 ).then_inc(s["xt"], 1)

            pe.wait_ge(loaded, 64)
            transpose(0)

            def a_project(b, p, i, free):
                if i == 0:
                    pe.wait_ge(a_xb, b + 1)
                for bank in range(2 if i < 2 else 1):
                    if free and bank == 0:
                        pe.wait_ge(a_evd, b * 3 + i)
                    if free and bank == 1:
                        pe.wait_ge(a_eva, b * 2 + i)
                    dst = pb[bank]
                    if i == 0:
                        for j in range(4):
                            for h in range(2):
                                jq = 4 * bank + j
                                last = pe.matmul(dst[64 * h:64 * h + 64, j * P:(j + 1) * P],
                                                 Mq[:, jq * KA:(jq + 1) * KA], xb[:, p, h * P:(h + 1) * P],
                                                 start=True, stop=True)
                    elif i == 1:
                        for m in range(2):
                            mq = 2 * bank + m
                            last = pe.matmul(dst[:, m * T:(m + 1) * T], Mk[:, mq * P:(mq + 1) * P],
                                             xb[:, p, :], start=True, stop=True)
                    else:
                        for j in range(HA):
                            for g in range(4):
                                last = pe.matmul(dst[32 * g:32 * g + 32, 32 * j:32 * j + 32],
                                                 xb[:, p, j * RT:(j + 1) * RT],
                                                 Mv[:, :].rearrange("p (c g d) -> p c g d", c=2, g=4)[:, :, g, :],
                                                 start=True, stop=True)
                    last.then_inc(a_proj, 1)

            def a_values_out(g, q):
                pe.wait_ge(a_vs, g + 1)
                for h in range(2):
                    for c in range(2):
                        for jp in range(4):
                            last = pe.matmul(pb[2][32 * jp:32 * jp + 32, 64 * h:64 * h + 64],
                                             vs[:, q, h, c, 32 * jp:32 * jp + 32],
                                             E[:, q, h, c, 64 * jp:64 * jp + 64], start=(c == 0), stop=(c == 1))
                last.then_inc(a_av, 1)

            def a_final(b):
                pe.wait_ge(a_ot, b * 4 + 4)
                for h in range(2):
                    for jj in range(2):
                        last = pe.matmul(pb[3][:, h * P:(h + 1) * P], OT[:, h, jj, :, :],
                                         const("pick")[:, jj * P:(jj + 1) * P], start=(jj == 0), stop=(jj == 1))
                last.then_inc(a_f, 1)

            def a_step(b, hp, p, lag, nxt):
                g = b * 4 + hp
                if hp >= 2 or lag:
                    pe.wait_ge(a_exp, g - 1)
                if hp == 0:
                    pe.wait_ge(a_evd, b * 3 + 3)
                    pe.wait_ge(a_eva, b * 2 + 2)
                for h in range(2):
                    for c in range(2):
                        last = pe.matmul(S[hp % 2][:, h, c * T:(c + 1) * T],
                                         KT[:, p, h, hp, 4 * c:4 * c + 4, :],
                                         QT[:, p, :, hp * RT:(hp + 1) * RT], start=True, stop=True)
                last.then_inc(a_scores, 1)
                if nxt and hp < 3:
                    a_project(b + 1, 1 - p, hp, True)
                if hp == 2 and lag:
                    a_final(b - 1)
                if hp >= 2 or lag:
                    if not (hp == 2 and not lag):
                        pe.wait_ge(a_ot, g - 2)
                    a_values_out(g - 2, (hp + 2) % 4)

            for i in range(3):
                if i == 0:
                    pe.wait_ge(norm[0]["xnT"], 4)
                a_project(0, 0, i, i > 0)
            for hp in range(4):
                a_step(0, hp, 0, False, True)
            with pe.Fori(0, 3) as h:
                for hp in range(4):
                    a_step(h * 2 + 1, hp, 1, True, True)
                for hp in range(4):
                    a_step(h * 2 + 2, hp, 0, True, True)
            for hp in range(4):
                a_step(7, hp, 1, True, False)
            for g in (30, 31):
                pe.wait_ge(a_ot, g)
                a_values_out(g, g % 4)
            a_final(7)

            def ffn_logits(n):
                f, s = ffn[n], norm[2 * n + 1]
                for t in range(NT):
                    pe.wait_ge(s["xnT"], t // 4 + 1)
                    last = pe.matmul(pb[2][:, t * NE:(t + 1) * NE], xnT[:, t, :], wg[:, :], start=True, stop=True)
                last.then_inc(f["logits"], 1)
                pe.wait_ge(f["counts"], 1)
                row = count[:, :, NT - 1]
                pe.matmul(pb[3][:, 0:NE], const("before"), row, start=True, stop=True)
                pe.matmul(pb[3][:, NE:2 * NE], const("ones"), row, start=True, stop=True).then_inc(f["totals"], 1)

            def ffn_tiles(n):
                f = ffn[n]
                pe.wait_ge(f["table"], 1)

                def step(s, par):
                    if live(s + 1):
                        if isinstance(s, int):
                            pe.wait_ge(f[f"in{1 - par}"], 16 * ((s + 1) // 2 + 1))
                        else:
                            pe.wait_ge(f[f"in{1 - par}"], (s + 1 - (1 - par)) * 8 + 16)
                        waits(pe, f["xgT"], s + 1)
                        pe.transpose(pb[0][:, 0:P], xg[:, 1 - par, :], ident).then_inc(f["xt"], 1)
                    if live(s):
                        e = pe.value_load(expert[0:1, bass.ds(s, 1)], min_val=0, max_val=NE - 1)
                        pe.wait_ge(f["xgT"], s + 1)
                        waits(pe, f["hb"], s - 1)
                        pe.matmul(S4[:, par, :], xgT[:, par, :], W1[:, bass.ds(e, 1), :].squeeze(1), start=True, stop=True
                                  ).then_inc(f["h"], 1)
                    if live(s - 1):
                        pe.wait_ge(f["hb"], s)
                        waits(pe, f["hT"], s - 2)
                        for c in range(MC):
                            last = pe.transpose(S4[:, 3 - par, c * P:(c + 1) * P],
                                                hb[:, 1 - par, c * P:(c + 1) * P], ident)
                        last.then_inc(f["ht"], 1)
                    if live(s - 2):
                        e2 = pe.value_load(expert[0:1, bass.ds(s - 2, 1)], min_val=0, max_val=NE - 1)
                        pe.wait_ge(f["hT"], s - 1)
                        waits(pe, f["yo"], s - 3)
                        for c in range(MC):
                            last = pe.matmul(pb[1 + par][:, 0:D], hT[:, par, c, :],
                                             W2[:, bass.ds(e2, 1), c, :].squeeze(1), start=(c == 0), stop=(c == MC - 1))
                        last.then_inc(f["y"], 1)

                slot_steps(pe, step, SLOTS + 1)

            transpose(1)
            pe.wait_ge(w_loaded, 96)
            ffn_logits(0)
            ffn_tiles(0)

            def b_q(b, p):
                pe.wait_ge(bs["xb"], b + 1)
                for u in range(2):
                    pe.matmul(pb[0][:, u * D:(u + 1) * D], xb[:, p, u * P:(u + 1) * P], wq[:, :], start=True, stop=True)
                pe.matmul(pb[0][0:LAT, T:2 * T], wdown[:, :], xb[:, p, :], start=True, stop=True).then_inc(bs["p1"], 1)

            def b_kv(b):
                pe.wait_ge(bs["latT"], b + 1)
                pe.wait_ge(bs["turnq"], b + 1)
                for u in range(2):
                    last = pe.matmul(pb[0][:, 2 * u * D:2 * (u + 1) * D], latT[:, u * P:(u + 1) * P], wkv[:, :],
                                     start=True, stop=True)
                last.then_inc(bs["p2"], 1)

            def b_transpose(src, p, i, done):
                dst = pb[0][:, :].bitcast(BF16)
                for n in range(4):
                    for u in range(2):
                        last = pe.transpose(dst[:, n * T + u * P:n * T + (u + 1) * P],
                                            src[:, p, u, 2 * (4 * i + n):2 * (4 * i + n) + 2, :]
                                            .rearrange("p h c -> p (h c)"), identb[:, :])
                last.then_inc(done, 1)

            def b_tq(b, p, i):
                if i == 0:
                    pe.wait_ge(bs["rep"], b + 1)
                b_transpose(qs, p, i, bs["tq"])

            def b_tk(b, p, i):
                pe.wait_ge(bs["qT"], b * 2 + i + 1)
                b_transpose(ks, p, i, bs["tk"])

            def b_scores(b, p, q):
                if q % 2 == 0:
                    pe.wait_ge(bs["qT"], b * 2 + 1 + q // 2)
                    pe.wait_ge(bs["kT"], b * 2 + 1 + q // 2)
                waits(pe, bs["max"], b * 4 + q)
                for d in range(2):
                    n = 2 * q + d
                    pe.matmul(pb[2 + d][:, :], qT[:, p, n, P:T], kT[:, p, n, :, :], start=True, stop=True)
                for d in range(2):
                    n = 2 * q + d
                    last = pe.matmul(S4[:, 3, d * T:(d + 1) * T], qT[:, p, n, 0:P], kT[:, p, n, :, 0:P],
                                     start=True, stop=True)
                last.then_inc(bs["s"], 1)

            def b_scoresT(b, p, q):
                if q == 0:
                    pe.wait_ge(bs["mT"], b + 1)
                waits(pe, bs["exp"], b * 4 + q)
                for d in range(2):
                    for h in range(2):
                        n, hh = 2 * q + d, 4 * q + 2 * d + h
                        dst = S4[:, d, h * T:(h + 1) * T]
                        pe.matmul(dst, kT[:, p, n, h, 0:P], qT[:, p, n, :], start=True, stop=False)
                        pe.matmul(dst, sel[:, hh, :], mT[:, :, :], start=False, stop=True)
                        dst = S4[:, 2, (2 * d + h) * P:(2 * d + h + 1) * P]
                        pe.matmul(dst, kT[:, p, n, h, P:T], qT[:, p, n, P:T], start=True, stop=False)
                        last = pe.matmul(dst, sel[:, hh, :], mT[:, 1, :], start=False, stop=True)
                last.then_inc(bs["st"], 1)

            def b_values(b, p, q):
                if q == 0:
                    pe.wait_ge(bs["vb"], b + 1)
                pe.wait_ge(bs["exp"], b * 4 + q + 1)
                for h in range(4):
                    pe.matmul(pb[1][32 * h:32 * h + 32, 0:T], Vb[:, p, 0, 4 * q + h, :],
                              Eb[:, q % 2, h // 2, (h % 2) * T:(h % 2 + 1) * T], start=True, stop=False)
                for h in range(4):
                    last = pe.matmul(pb[1][32 * h:32 * h + 32, P:T], Vb[:, p, 1, 4 * q + h, :],
                                     Eb[:, q % 2, 2, h * P:(h + 1) * P], start=False, stop=True)
                last.then_inc(bs["pv"], 1)

            def b_natural(b, p, u):
                if u == 0:
                    pe.wait_ge(bs["ot"], b * 4 + 4)
                for q in range(4):
                    last = pe.transpose(pb[1][:, q * P:(q + 1) * P], OTb[:, p, q, u * P:(u + 1) * P], ident)
                last.then_inc(bs["on"], 1)

            def b_round(b, p):
                n, nnn, c, l = there(b + 1), there(b + 3), there(b), there(b - 1)
                if n:
                    waits(pe, bs["mT"], b + 1)
                    b_tq(b + 1, 1 - p, 0)
                if l:
                    waits(pe, bs["x"], b - 1)
                    b_values(b - 1, 1 - p, 3)
                if c: b_scoresT(b, p, 0)
                if n: b_tk(b + 1, 1 - p, 0)
                if l: b_natural(b - 1, 1 - p, 0)
                if n:
                    pe.wait_ge(bs["kT"], b * 2 + 3)
                    b_tq(b + 1, 1 - p, 1)
                if c: b_scoresT(b, p, 1)
                if n: b_scores(b + 1, 1 - p, 0)
                if c:
                    waits(pe, bs["att"], b * 2 - 1)
                    b_values(b, p, 0)
                if n: b_tk(b + 1, 1 - p, 1)
                if l:
                    if c: pe.wait_ge(bs["ot"], b * 4 + 1)
                    else: pe.wait_ge(bs["att"], b * 2 - 1)
                    b_natural(b - 1, 1 - p, 1)
                if n: b_scores(b + 1, 1 - p, 1)
                if c: b_scoresT(b, p, 2)
                if nnn:
                    pe.wait_ge(bs["kT"], b * 2 + 4)
                    b_q(b + 3, 1 - p)
                if n: b_scores(b + 1, 1 - p, 2)
                if c:
                    if l: pe.wait_ge(bs["att"], b * 2)
                    else: pe.wait_ge(bs["ot"], b * 4 + 1)
                    b_values(b, p, 1)
                if l:
                    pe.wait_ge(bs["att"], b * 2)
                    if c: pe.wait_ge(bs["ot"], b * 4 + 2)
                    for u in range(2):
                        last = pe.transpose(pb[1][:, u * P:(u + 1) * P], att[:, u, :], ident)
                    last.then_inc(bs["at"], 1)
                if n: b_scores(b + 1, 1 - p, 3)
                if c: b_scoresT(b, p, 3)
                if nnn: b_kv(b + 3)
                if l: pe.wait_ge(bs["attT"], b)
                if c:
                    pe.wait_ge(bs["ot"], b * 4 + 2)
                    b_values(b, p, 2)
                    pe.wait_ge(bs["ot"], b * 4 + 3)
                if l:
                    for u in range(2):
                        last = pe.matmul(pb[1][:, u * D:(u + 1) * D], attT[:, u, :], wo[:, :], start=True, stop=True)
                    last.then_inc(bs["y"], 1)
                if n:
                    pe.wait_ge(bs["ms"], b + 2)
                    if nnn:
                        pe.wait_ge(bs["turnk"], b + 4)
                        pe.wait_ge(bs["v"], b + 4)
                    else:
                        pe.wait_ge(bs["kT"], b * 2 + 4)
                    for u in range(2):
                        last = pe.transpose(pb[0][:, 0:P].bitcast(BF16)[:, u * P:(u + 1) * P], ms[:, u, :], identb[:, :])
                    last.then_inc(bs["mt"], 1)

            transpose(2)
            pe.wait_ge(b_loaded, 80)
            pe.wait_ge(bs["const"], 13)
            pe.wait_ge(bs["zero"], 1)
            for b in range(2):
                b_q(b, b)
                b_kv(b)
                pe.wait_ge(bs["turnk"], b + 1)
                pe.wait_ge(bs["v"], b + 1)
            b_rounds(pe, b_round)
            transpose(3)
            ffn_logits(1)
            ffn_tiles(1)


def _constants():
    i = np.arange(P)
    cols = {}
    cols["ident"] = np.eye(P)
    cols["pick"] = np.concatenate([np.eye(P) * ((i // VA) % 2 == jj)[:, None] for jj in range(2)], 1)
    inv = 1.0 / 10000.0 ** (np.arange(0, DB, 2, dtype=np.float32) / DB)
    ang = np.outer(np.arange(T, dtype=np.float32), inv)
    cos, sin = np.repeat(np.cos(ang), 2, 1), np.repeat(np.sin(ang), 2, 1)
    sin[:, 0::2] *= -1
    page = np.arange(T)[:, None] // PAGE
    pages = np.arange(NPG)[None, :]
    zero = np.zeros((T, 8))
    qmask = np.concatenate([np.where(page < pages, MASKED, 0.0), zero], 1)
    kmask = np.concatenate([page == pages, zero], 1)
    for name, c in (("cos", cos), ("sin", sin), ("qmask", qmask), ("kmask", kmask)):
        cols[name] = np.concatenate([c[:P], c[P:]], 1)
    cols["order"] = np.tile(NE - np.arange(NE), (P, 1))
    cols["within"] = np.tile((np.arange(NE * NT) % NT > 0), (P, 1))
    cols["steps"] = np.tile(P * np.arange(NT), (P, 1))
    cols["slots"] = np.tile(np.arange(SLOTS), (P, 1))
    cols["ones"] = np.ones((P, P))
    cols["before"] = np.triu(np.ones((P, P)), 1)
    return cols


def _select():
    s = np.zeros((P, HB, P), np.float32)
    for h in range(HB):
        s[3 * h:3 * h + 3, h, :] = 1.0
    return s.reshape(P, HB * P)


CST, NCST = {}, 0
for _name, _c in _constants().items():
    CST[_name] = (NCST, NCST + _c.shape[1])
    NCST += _c.shape[1]


_INS = ["L0_attn_a_x", "L0_attn_a_Mq", "L0_attn_a_Mk", "L0_attn_a_Mv", "L0_attn_b_wq", "L0_attn_b_w_down",
        "L0_attn_b_wk_up", "L0_attn_b_wv_up", "L0_attn_b_wo", "L0_ffn_w_gate", "L0_ffn_b_gate", "L0_ffn_W1",
        "L0_ffn_b1", "L0_ffn_W2", "L0_ffn_b2"]


def kernel(**inputs):
    import concourse.bacc as _bacc
    from concourse.bass_utils import run_bass_kernel_spmd as _run

    nc = _bacc.Bacc("TRN2", target_bir_lowering=False, num_devices=1)
    arrays = {f"in_{n}": np.ascontiguousarray(inputs[n]) for n in _INS}
    arrays["in_constants"] = np.concatenate(list(_constants().values()), 1).astype(np.float32)
    arrays["in_select"] = _select()
    args = [nc.dram_tensor(n, a.shape, mybir.dt.from_np(a.dtype), kind="ExternalInput").ap()
            for n, a in arrays.items()]
    out = nc.dram_tensor("out_0", (B, T, D), F32, kind="ExternalOutput").ap()
    xs = nc.dram_tensor("slots_in", (SLOTS * P, D), F32).ap()
    ys = nc.dram_tensor("slots_out", (SLOTS * P, D), F32).ap()
    build(nc, *args, out, xs, ys)
    r = _run(nc, [arrays], core_ids=[0])
    return r.results[0]["out_0"]
```

```python
from contextlib import ExitStack

import numpy as np

import concourse.bass as bass
from concourse import mybir

ALU = mybir.AluOpType
ACT = mybir.ActivationFunctionType
AX = mybir.AxisListType
F32 = mybir.dt.float32
BF16 = mybir.dt.bfloat16
I32 = mybir.dt.int32
U32 = mybir.dt.uint32

P = 128
D = 128
B = 8
T = 256
NT = B * T // P
EPS = 1e-5

HA = 8
KA = 64
VA = D // HA
RT = T // HA
SCALE_A = 1.0 / 8.0

NE = 8
MLP = 512
MC = MLP // P
SLOTS = NT + NE - 1
REGION = NT * P
ROWS = NE * REGION + (SLOTS - NT) * P

HB = 16
DB = D // HB
LAT = 64
PAGE = 32
NPG = T // PAGE
SCALE_B = float(1.0 / np.sqrt(np.float32(DB)))
MASKED = -1e30


class Chain:

    def __init__(self, eng, sem):
        self.eng, self.sem, self.base, self.k = eng, sem, 0, 0

    def inc(self, ins):
        ins.then_inc(self.sem, 1)
        self.k += 1

    def wait(self):
        self.eng.wait_ge(self.sem, self.base + self.k)

    def link(self, ins):
        self.inc(ins)
        self.wait()

    def restart(self, base):
        self.base, self.k = base, 0


def build(nc, x_in, Mq_in, Mk_in, Mv_in, wq_in, wdown_in, wkup_in, wvup_in, wo_in,
          wg_in, bg_in, W1_in, b1_in, W2_in, b2_in, cst_in, sel_in, out, xs_dram):
    with ExitStack() as ctx:
        def sb(name, shape, dt=F32):
            return ctx.enter_context(nc.sbuf_tensor(name, shape, dt))

        def sem(name):
            return ctx.enter_context(nc.semaphore(name))

        x = sb("x", [P, NT, D])
        xnb = sb("xnb", [P, 2, 2, D])
        xnT = sb("xnT", [D, NT + 2, P])
        xnTb = sb("xnTb", [D, 2, 2, P])
        cst = sb("cst", [P, NCST])
        def const(name):
            a, b = CST[name]
            return cst[:, a:b]
        ident = const("ident")
        stat = sb("stat", [P, 2, 2, 6])
        mv = sb("mv", [P, 2, 2, 2])
        rstd = sb("rstd", [P, 2, 2])
        consts = sb("consts", [P, 2, 2])
        Mq = sb("Mq", [D, HA * KA])
        Mk = sb("Mk", [D, HA * KA])
        Mv = sb("Mv", [D, HA * VA])
        xb = sb("xb", [D, 2, T])
        QT = sb("QT", [P, 2, HA, P])
        KT = sb("KT", [P, 2, 2, 4, HA, RT])
        Va = sb("Va", [P, 2, 2, HA * VA])
        E = sb("E", [P, 4, 2, 2, T])
        nmax = sb("nmax", [P, 4, 4])
        den = sb("den", [P, 4, 4])
        rden = sb("rden", [P, 4, 4])
        vs = sb("vs", [P, 4, 2, 2, HA * VA])
        OT = sb("OT", [P, 2, 2, 4, RT])

        W1 = sb("W1", [D, NE, MLP])
        W2 = sb("W2", [P, NE, MC, D])
        b1 = sb("b1", [P, NE, MLP])
        b2 = sb("b2", [P, NE, D])
        wg = sb("wg", [D, NE])
        bg = sb("bg", [P, NE])
        zeros = sb("zeros", [P, D])
        lg = sb("lg", [P, 2, NE])
        lmax = sb("lmax", [P, 2])
        lsub = sb("lsub", [P, NT, NE])
        lexp = sb("lexp", [P, NT, NE])
        route_p = sb("route_p", [P, 2, NT])
        cand = sb("cand", [P, 2, NE])
        cmax = sb("cmax", [P, 2])
        onehot = sb("onehot", [P, 2, NE])
        pair = sb("pair", [P, NE])
        sofar = sb("sofar", [P, NE])
        above = sb("above", [P, NE, NT])
        tiles = sb("tiles", [P, 4, NE])
        place = sb("place", [P, 2, NE])
        mine = sb("mine", [P, 2, NE])
        pos_f = sb("pos_f", [P, 2])
        pos = sb("pos", [P, NT], U32)
        posb = sb("posb", [P, 2, 2], U32)
        past = sb("past", [P, SLOTS, NE])
        expert_f = sb("expert_f", [P, SLOTS])
        expert = sb("expert", [P, SLOTS], I32)
        skip = sb("skip", [P, NE])
        skipped = sb("skipped", [P, SLOTS, NE])
        row_f = sb("row_f", [P, SLOTS])
        row = sb("row", [P, SLOTS], I32)
        xg = sb("xg", [P, 2, D])
        xgT = sb("xgT", [D, 2, P])
        hb = sb("hb", [P, 2, MLP])
        hT = sb("hT", [P, 2, MC, P])
        yo = sb("yo", [P, 2, D])
        yg = sb("yg", [P, NT, D])

        sel = sb("sel", [P, HB, P], BF16)
        identb = sb("identb", [P, P], BF16)
        wq = sb("wq", [D, HB * DB])
        wdown = sb("wdown", [D, LAT])
        wkv = sb("wkv", [LAT, 2 * D])
        wo = sb("wo", [D, D])
        latT = sb("latT", [LAT, T])
        turn = sb("turn", [P, 2, 2, 2, D])
        rest = sb("rest", [P, 2, 2, D])
        rest2 = sb("rest2", [P, 2, 2, D])
        qs = sb("qs", [P, 2, 2, HB, 64], BF16)
        ks = sb("ks", [P, 2, 2, HB, 64], BF16)
        vst = sb("vst", [P, 2, 2, D])
        Vb = sb("Vb", [P, 2, 2, HB, 32])
        nm = sb("nm", [P, 2, HB])
        nmr = sb("nmr", [P, 2, HB])
        ms = sb("ms", [P, 2, P], BF16)
        mT = sb("mT", [P, 2, P], BF16)
        rsum = sb("rsum", [P, 2, HB])
        OTb = vs[:, :, :, :, :].rearrange("p s h c n -> p (s h c n)").rearrange(
            "p (a q t) -> p a q t", a=2, t=T)
        spare = OT[:, :, :, :, :].rearrange("p h j s i -> p (h j s i)").rearrange("p (k u c) -> p k u c", k=2, u=2)
        att, attT = spare[:, 0, :, :], spare[:, 1, :, :]
        qT = QT[:, :, :, :].rearrange("p a j t -> p (a j t)").bitcast(BF16).rearrange(
            "p (a n t) -> p a n t", a=2, t=T)
        kT = KT[:, :, :, :, :, :].rearrange("p a h s j i -> p (a h s j i)").bitcast(BF16).rearrange(
            "p (a n h t) -> p a n h t", a=2, h=2, t=T)
        Eb = E[:, :, :, :, :].rearrange("p s h c q -> p (s h c q)")[:, 0:2 * 3 * 512].rearrange(
            "p (a k c) -> p a k c", a=2, c=512)

        pb = [ctx.enter_context(nc.psum_tensor(f"bank{i}", [P, 512], F32)) for i in range(4)]
        S4 = ctx.enter_context(nc.psum_tensor("S4", [P, 4, 512], F32))
        S = [S4[:, 0:2, :], S4[:, 2:4, :]]

        loaded = sem("loaded")
        x_loaded = [sem(f"x_loaded{g}") for g in range(4)]
        stored = sem("stored")

        norm = []
        for n in range(4):
            norm.append({k: sem(f"n{n}_{k}") for k in
                         ("stats", "go", "mv", "vareps", "rstd", "xn", "xt", "xnT")})
        a_zero = sem("a_zero")
        a_xb = sem("a_xb")
        a_proj = sem("a_proj")
        a_evd = sem("a_evd")
        a_eva = sem("a_eva")
        a_scores = sem("a_scores")
        a_max = sem("a_max")
        a_exp = sem("a_exp")
        a_rden = sem("a_rden")
        a_vs = sem("a_vs")
        a_av = sem("a_av")
        a_ot = sem("a_ot")
        a_f = sem("a_f")
        a_x = sem("a_x")

        ffn = []
        for n in range(2):
            ffn.append({k: sem(f"f{n}_{k}") for k in
                        ("logits", "chain", "chain1", "chain2", "exp", "counts", "rank", "totals", "pos", "go",
                         "table", "scat0", "scat1",
                         "in0", "in1", "xt", "xgT", "h", "hb", "ht", "hT", "y", "yo",
                         "out0", "out1", "x")})
        gathered = [sem(f"gathered{c}") for c in range(B)]
        bs = {k: sem(f"b_{k}") for k in
              ("const", "chain0", "zero", "xb", "p1", "latT", "turnq", "p2", "turnk", "v", "vb", "chain", "split", "rep", "tq", "qT", "tk",
               "kT", "kTa", "s", "max", "mchain", "ms", "mt", "mT", "st", "exp", "pv", "ot", "on", "rsum", "att",
               "at", "attT", "y", "x")}
        b_loaded = sem("b_loaded")
        sel_loaded = sem("sel_loaded")
        w_loaded = sem("w_loaded")
        pool_const = sem("pool_const")
        copied = sem("copied")
        slots_zero = sem("slots_zero")

        block = ctx.enter_context(nc.Block())

        copies = [(sel[:, 4 * k:4 * k + 4, :], yg[:, 4 * k:4 * k + 4, :]) for k in range(4)]
        for t, name in ((qs, "qmask"), (ks, "kmask")):
            for u in range(2):
                mask = const(name)[:, 16 * u:16 * u + 16].unsqueeze(1).unsqueeze(1).to_broadcast([P, 2, HB, 16])
                copies.append((t[:, :, u, :, 48:64], mask))
        copies.append((identb[:, :], ident))

        def own(n, c):
            return n == 3 or (n == 1 and isinstance(c, int) and c >= B - 2)

        def normed(n, c, p):
            if own(n, c):
                return yg[:, 2 * c:2 * c + 2, :]
            return xnb[:, p, :, :]

        def waits(eng, s, value):
            if not isinstance(value, int) or value > 0:
                eng.wait_ge(s, value)

        def live(tile):
            return not isinstance(tile, int) or 0 <= tile < SLOTS

        def there(b):
            return not isinstance(b, int) or 0 <= b < B

        def b_rounds(eng, round_):
            for b in (-1, 0):
                round_(b, b % 2)
            with eng.Fori(0, 2) as h:
                round_(h * 2 + 1, 1)
                round_(h * 2 + 2, 0)
            for b in range(5, B + 1):
                round_(b, b % 2)

        def router_at(b, point):
            return {(5, 0): 1, (6, 0): 2, (7, 0): 3, (7, 1): 4, (7, 2): 5, (7, 3): 6, (8, 0): 7}.get(
                (b, point) if isinstance(b, int) else None)

        def b_parts(eng, chain, p, k):
            def part(i, k):
                m = ((0, 2, 5), (0, 1, 4))[i][k]
                return (qs, ks)[i][:, p, :, :, 8 * m:8 * m + 8].rearrange("p u h d -> p (u h) d")

            def view(t, i):
                return t[:, i, :, :].rearrange("p u (h d) -> p (u h) d", d=DB)

            if k == 0:
                flat = [turn[:, j, :, :, :].rearrange("p i u c -> p (i u c)") for j in range(2)]
                chain.inc(eng.tensor_tensor(rest[:, :, :, :].rearrange("p i u c -> p (i u c)"), flat[0], flat[1], ALU.add))
            for i in range(2):
                if k == 0:
                    chain.inc(eng.tensor_tensor(part(i, 0), view(turn[:, 0, :, :, :], i), view(turn[:, 1, :, :, :], i),
                                                ALU.add))
                elif k == 1:
                    chain.inc(eng.tensor_tensor(part(i, 1), view(rest, i), part(i, 0), ALU.subtract))
                    chain.inc(eng.tensor_tensor(view(rest2, i), view(rest, i), part(i, 0), ALU.subtract))
                else:
                    chain.inc(eng.tensor_tensor(part(i, 2), view(rest2, i), part(i, 1), ALU.subtract))
            chain.wait()

        def slot_steps(eng, step, last):
            held = None
            for s in range(-1, 3):
                held = step(s, s % 2, held)
            each = 6
            with eng.Fori(0, (SLOTS - 5) // each) as k:
                held = None
                for i in range(each):
                    held = step(k * each + (3 + i), (3 + i) % 2, held)
            held = None
            for s in range(SLOTS - 2, last + 1):
                held = step(s, s % 2, held)

        x_view = x_in.rearrange("b (u p) d -> p (b u) d", p=P)
        out_view = out.rearrange("b (u p) d -> p (b u) d", p=P)

        @block.sync
        def _(sp):
            for g in range(4):
                sp.dma_start(x[:, 4 * g:4 * g + 4, :], x_view[:, 4 * g:4 * g + 4, :]).then_inc(x_loaded[g], 16)
            sp.dma_start(cst[:, :], cst_in).then_inc(loaded, 16)
            sp.dma_start(Mq[:, :], Mq_in).then_inc(loaded, 16)
            sp.dma_start(Mk[:, :], Mk_in).then_inc(loaded, 16)
            sp.dma_start(Mv[:, :], Mv_in).then_inc(loaded, 16)
            sp.dma_start(yg[:, :, :], sel_in.rearrange("p (h k) -> p h k", h=HB)).then_inc(sel_loaded, 16)
            sp.dma_start(wq[:, :], wq_in).then_inc(b_loaded, 16)
            sp.dma_start(wdown[:, :], wdown_in).then_inc(b_loaded, 16)
            sp.dma_start(wkv[:, 0:D], wkup_in).then_inc(b_loaded, 16)
            sp.dma_start(wkv[:, D:2 * D], wvup_in).then_inc(b_loaded, 16)
            sp.dma_start(wo[:, :], wo_in).then_inc(b_loaded, 16)
            sp.dma_start(wg[:, :], wg_in).then_inc(w_loaded, 16)
            sp.dma_start(bg[:, :], bg_in.unsqueeze(0).to_broadcast([P, NE])).then_inc(w_loaded, 16)
            sp.dma_start(W1[:, :, :], W1_in.rearrange("e d m -> d e m")).then_inc(w_loaded, 16)
            sp.dma_start(W2[:, :, :, :], W2_in.rearrange("e (c p) d -> p e c d", p=P)).then_inc(w_loaded, 16)
            sp.dma_start(b1[:, :, :], b1_in.unsqueeze(0).to_broadcast([P, NE, MLP])).then_inc(w_loaded, 16)
            sp.dma_start(b2[:, :, :], b2_in.unsqueeze(0).to_broadcast([P, NE, D])).then_inc(w_loaded, 16)
            sp.wait_ge(pool_const, 1)
            sp.dma_start(xs_dram.rearrange("(s p) d -> p s d", p=P),
                         zeros[:, :].unsqueeze(1).to_broadcast([P, ROWS // P, D])).then_inc(slots_zero, 16)

            def ffn_loads(n):
                f = ffn[n]
                sp.wait_ge(f["scat0"], 16 * NT // 2)
                sp.wait_ge(f["scat1"], 16 * NT // 2)
                sp.wait_ge(f["table"], 1)

                def load(s, par):
                    at = sp.value_load(row[0:1, bass.ds(s, 1)], min_val=0, max_val=ROWS - P)
                    waits(sp, f["xt"], s - 1)
                    sp.dma_start(xg[:, par, :], xs_dram[bass.ds(at, P), :]).then_inc(f[f"in{par}"], 16)

                load(0, 0)
                load(1, 1)
                with sp.Fori(1, SLOTS // 2) as k:
                    load(k * 2, 0)
                    load(k * 2 + 1, 1)
                load(SLOTS - 1, 0)

            ffn_loads(0)
            ffn_loads(1)
            for c in range(B):
                sp.wait_ge(ffn[1]["x"], 2 * c + 2)
                sp.dma_start(out_view[:, 2 * c:2 * c + 2, :], x[:, 2 * c:2 * c + 2, :]).then_inc(stored, 16)
            sp.wait_ge(stored, 16 * B)

        def evacuate_a(eng, p, i, bank):
            copy = eng.tensor_copy if eng.engine == mybir.EngineType.DVE else eng.copy
            j0 = 4 * bank
            if i == 0:
                src = pb[bank][:, :].rearrange("p (j t) -> p j t", j=4)
                if eng.engine == mybir.EngineType.DVE:
                    return eng.tensor_scalar(QT[:, p, j0:j0 + 4, :], src, SCALE_A, None, ALU.mult)
                return eng.mul(QT[:, p, j0:j0 + 4, :], src, SCALE_A)
            if i == 1:
                for jj in range(2):
                    for h in range(2):
                        src = pb[bank][64 * jj:64 * jj + 64, :].rearrange("p (m h t) -> p m h t", m=2, h=2)
                        dst = KT[64 * h:64 * h + 64, p, h, :, j0 + jj:j0 + 4:2, :].rearrange("p s m i -> p m s i")
                        last = copy(dst, src[:, :, h, :].rearrange("p m (s i) -> p m s i", s=4))
                return last
            src = pb[bank][:, 0:HA * 32].rearrange("p (j c d) -> p j c d", j=HA, c=2)
            last = copy(Va[:, p, :, :].rearrange("p c (j d) -> p j c d", d=VA), src)
            return last

        @block.vector
        def _(dve):
            def norm_stats(n, c, p):
                s = norm[n]
                for u in range(2):
                    dve.bn_stats(stat[:, p, u, :], x[:, bass.ds(c * 2 + u, 1), :].squeeze(1)).then_inc(s["stats"], 1)
                dve.wait_ge(s["stats"], c * 2 + 2)
                dve.sem_inc(s["go"], 1)
                for u in range(2):
                    last = dve.bn_aggr(mv[:, p, u, :], stat[:, p, u, :])
                last.then_inc(s["mv"], 1)

            def norm_apply(n, c, p):
                s = norm[n]
                dve.wait_ge(s["rstd"], c + 1)
                if own(n, c):
                    if n == 1:
                        dve.wait_ge(copied, len(copies))
                elif isinstance(c, int) and c < 2:
                    if n > 0:
                        dve.wait_ge(norm[n - 1]["xt"], B)
                        if n == 2:
                            dve.wait_ge(ffn[0][f"scat{p}"], 16 * (NT // 2 - 2))
                else:
                    dve.wait_ge(s["xt"], c - 1)
                    if n % 2:
                        dve.wait_ge(ffn[n // 2][f"scat{p}"], (c - p) * 16)
                for u in range(2):
                    last = dve.tensor_scalar(normed(n, c, p)[:, u, :], x[:, bass.ds(c * 2 + u, 1), :].squeeze(1),
                                             mv[:, p, u, 0:1], rstd[:, p, u:u + 1], ALU.subtract, ALU.mult)
                last.then_inc(s["xn"], 1)

            def route_logits(n, c, p, bank):
                f = ffn[n]
                chain = Chain(dve, f["chain1"])
                chain.restart(c * 7)
                dve.wait_ge(f["logits"], c + 1)
                chain.link(dve.tensor_tensor(lg[:, :, :], bank[:, 0:2 * NE].rearrange("p (t e) -> p t e", e=NE),
                                             bg[:, :].unsqueeze(1).to_broadcast([P, 2, NE]), ALU.add))
                chain.link(dve.tensor_reduce(lmax[:, :], lg[:, :, :], AX.X, ALU.max))
                lmb = lmax[:, :].unsqueeze(2).to_broadcast([P, 2, NE])
                chain.inc(dve.tensor_tensor(lsub[:, bass.ds(c * 2, 2), :], lg[:, :, :], lmb, ALU.subtract))
                chain.link(dve.tensor_tensor(cand[:, :, :], lg[:, :, :], lmb, ALU.is_equal))
                chain.link(dve.tensor_tensor(cand[:, :, :], cand[:, :, :],
                                             const("order").unsqueeze(1).to_broadcast([P, 2, NE]), ALU.mult))
                chain.link(dve.tensor_reduce(cmax[:, :], cand[:, :, :], AX.X, ALU.max))
                chain.link(dve.tensor_tensor(onehot[:, :, :], cand[:, :, :],
                                             cmax[:, :].unsqueeze(2).to_broadcast([P, 2, NE]), ALU.is_equal))
                assert chain.k == 7
                dve.tensor_tensor(pair[:, :], onehot[:, 0, :], onehot[:, 1, :], ALU.add).then_inc(f["counts"], 1)

            def route_places(n, c, p, bank):
                f = ffn[n]
                chain = Chain(dve, f["chain2"])
                chain.restart(c * 5)
                dve.wait_ge(f["rank"], c + 1)
                chain.link(dve.tensor_tensor(place[:, 0, :], bank[:, 2 * NE:3 * NE], const("region"), ALU.add))
                chain.link(dve.tensor_tensor(place[:, 1, :], place[:, 0, :], onehot[:, 0, :], ALU.add))
                chain.link(dve.tensor_tensor(mine[:, :, :], place[:, :, :], onehot[:, :, :], ALU.mult))
                chain.link(dve.tensor_reduce(pos_f[:, :], mine[:, :, :], AX.X, ALU.add))
                last = dve.tensor_copy(pos[:, bass.ds(c * 2, 2)], pos_f[:, :])
                if not own(2 * n + 1, c):
                    last = dve.tensor_copy(posb[:, p, :], pos_f[:, :])
                last.then_inc(f["pos"], 1)
                chain.link(dve.tensor_tensor(sofar[:, :], sofar[:, :], pair[:, :], ALU.add))
                assert chain.k == 5

            def router_first(n, h):
                if there(h - 2): route_logits(n, h - 2, h % 2, pb[3])

            def router_second(n, h):
                if there(h - 2): route_places(n, h - 2, h % 2, pb[3])

            def a_norm(c):
                if there(c): norm_apply(0, c, c % 2)
                if there(c + 1):
                    dve.wait_ge(x_loaded[(c + 1) // 2], 16)
                    norm_stats(0, c + 1, (c + 1) % 2)

            dve.memset(KT[:, 0, :, :, :, :], 0.0).then_inc(a_zero, 1)
            dve.wait_ge(pool_const, 3)
            a_norm(-1)
            dve.wait_ge(x_loaded[0], 16)
            norm_stats(0, 1, 1)
            norm_apply(0, 0, 0)
            dve.wait_ge(x_loaded[1], 16)
            norm_stats(0, 2, 0)
            norm_apply(0, 1, 1)

            def a_evacuate(b, p, i):
                dve.wait_ge(a_proj, b * 5 + 2 * i + 1)
                evacuate_a(dve, p, i, 0).then_inc(a_evd, 1)

            def a_step(b, hp, p, lag, nxt):
                g = b * 4 + hp
                dve.wait_ge(a_scores, g + 1)
                dve.tensor_reduce(nmax[:, hp, :], S4[:, 2 * (hp % 2):2 * (hp % 2) + 2, :]
                                  .rearrange("p h (c q) -> p h c q", c=2), AX.X, ALU.max,
                                  negate=True).then_inc(a_max, 1)
                if nxt and hp < 3:
                    a_evacuate(b + 1, 1 - p, hp)
                if hp or lag:
                    a_recip(b * 4 + hp - 1, (hp + 3) % 4)
                if hp == 2 and lag:
                    a_add(b - 1)
                if hp >= 2 or lag:
                    a_outT(g - 2, (hp + 2) % 4)
                if isinstance(b, int) and 4 * b + hp + 2 < B:
                    if 4 * b + hp + 3 < B:
                        dve.wait_ge(x_loaded[(4 * b + hp + 3) // 2], 16)
                        norm_stats(0, 4 * b + hp + 3, (hp + 3) % 2)
                    norm_apply(0, 4 * b + hp + 2, hp % 2)
                if hp == 0 and there(b - 3):
                    route_logits(0, b - 3, 1 - p, pb[3])
                if hp == 1:
                    if there(b - 3): route_places(0, b - 3, 1 - p, pb[3])
                if hp == 2:
                    if there(b - 1): dve.wait_ge(a_x, b)
                    if there(b - 2): norm_apply(1, b - 2, p)
                    if there(b - 1):
                        norm_stats(1, b - 1, 1 - p)

            def a_recip(g, q):
                dve.wait_ge(a_exp, g + 1)
                dve.reciprocal(rden[:, q, :], den[:, q, :]).then_inc(a_rden, 1)

            def a_outT(g, q):
                dve.wait_ge(a_av, g + 1)
                dve.tensor_copy(OT[:, :, :, q, :], pb[2][:, 0:128].rearrange("p (h j i) -> p h j i", h=2, j=2)
                                ).then_inc(a_ot, 1)

            def a_add(b, bank=pb[3]):
                dve.wait_ge(a_f, b + 1)
                xs = x[:, bass.ds(b * 2, 2), :]
                dve.tensor_tensor(xs, xs, bank[:, 0:256].rearrange("p (h c) -> p h c", h=2), ALU.add
                                  ).then_inc(a_x, 1)

            dve.wait_ge(a_zero, 2)
            for i in range(3):
                a_evacuate(0, 0, i)
            for b in range(3):
                for hp in range(4):
                    a_step(b, hp, b % 2, b > 0, True)
            dve.wait_ge(w_loaded, 96)
            with dve.Fori(0, 2) as h:
                for hp in range(4):
                    a_step(h * 2 + 3, hp, 1, True, True)
                for hp in range(4):
                    a_step(h * 2 + 4, hp, 0, True, True)
            for hp in range(4):
                a_step(7, hp, 1, True, False)
            a_recip(31, 3)
            norm_apply(1, 6, 0)
            a_outT(30, 2)
            route_logits(0, 5, 1, pb[3])
            a_outT(31, 3)
            route_places(0, 5, 1, pb[3])
            a_add(7, pb[0])
            dve.wait_ge(a_x, 8)
            norm_stats(1, 7, 1)
            route_logits(0, 6, 0, pb[3])
            norm_apply(1, 7, 1)
            route_places(0, 6, 0, pb[3])
            route_logits(0, 7, 1, pb[3])
            route_places(0, 7, 1, pb[3])

            def ffn_table(n):
                f = ffn[n]
                chain = Chain(dve, f["chain"])
                link = chain.link
                dve.wait_ge(f["totals"], 1)
                link(dve.tensor_tensor(above[:, :, :], pb[3][:, 3 * NE:4 * NE].unsqueeze(2).to_broadcast([P, NE, NT]),
                                       const("steps").unsqueeze(1).to_broadcast([P, NE, NT]), ALU.is_gt))
                link(dve.tensor_reduce(tiles[:, 0, :], above[:, :, :], AX.X, ALU.add))
                link(dve.tensor_tensor_scan(tiles[:, 1, :], const("ones")[:, 0:NE], tiles[:, 0, :], 0.0,
                                            ALU.mult, ALU.add))
                chain.inc(dve.tensor_tensor(past[:, :, :],
                                            const("slots").unsqueeze(2).to_broadcast([P, SLOTS, NE]),
                                            tiles[:, 1, :].unsqueeze(1).to_broadcast([P, SLOTS, NE]), ALU.is_ge))
                link(dve.tensor_scalar(skip[:, :], tiles[:, 0, :], -float(P), float(REGION), ALU.mult, ALU.add))
                chain.inc(dve.tensor_reduce(expert_f[:, :], past[:, :, :], AX.X, ALU.add))
                link(dve.tensor_tensor(skipped[:, :, 0:NE - 1], past[:, :, 0:NE - 1],
                                       skip[:, 0:NE - 1].unsqueeze(1).to_broadcast([P, SLOTS, NE - 1]), ALU.mult))
                chain.inc(dve.tensor_scalar(expert[:, :], expert_f[:, :], float(NE - 1), None, ALU.min))
                link(dve.tensor_reduce(row_f[:, :], skipped[:, :, 0:NE - 1], AX.X, ALU.add))
                dve.scalar_tensor_tensor(out=row[:, :], in0=const("slots"), scalar=float(P), in1=row_f[:, :],
                                         op0=ALU.mult, op1=ALU.add).then_inc(f["table"], 1)

            def ffn_weights(n):
                f = ffn[n]
                chain = Chain(dve, f["chain"])
                chain.restart(9)
                dve.wait_ge(f["exp"], 2)
                chain.link(dve.tensor_reduce(route_p[:, 1, :], lexp[:, :, :], AX.X, ALU.add))
                chain.link(dve.reciprocal(route_p[:, 0, :], route_p[:, 1, :]))

            def ffn_tiles(n):
                f = ffn[n]
                dve.wait_ge(f["table"], 1)

                def step(s, par, held):
                    if live(s):
                        e = dve.value_load(expert[0:1, bass.ds(s, 1)], min_val=0, max_val=NE - 1)
                    if live(s + 1):
                        dve.wait_ge(f["xt"], s + 2)
                        waits(dve, f["h"], s)
                        dve.tensor_copy(xgT[:, 1 - par, :], pb[0][:, 0:P]).then_inc(f["xgT"], 1)
                    if live(s):
                        dve.wait_ge(f["h"], s + 1)
                        waits(dve, f["ht"], s - 1)
                        dve.tensor_tensor(hb[:, par, :], S4[:, par, :], b1[:, bass.ds(e, 1), :].squeeze(1), ALU.add
                                          ).then_inc(f["hb"], 1)
                    if live(s - 2):
                        e2 = dve.value_load(expert[0:1, bass.ds(s - 2, 1)], min_val=0, max_val=NE - 1)
                        dve.wait_ge(f["y"], s - 1)
                        if isinstance(s, int):
                            waits(dve, f[f"out{par}"], 16 * ((s - 2) // 2))
                        else:
                            dve.wait_ge(f[f"out{par}"], (s - 2 - par) * 8)
                        dve.tensor_tensor(yo[:, par, :], pb[1 + par][:, 0:D], b2[:, bass.ds(e2, 1), :].squeeze(1),
                                          ALU.add).then_inc(f["yo"], 1)

                slot_steps(dve, step, SLOTS + 1)

            def ffn_add(n, c):
                f = ffn[n]
                dve.wait_ge(gathered[c], 32 * n + 32)
                for t in (2 * c, 2 * c + 1):
                    dve.scalar_tensor_tensor(out=x[:, t, :], in0=yg[:, t, :], scalar=route_p[:, 0, t:t + 1],
                                             in1=x[:, t, :], op0=ALU.mult, op1=ALU.add).then_inc(f["x"], 1)

            dve.wait_ge(ffn[0]["chain1"], 7 * B)
            dve.sem_inc(ffn[0]["exp"], 1)
            ffn_table(0)
            ffn_weights(0)
            ffn_tiles(0)

            def b_turn(b, i, src, done):
                dve.wait_ge(bs["latT"] if i == 0 else bs["v"], b + 1)
                cos = const("cos").rearrange("p (u d) -> p u d", u=2)
                sin = const("sin").rearrange("p (u r) -> p u r", u=2)
                for u in range(2):
                    v = src(u).rearrange("p (h d) -> p h d", d=DB)
                    o = [turn[:, k, i, u, :].rearrange("p (h d) -> p h d", d=DB) for k in range(2)]
                    c = cos[:, u, :].unsqueeze(1).to_broadcast([P, HB, DB])
                    sn = sin[:, u, 0:DB].unsqueeze(1).to_broadcast([P, HB, DB])
                    dve.tensor_tensor(o[0], v, c, ALU.mult)
                    dve.tensor_tensor(o[1][:, :, 0:DB:2], v[:, :, 1:DB:2], sn[:, :, 0:DB:2], ALU.mult)
                    last = dve.tensor_tensor(o[1][:, :, 1:DB:2], v[:, :, 0:DB:2], sn[:, :, 1:DB:2], ALU.mult)
                last.then_inc(done, 1)

            def b_kT(b, p, i):
                dve.wait_ge(bs["tk"], b * 2 + i + 1)
                src = pb[0][0:64, :].bitcast(BF16).rearrange("p (n t) -> p n t", n=4)
                dve.tensor_copy(kT[0:64, p, 4 * i:4 * i + 4, 0, :], src).then_inc(bs["kT"], 1)

            def b_repeat(b, p):
                dve.wait_ge(bs["split"], b + 1)
                waits(dve, bs["tk"], b * 2 - 2)
                for t, hi, mid in ((qs, (0, 1), (2, 3)), (ks, (0, 2), (1, 3))):
                    v = t[:, p, :, :, :].rearrange("p u h c -> p (u h) c")
                    dst = v[:, :, 8 * hi[1]:8 * hi[1] + 32].rearrange("p n (m d) -> p n m d", d=8)[:, :, 0:4:3, :]
                    dve.tensor_copy(dst, v[:, :, 0:8].unsqueeze(2).to_broadcast([P, 2 * HB, 2, 8]))
                    last = dve.tensor_copy(v[:, :, 8 * mid[1]:8 * mid[1] + 8], v[:, :, 8 * mid[0]:8 * mid[0] + 8])
                last.then_inc(bs["rep"], 1)

            def b_max(b, q):
                if q == 0:
                    waits(dve, bs["ms"], b)
                for d in range(2):
                    h0 = 4 * q + 2 * d
                    dve.wait_ge(bs["s"], (b * 4 + q) * 3 + d + 1)
                    dve.tensor_reduce(nm[:, 1, h0:h0 + 2], pb[2 + d][:, :].rearrange("p (h k) -> p h k", h=2),
                                      AX.X, ALU.max, negate=True).then_inc(bs["max"], 1)
                dve.wait_ge(bs["s"], (b * 4 + q) * 3 + 3)
                dve.tensor_reduce(nm[:, 0, 4 * q:4 * q + 4], S4[:, 3, :].rearrange("p (h k) -> p h k", h=4),
                                  AX.X, ALU.max, negate=True).then_inc(bs["max"], 1)

            def b_normal(b, u):
                dve.wait_ge(bs["on"], b * 2 + u + 1)
                o = pb[1][:, :].rearrange("p (h r) -> p h r", r=32)
                dve.reciprocal(rsum[:, u, :], o[:, :, DB]).then_inc(bs["rsum"], 1)
                dve.wait_ge(bs["rsum"], b * 2 + u + 1)
                waits(dve, bs["at"], b)
                dve.tensor_tensor(att[:, u, :].rearrange("p (h d) -> p h d", d=DB), o[:, :, 0:DB],
                                  rsum[:, u, :].unsqueeze(2).to_broadcast([P, HB, DB]), ALU.mult
                                  ).then_inc(bs["att"], 1)

            def b_turn_q(b):
                dve.wait_ge(bs["p1"], b + 1)
                if not isinstance(b, int) or b > 1:
                    dve.wait_ge(bs["split"], b)
                b_turn(b, 0, lambda u: pb[0][:, u * D:(u + 1) * D], bs["turnq"])

            def b_turn_k(b):
                dve.wait_ge(bs["p2"], b + 1)
                b_turn(b, 1, lambda u: pb[0][:, 2 * u * D:(2 * u + 1) * D], bs["turnk"])

            def b_round(b, p):
                n, nn, nnn, l = there(b + 1), there(b + 2), there(b + 3), there(b - 1)
                if isinstance(b, int) and b == 5:
                    dve.wait_ge(bs["x"], 4)
                    for c in range(2):
                        norm_stats(3, c, c)
                b_router(b, 0, (6, 7), router_first)
                if isinstance(b, int) and b == 7:
                    dve.wait_ge(bs["x"], 6)
                    norm_stats(3, 4, 0)
                    b_router(b, 0, (7,), router_second)
                if n: b_kT(b + 1, 1 - p, 0)
                if isinstance(b, int) and b == 5:
                    norm_apply(3, 0, 0)
                if isinstance(b, int) and b in (5, 6):
                    norm_stats(3, b - 3, (b - 3) % 2)
                if l: b_normal(b - 1, 0)
                if isinstance(b, int) and b == 7:
                    norm_apply(3, 4, 0)
                b_router(b, 0, (5, 6), router_second)
                b_router(b, 1, (7,), router_first)
                if n: b_max(b + 1, 0)
                if n: b_max(b + 1, 1)
                if n: b_kT(b + 1, 1 - p, 1)
                if isinstance(b, int) and b == 7:
                    norm_stats(3, 5, 1)
                if l: b_normal(b - 1, 1)
                if isinstance(b, int) and b == 7:
                    norm_apply(3, 5, 1)
                b_router(b, 1, (7,), router_second)
                if isinstance(b, int) and b == 8:
                    norm_apply(3, 6, 0)
                b_router(b, 2, (7,), router_first)
                if n: b_max(b + 1, 2)
                if nn: b_repeat(b + 2, p)
                if nnn: b_turn_q(b + 3)
                if l:
                    dve.wait_ge(bs["at"], b)
                    dve.tensor_copy(attT[:, :, :], pb[1][:, 0:T].rearrange("p (u t) -> p u t", u=2)
                                    ).then_inc(bs["attT"], 1)
                b_router(b, 0, (8,), router_first)
                b_router(b, 2, (7,), router_second)
                b_router(b, 3, (7,), router_first)
                if n: b_max(b + 1, 3)
                if nnn: b_turn_k(b + 3)
                if l:
                    dve.wait_ge(bs["y"], b)
                    xs = x[:, bass.ds((b - 1) * 2, 2), :]
                    dve.tensor_tensor(xs, xs, pb[1][:, 0:T].rearrange("p (u c) -> p u c", u=2), ALU.add
                                      ).then_inc(bs["x"], 1)
                if isinstance(b, int) and b >= 7:
                    dve.wait_ge(bs["x"], b)
                    norm_stats(3, b - 1, (b - 1) % 2)
                b_router(b, 3, (7,), router_second)
                b_router(b, 0, (8,), router_second)
                if isinstance(b, int) and b in (5, 6):
                    for c in ((1, 2) if b == 5 else (3,)):
                        norm_apply(3, c, c % 2)

            def b_router(b, point, rounds, what):
                if isinstance(b, int) and b in rounds:
                    what(1, router_at(b, point))

            chain0 = Chain(dve, bs["chain0"])
            for c in range(B + 1):
                if c < B:
                    ffn_add(0, c)
                    dve.wait_ge(ffn[0]["x"], 2 * c + 2)
                    norm_stats(2, c, c % 2)
                if c > 0:
                    norm_apply(2, c - 1, (c - 1) % 2)
                if c == 2: b_turn_q(0)
                if c == 3:
                    b_turn_k(0)
                    dve.wait_ge(bs["turnk"], 1)
                if c in (4, 5, 6): b_parts(dve, chain0, 0, c - 4)
                if c == 5: b_turn_q(1)
                if c == 6: b_turn_k(1)
            dve.sem_inc(bs["split"], 1)
            b_repeat(0, 0)
            b_rounds(dve, b_round)
            norm_apply(3, B - 1, 1)
            for h in range(B, B + 2):
                router_first(1, h)
                router_second(1, h)
            dve.wait_ge(ffn[1]["chain1"], 7 * B)
            dve.sem_inc(ffn[1]["exp"], 1)
            ffn_table(1)
            ffn_weights(1)
            ffn_tiles(1)
            for c in range(B):
                ffn_add(1, c)

        @block.scalar
        def _(act):
            def norm_out(n, c, p, bank):
                s = norm[n]
                act.wait_ge(s["xt"], c + 1)
                if n % 2:
                    dst = xnTb[:, p, :, :]
                elif c < 2:
                    dst = xb[:, c, :].rearrange("p (u t) -> p u t", u=2)
                else:
                    dst = xnT[:, 2 * c:2 * c + 2, :]
                act.copy(dst, bank[:, 0:T].rearrange("p (t c) -> p t c", t=2)).then_inc(s["xnT"], 1)

            norm_out(0, 0, 0, pb[2])
            norm_out(0, 1, 1, pb[3])

            def a_evacuate(b, p, i):
                act.wait_ge(a_proj, b * 5 + 2 * i + 2)
                evacuate_a(act, p, i, 1).then_inc(a_eva, 1)

            def a_step(b, hp, p, lag, nxt):
                g = b * 4 + hp
                act.wait_ge(a_max, g + 1)
                if lag:
                    act.wait_ge(a_av, g - 3)
                    act.wait_ge(a_rden, g - 3)
                for h in range(2):
                    for c in range(2):
                        k = 2 * h + c
                        last = act.activation(E[:, hp, h, c, :], S[hp % 2][:, h, c * T:(c + 1) * T], ACT.Exp,
                                              bias=nmax[:, hp, k:k + 1], accum_out=den[:, hp, k:k + 1])
                last.then_inc(a_exp, 1)
                if nxt and hp < 2:
                    a_evacuate(b + 1, 1 - p, hp)
                if hp == 3 and there(b - 2):
                    norm_out(1, b - 2, p, pb[3])
                if isinstance(b, int) and 4 * b + hp + 2 < B:
                    norm_out(0, 4 * b + hp + 2, hp % 2, pb[3])
                if isinstance(b, int) and 4 * b + hp < len(copies):
                    if 4 * b + hp == 0:
                        act.wait_ge(loaded, 64)
                        act.wait_ge(sel_loaded, 16)
                    act.copy(*copies[4 * b + hp]).then_inc(copied, 1)

            act.wait_ge(a_zero, 2)
            for i in range(2):
                a_evacuate(0, 0, i)
            for b in range(3):
                for hp in range(4):
                    a_step(b, hp, b % 2, b > 0, True)
            with act.Fori(0, 2) as h:
                for hp in range(4):
                    a_step(h * 2 + 3, hp, 1, True, True)
                for hp in range(4):
                    a_step(h * 2 + 4, hp, 0, True, True)
            for hp in range(4):
                a_step(7, hp, 1, True, False)

            def ffn_exp(n):
                f = ffn[n]
                act.wait_ge(f["exp"], 1)
                act.activation(lexp[:, :, :], lsub[:, :, :], ACT.Exp).then_inc(f["exp"], 1)

            def ffn_tiles(n):
                f = ffn[n]

                def step(s, par, held):
                    if live(s - 3):
                        at = act.value_load(row[0:1, bass.ds(s - 3, 1)], min_val=0, max_val=ROWS - P)
                    if live(s - 1):
                        act.wait_ge(f["ht"], s)
                        waits(act, f["y"], s - 2)
                        act.activation(hT[:, 1 - par, :, :], S4[:, 3 - par, :].rearrange("p (c t) -> p c t", c=MC),
                                       ACT.Relu).then_inc(f["hT"], 1)
                    if live(s - 3):
                        act.wait_ge(f["yo"], s - 2)
                        act.dma_start(xs_dram[bass.ds(at, P), :], yo[:, 1 - par, :]
                                      ).then_inc(f[f"out{1 - par}"], 16)

                slot_steps(act, step, SLOTS + 2)

            norm_out(1, 6, 0, pb[1])
            norm_out(1, 7, 1, pb[1])
            ffn_exp(0)
            ffn_tiles(0)

            def b_latent(b):
                act.wait_ge(bs["p1"], b + 1)
                waits(act, bs["p2"], b)
                act.copy(latT[:, :], pb[0][0:LAT, T:2 * T]).then_inc(bs["latT"], 1)

            def b_v(b, p):
                act.wait_ge(bs["p2"], b + 1)
                src = pb[0][:, :].rearrange("p (u i h d) -> p u i h d", u=2, i=2, d=DB)
                waits(act, bs["vb"], b - 1)
                act.copy(vst[:, p, :, :].rearrange("p u (h d) -> p u h d", d=DB), src[:, :, 1, :, :]).then_inc(bs["v"], 1)

            def b_qT(b, p, i):
                act.wait_ge(bs["tq"], b * 2 + i + 1)
                src = pb[0][:, :].bitcast(BF16).rearrange("p (n t) -> p n t", n=4)
                act.copy(qT[:, p, 4 * i:4 * i + 4, :], src).then_inc(bs["qT"], 1)

            def b_kT(b, p, i):
                act.wait_ge(bs["tk"], b * 2 + i + 1)
                src = pb[0][64:128, :].bitcast(BF16).rearrange("p (n t) -> p n t", n=4)
                act.copy(kT[64:128, p, 4 * i:4 * i + 4, 1, :], src).then_inc(bs["kTa"], 1)

            def b_exp(b, q):
                act.wait_ge(bs["st"], b * 4 + q + 1)
                waits(act, bs["pv"], b * 4 + q - 1)
                act.activation(Eb[:, q % 2, :, :], S4[:, 0:3, :], ACT.Exp, scale=SCALE_B).then_inc(bs["exp"], 1)

            def b_outT(b, p, q):
                act.wait_ge(bs["pv"], b * 4 + q + 1)
                act.copy(OTb[:, p, q, :], pb[1][:, 0:T]).then_inc(bs["ot"], 1)

            def b_round(b, p):
                n, nnn, c, l = there(b + 1), there(b + 3), there(b), there(b - 1)
                if n: b_qT(b + 1, 1 - p, 0)
                if router_at(b, 0) == 3: b_router(b, 0)
                if l: b_outT(b - 1, 1 - p, 3)
                if router_at(b, 0) in (2, 7): b_router(b, 0)
                if n: b_kT(b + 1, 1 - p, 0)
                if c: b_exp(b, 0)
                if router_at(b, 0) == 1: b_router(b, 0)
                b_router(b, 1)
                if n: b_qT(b + 1, 1 - p, 1)
                if c: b_exp(b, 1)
                if c: b_outT(b, p, 0)
                if n: b_kT(b + 1, 1 - p, 1)
                if c: b_exp(b, 2)
                b_router(b, 2)
                if nnn: b_latent(b + 3)
                if c: b_outT(b, p, 1)
                if nnn: b_v(b + 3, 1 - p)
                if c: b_outT(b, p, 2)
                if c: b_exp(b, 3)
                b_router(b, 3)
                if n:
                    act.wait_ge(bs["mt"], b + 2)
                    act.copy(mT[:, :, :], pb[2][:, 0:P].bitcast(BF16).rearrange("p (u t) -> p u t", u=2)
                             ).then_inc(bs["mT"], 1)

            def b_router(b, point):
                h = router_at(b, point)
                if h is not None:
                    norm_out(3, h - 1, (h - 1) % 2, pb[2])

            for c in range(B):
                norm_out(2, c, c % 2, pb[2 + c % 2])
                if c in (0, 2): b_latent(c // 2)
                if c in (1, 4): b_v(c // 3, c // 3)
            b_rounds(act, b_round)
            norm_out(3, B - 1, 1, pb[2])
            ffn_exp(1)
            ffn_tiles(1)

        @block.gpsimd
        def _(pool):
            pool.memset(zeros[:, :], 0.0).then_inc(pool_const, 1)
            pool.memset(consts[:, 0, :], EPS).then_inc(pool_const, 1)
            pool.memset(consts[:, 1, :], -0.5).then_inc(pool_const, 1)
            pool.memset(sofar[:, :], 0.0).then_inc(pool_const, 1)
            pool.memset(xnT[:, NT:NT + 2, :], 0.0).then_inc(pool_const, 1)
            pool.wait_ge(pool_const, 5)

            def inverse_deviation(n, c, p):
                s = norm[n]
                pool.wait_ge(s["mv"], c + 1)
                pool.tensor_tensor(rstd[:, p, :], mv[:, p, :, 1], consts[:, 0, :], ALU.add).then_inc(s["vareps"], 1)
                pool.wait_ge(s["vareps"], c + 1)
                pool.tensor_tensor(rstd[:, p, :], rstd[:, p, :], consts[:, 1, :], ALU.pow).then_inc(s["rstd"], 1)

            def scatter(n, c, p):
                f = ffn[n]
                pool.wait_ge(f["pos"], c + 1)
                pool.sem_inc(f["go"], 1)
                for u in range(2):
                    place = pos[:, 2 * c + u:2 * c + u + 1] if own(2 * n + 1, c) else posb[:, p, u:u + 1]
                    pool.indirect_dma_start(out=xs_dram, out_offset=bass.IndirectOffsetOnAxis(place, 0),
                                            in_=normed(2 * n + 1, c, p)[:, u, :], in_offset=None).then_inc(f[f"scat{p}"], 16)

            for c in range(3):
                inverse_deviation(0, c, c % 2)
                if c == 1:
                    pool.memset(KT[:, 1, :, :, :, :], 0.0).then_inc(a_zero, 1)
            pool.memset(Vb[:, :, :, :, :], 0.0).then_inc(bs["const"], 1)
            pool.memset(ms[:, :, :], 0.0).then_inc(bs["const"], 1)
            pool.wait_ge(bs["const"], 2)
            pool.memset(Vb[:, :, :, :, DB:DB + 1], 1.0).then_inc(bs["const"], 1)

            def a_stage(b, p):
                pool.tensor_tensor(xb[:, p, :].rearrange("p (u t) -> p u t", u=2), xnT[:, bass.ds(b * 2, 2), :],
                                   zeros[:, :].unsqueeze(1).to_broadcast([P, 2, P]), ALU.add).then_inc(a_xb, 1)

            def a_values(g, q, p, reuse):
                pool.wait_ge(a_rden, g + 1)
                if reuse:
                    pool.wait_ge(a_av, g - 3)
                v = Va[:, p, :, :].unsqueeze(1).to_broadcast([P, 2, 2, HA * VA])
                r = rden[:, q, :].rearrange("p (h c) -> p h c", h=2).unsqueeze(3).to_broadcast([P, 2, 2, HA * VA])
                pool.tensor_tensor(vs[:, q, :, :, :], v, r, ALU.mult).then_inc(a_vs, 1)

            def a_batch(b, p, lag, ahead):
                for hp in range(4):
                    if hp == 0:
                        pool.wait_ge(a_evd, b * 3 + 3)
                    if hp == (3 if isinstance(b, int) and b < 3 else 0) and ahead:
                        pool.wait_ge(a_proj, b * 5 + 5)
                        if isinstance(b, int):
                            pool.wait_ge(norm[0]["xnT"], b + 3)
                        a_stage(b + 2, p)
                    if isinstance(b, int) and 4 * b + hp + 3 < B:
                        inverse_deviation(0, 4 * b + hp + 3, (hp + 3) % 2)
                    a_values(b * 4 + hp, hp, p, lag)
                    if hp == 1 and there(b - 3):
                        scatter(0, b - 3, 1 - p)
                    if hp == 2 and there(b - 1):
                        inverse_deviation(1, b - 1, 1 - p)

            for b in range(3):
                a_batch(b, b % 2, b > 0, True)
            pool.wait_ge(slots_zero, 16)
            with pool.Fori(0, 2) as h:
                a_batch(h * 2 + 3, 1, True, True)
                a_batch(h * 2 + 4, 0, True, True)
            a_batch(7, 1, True, False)
            scatter(0, 5, 1)
            inverse_deviation(1, 7, 1)
            scatter(0, 6, 0)
            scatter(0, 7, 1)
            pool.wait_ge(a_scores, 4 * B)
            pool.memset(KT[:, :, :, :, :, :], 0.0).then_inc(bs["zero"], 1)
            pool.wait_ge(ffn[0]["totals"], 1)
            pool.memset(sofar[:, :], 0.0).then_inc(pool_const, 1)

            def gather(n, c):
                f = ffn[n]
                for t in (2 * c, 2 * c + 1):
                    pool.indirect_dma_start(out=yg[:, t, :], out_offset=None, in_=xs_dram,
                                            in_offset=bass.IndirectOffsetOnAxis(pos[:, t:t + 1], 0)
                                            ).then_inc(gathered[c], 16)

            def all_out(n):
                f = ffn[n]
                pool.wait_ge(f["out0"], 16 * ((SLOTS + 1) // 2))
                pool.wait_ge(f["out1"], 16 * (SLOTS // 2))

            all_out(0)
            for c in range(B + 1):
                if c < B:
                    gather(0, c)
                if c > 0:
                    inverse_deviation(2, c - 1, (c - 1) % 2)

            def b_stage(b, p):
                pool.tensor_tensor(xb[:, p, :].rearrange("p (u t) -> p u t", u=2), xnT[:, bass.ds(b * 2, 2), :],
                                   zeros[:, :].unsqueeze(1).to_broadcast([P, 2, P]), ALU.add).then_inc(bs["xb"], 1)

            def b_split(b, p):
                chain = Chain(pool, bs["chain"])
                chain.restart((b - 1) * 9)
                pool.wait_ge(bs["turnq"], b + 1)
                pool.wait_ge(bs["turnk"], b + 1)
                if isinstance(b, int) and b == 1:
                    pool.wait_ge(bs["split"], 1)
                waits(pool, bs["tk"], b * 2 - 2)
                for k in range(3):
                    b_parts(pool, chain, p, k)
                assert chain.k == 9
                pool.sem_inc(bs["split"], 1)

            def b_maxima(b):
                chain = Chain(pool, bs["mchain"])
                chain.restart(b * 4)
                pool.wait_ge(bs["max"], b * 12 + 12)
                waits(pool, bs["mt"], b)
                parts = ms[:, :, 0:3 * HB].rearrange("p u (h k) -> p u h k", k=3)
                chain.link(pool.tensor_tensor(
                    parts[:, :, :, 0], nm[:, :, :], zeros[:, 0:2 * HB].rearrange("p (u h) -> p u h", u=2), ALU.add))
                chain.inc(pool.tensor_tensor(nmr[:, :, :], nm[:, :, :], parts[:, :, :, 0], ALU.subtract))
                chain.link(pool.tensor_tensor(parts[:, :, :, 1], nm[:, :, :], parts[:, :, :, 0], ALU.subtract))
                chain.link(pool.tensor_tensor(parts[:, :, :, 2], nmr[:, :, :], parts[:, :, :, 1], ALU.subtract))
                pool.sem_inc(bs["ms"], 1)

            def b_place_v(b, p):
                pool.wait_ge(bs["v"], b + 1)
                waits(pool, bs["pv"], b * 4 - 4)
                z = zeros[:, :].rearrange("p (h d) -> p h d", d=DB)
                for u in range(2):
                    last = pool.tensor_tensor(Vb[:, p, u, :, 0:DB], vst[:, p, u, :].rearrange("p (h d) -> p h d", d=DB), z,
                                              ALU.add)
                last.then_inc(bs["vb"], 1)

            def b_round(b, p):
                if isinstance(b, int) and b == 5:
                    for c in range(2):
                        inverse_deviation(3, c, c)
                if there(b + 1):
                    b_place_v(b + 1, 1 - p)
                if there(b + 2):
                    b_split(b + 2, p)
                if isinstance(b, int) and b in (5, 6):
                    inverse_deviation(3, b - 3, (b - 3) % 2)
                if there(b + 4):
                    pool.wait_ge(bs["latT"], b + 3)
                    b_stage(b + 4, p)
                if there(b + 1):
                    b_maxima(b + 1)
                if isinstance(b, int) and b == 6:
                    scatter(1, 0, 0)
                if isinstance(b, int) and b == 7:
                    inverse_deviation(3, 4, 0)
                    scatter(1, 1, 1)
                    inverse_deviation(3, 5, 1)
                    for c in (2, 3):
                        scatter(1, c, c % 2)
                    inverse_deviation(3, 6, 0)
                    scatter(1, 4, 0)
                if isinstance(b, int) and b == 8:
                    inverse_deviation(3, 7, 1)
                    scatter(1, 5, 1)

            pool.wait_ge(norm[2]["xnT"], B)
            pool.wait_ge(bs["latT"], 1)
            b_stage(2, 0)
            b_rounds(pool, b_round)
            for c in (6, 7):
                scatter(1, c, c % 2)
            all_out(1)
            for c in range(B):
                gather(1, c)

        @block.tensor
        def _(pe):
            def norm_transpose(n, c, p, bank):
                s = norm[n]
                pe.wait_ge(s["xn"], c + 1)
                if n % 2 == 0 and not (n == 0 and c < 2):
                    waits(pe, s["xnT"], c - (0 if n == 0 else 1))
                for u in range(2):
                    last = pe.transpose(bank[:, u * P:(u + 1) * P], normed(n, c, p)[:, u, :], ident)
                last.then_inc(s["xt"], 1)

            def logits(n, c, p, bank):
                pe.wait_ge(norm[2 * n + 1]["xnT"], c + 1)
                for u in range(2):
                    last = pe.matmul(bank[:, u * NE:(u + 1) * NE], xnTb[:, p, u, :], wg[:, :], start=True, stop=True)
                last.then_inc(ffn[n]["logits"], 1)

            def ranks(n, c, bank):
                f = ffn[n]
                pe.wait_ge(f["counts"], c + 1)
                waits(pe, f["chain2"], c * 5)
                pe.matmul(bank[:, 2 * NE:3 * NE], const("ones"), sofar[:, :], start=True, stop=False)
                pe.matmul(bank[:, 2 * NE:3 * NE], const("before"), pair[:, :], start=False, stop=True
                          ).then_inc(f["rank"], 1)

            def totals(n):
                f = ffn[n]
                pe.wait_ge(f["chain2"], 5 * B)
                pe.matmul(pb[3][:, 3 * NE:4 * NE], const("ones"), sofar[:, :], start=True, stop=True
                          ).then_inc(f["totals"], 1)

            pe.wait_ge(loaded, 64)
            norm_transpose(0, 0, 0, pb[2])
            norm_transpose(0, 1, 1, pb[3])

            def a_project(b, p, i, free):
                if i == 0:
                    if isinstance(b, int) and b < 2:
                        pe.wait_ge(norm[0]["xnT"], b + 1)
                    else:
                        pe.wait_ge(a_xb, b - 1)
                for bank in range(2 if i < 2 else 1):
                    if free and bank == 0:
                        pe.wait_ge(a_evd, b * 3 + i)
                    if free and bank == 1:
                        pe.wait_ge(a_eva, b * 2 + i)
                    dst = pb[bank]
                    if i == 0:
                        for j in range(4):
                            for h in range(2):
                                jq = 4 * bank + j
                                last = pe.matmul(dst[64 * h:64 * h + 64, j * P:(j + 1) * P],
                                                 Mq[:, jq * KA:(jq + 1) * KA], xb[:, p, h * P:(h + 1) * P],
                                                 start=True, stop=True)
                    elif i == 1:
                        for m in range(2):
                            mq = 2 * bank + m
                            last = pe.matmul(dst[:, m * T:(m + 1) * T], Mk[:, mq * P:(mq + 1) * P],
                                             xb[:, p, :], start=True, stop=True)
                    else:
                        for j in range(HA):
                            for g in range(4):
                                last = pe.matmul(dst[32 * g:32 * g + 32, 32 * j:32 * j + 32],
                                                 xb[:, p, j * RT:(j + 1) * RT],
                                                 Mv[:, :].rearrange("p (c g d) -> p c g d", c=2, g=4)[:, :, g, :],
                                                 start=True, stop=True)
                    last.then_inc(a_proj, 1)

            def a_values_out(g, q):
                pe.wait_ge(a_vs, g + 1)
                for h in range(2):
                    for c in range(2):
                        for jp in range(4):
                            last = pe.matmul(pb[2][32 * jp:32 * jp + 32, 64 * h:64 * h + 64],
                                             vs[:, q, h, c, 32 * jp:32 * jp + 32],
                                             E[:, q, h, c, 64 * jp:64 * jp + 64], start=(c == 0), stop=(c == 1))
                last.then_inc(a_av, 1)

            def a_final(b, bank=pb[3]):
                pe.wait_ge(a_ot, b * 4 + 4)
                for h in range(2):
                    for jj in range(2):
                        last = pe.matmul(bank[:, h * P:(h + 1) * P], OT[:, h, jj, :, :],
                                         const("pick")[:, jj * P:(jj + 1) * P], start=(jj == 0), stop=(jj == 1))
                last.then_inc(a_f, 1)

            def a_step(b, hp, p, lag, nxt):
                g = b * 4 + hp
                if hp >= 2 or lag:
                    pe.wait_ge(a_exp, g - 1)
                if hp == 0:
                    pe.wait_ge(a_evd, b * 3 + 3)
                    pe.wait_ge(a_eva, b * 2 + 2)
                for h in range(2):
                    for c in range(2):
                        last = pe.matmul(S[hp % 2][:, h, c * T:(c + 1) * T],
                                         KT[:, p, h, hp, 4 * c:4 * c + 4, :],
                                         QT[:, p, :, hp * RT:(hp + 1) * RT], start=True, stop=True)
                last.then_inc(a_scores, 1)
                if hp == 0 and there(b - 3): logits(0, b - 3, 1 - p, pb[3])
                if hp == 1 and there(b - 3): ranks(0, b - 3, pb[3])
                if hp == 3 and there(b - 2):
                    pe.wait_ge(a_x, b)
                    norm_transpose(1, b - 2, p, pb[3])
                if nxt and hp < 3:
                    a_project(b + 1, 1 - p, hp, True)
                if hp == 2 and lag:
                    if there(b - 3):
                        pe.wait_ge(ffn[0]["pos"], b - 2)
                    if isinstance(b, int) and b == 1:
                        pe.wait_ge(norm[0]["xnT"], B)
                    a_final(b - 1)
                if hp >= 2 or lag:
                    if not (hp == 2 and not lag):
                        pe.wait_ge(a_ot, g - 2)
                    a_values_out(g - 2, (hp + 2) % 4)
                if isinstance(b, int) and 4 * b + hp + 2 < B:
                    norm_transpose(0, 4 * b + hp + 2, hp % 2, pb[3])

            pe.wait_ge(pool_const, 5)
            for i in range(3):
                a_project(0, 0, i, i > 0)
            for b in range(3):
                for hp in range(4):
                    a_step(b, hp, b % 2, b > 0, True)
            pe.wait_ge(w_loaded, 96)
            with pe.Fori(0, 2) as h:
                for hp in range(4):
                    a_step(h * 2 + 3, hp, 1, True, True)
                for hp in range(4):
                    a_step(h * 2 + 4, hp, 0, True, True)
            for hp in range(4):
                a_step(7, hp, 1, True, False)
            pe.wait_ge(a_ot, 30)
            a_values_out(30, 2)
            logits(0, 5, 1, pb[3])
            norm_transpose(1, 6, 0, pb[1])
            pe.wait_ge(a_ot, 31)
            a_values_out(31, 3)
            ranks(0, 5, pb[3])
            a_final(7, pb[0])
            pe.wait_ge(ffn[0]["pos"], 6)
            logits(0, 6, 0, pb[3])
            ranks(0, 6, pb[3])
            pe.wait_ge(norm[1]["xnT"], 7)
            norm_transpose(1, 7, 1, pb[1])
            pe.wait_ge(ffn[0]["pos"], 7)
            logits(0, 7, 1, pb[3])
            ranks(0, 7, pb[3])
            totals(0)

            def ffn_tiles(n):
                f = ffn[n]
                pe.wait_ge(f["table"], 1)

                def step(s, par, held):
                    e, before, e2 = None, *(held or (None, None))
                    if live(s - 2) and e2 is None:
                        e2 = pe.value_load(expert[0:1, bass.ds(s - 2, 1)], min_val=0, max_val=NE - 1)
                    if live(s):
                        e = pe.value_load(expert[0:1, bass.ds(s, 1)], min_val=0, max_val=NE - 1)
                    if live(s + 1):
                        if isinstance(s, int):
                            pe.wait_ge(f[f"in{1 - par}"], 16 * ((s + 1) // 2 + 1))
                        else:
                            pe.wait_ge(f[f"in{1 - par}"], (s + 1 - (1 - par)) * 8 + 16)
                        waits(pe, f["xgT"], s + 1)
                        pe.transpose(pb[0][:, 0:P], xg[:, 1 - par, :], ident).then_inc(f["xt"], 1)
                    if live(s):
                        pe.wait_ge(f["xgT"], s + 1)
                        waits(pe, f["hb"], s - 1)
                        pe.matmul(S4[:, par, :], xgT[:, par, :], W1[:, bass.ds(e, 1), :].squeeze(1), start=True, stop=True
                                  ).then_inc(f["h"], 1)
                    if live(s - 1):
                        pe.wait_ge(f["hb"], s)
                        waits(pe, f["hT"], s - 2)
                        for c in range(MC):
                            last = pe.transpose(S4[:, 3 - par, c * P:(c + 1) * P],
                                                hb[:, 1 - par, c * P:(c + 1) * P], ident)
                        last.then_inc(f["ht"], 1)
                    if live(s - 2):
                        pe.wait_ge(f["hT"], s - 1)
                        waits(pe, f["yo"], s - 3)
                        for c in range(MC):
                            last = pe.matmul(pb[1 + par][:, 0:D], hT[:, par, c, :],
                                             W2[:, bass.ds(e2, 1), c, :].squeeze(1), start=(c == 0), stop=(c == MC - 1))
                        last.then_inc(f["y"], 1)
                    return e, before

                slot_steps(pe, step, SLOTS + 1)

            ffn_tiles(0)

            def b_q(b, p):
                if isinstance(b, int) and b < 2:
                    pe.wait_ge(norm[2]["xnT"], b + 1)
                else:
                    pe.wait_ge(bs["xb"], b - 1)
                for u in range(2):
                    pe.matmul(pb[0][:, u * D:(u + 1) * D], xb[:, p, u * P:(u + 1) * P], wq[:, :], start=True, stop=True)
                pe.matmul(pb[0][0:LAT, T:2 * T], wdown[:, :], xb[:, p, :], start=True, stop=True).then_inc(bs["p1"], 1)

            def b_kv(b):
                pe.wait_ge(bs["latT"], b + 1)
                pe.wait_ge(bs["turnq"], b + 1)
                for u in range(2):
                    last = pe.matmul(pb[0][:, 2 * u * D:2 * (u + 1) * D], latT[:, u * P:(u + 1) * P], wkv[:, :],
                                     start=True, stop=True)
                last.then_inc(bs["p2"], 1)

            def b_transpose(src, p, i, done):
                dst = pb[0][:, :].bitcast(BF16)
                for n in range(4):
                    for u in range(2):
                        last = pe.transpose(dst[:, n * T + u * P:n * T + (u + 1) * P],
                                            src[:, p, u, 2 * (4 * i + n):2 * (4 * i + n) + 2, :]
                                            .rearrange("p h c -> p (h c)"), identb[:, :])
                last.then_inc(done, 1)

            def b_tq(b, p, i):
                if i == 0:
                    pe.wait_ge(bs["rep"], b + 1)
                b_transpose(qs, p, i, bs["tq"])

            def b_tk(b, p, i):
                pe.wait_ge(bs["qT"], b * 2 + i + 1)
                b_transpose(ks, p, i, bs["tk"])

            def b_scores(b, p, q):
                if q % 2 == 0:
                    pe.wait_ge(bs["qT"], b * 2 + 1 + q // 2)
                    kT_there(b, q // 2)
                before = (b * 4 + q) * 3 - 2
                for d in range(2):
                    n = 2 * q + d
                    waits(pe, bs["max"], before + d)
                    pe.matmul(pb[2 + d][:, :], qT[:, p, n, P:T], kT[:, p, n, :, :], start=True, stop=True
                              ).then_inc(bs["s"], 1)
                waits(pe, bs["max"], before + 2)
                for d in range(2):
                    n = 2 * q + d
                    last = pe.matmul(S4[:, 3, d * T:(d + 1) * T], qT[:, p, n, 0:P], kT[:, p, n, :, 0:P],
                                     start=True, stop=True)
                last.then_inc(bs["s"], 1)

            def kT_there(b, i):
                pe.wait_ge(bs["kT"], b * 2 + i + 1)
                pe.wait_ge(bs["kTa"], b * 2 + i + 1)

            def b_scoresT(b, p, q):
                if q == 0:
                    pe.wait_ge(bs["mT"], b + 1)
                waits(pe, bs["exp"], b * 4 + q)
                for d in range(2):
                    for h in range(2):
                        n, hh = 2 * q + d, 4 * q + 2 * d + h
                        dst = S4[:, d, h * T:(h + 1) * T]
                        pe.matmul(dst, kT[:, p, n, h, 0:P], qT[:, p, n, :], start=True, stop=False)
                        pe.matmul(dst, sel[:, hh, :], mT[:, :, :], start=False, stop=True)
                        dst = S4[:, 2, (2 * d + h) * P:(2 * d + h + 1) * P]
                        pe.matmul(dst, kT[:, p, n, h, P:T], qT[:, p, n, P:T], start=True, stop=False)
                        last = pe.matmul(dst, sel[:, hh, :], mT[:, 1, :], start=False, stop=True)
                last.then_inc(bs["st"], 1)

            def b_values(b, p, q):
                if q == 0:
                    pe.wait_ge(bs["vb"], b + 1)
                pe.wait_ge(bs["exp"], b * 4 + q + 1)
                for h in range(4):
                    pe.matmul(pb[1][32 * h:32 * h + 32, 0:T], Vb[:, p, 0, 4 * q + h, :],
                              Eb[:, q % 2, h // 2, (h % 2) * T:(h % 2 + 1) * T], start=True, stop=False)
                for h in range(4):
                    last = pe.matmul(pb[1][32 * h:32 * h + 32, P:T], Vb[:, p, 1, 4 * q + h, :],
                                     Eb[:, q % 2, 2, h * P:(h + 1) * P], start=False, stop=True)
                last.then_inc(bs["pv"], 1)

            def b_natural(b, p, u):
                if u == 0:
                    pe.wait_ge(bs["ot"], b * 4 + 4)
                for q in range(4):
                    last = pe.transpose(pb[1][:, q * P:(q + 1) * P], OTb[:, p, q, u * P:(u + 1) * P], ident)
                last.then_inc(bs["on"], 1)

            def b_round(b, p):
                n, nn, nnn, c, l = there(b + 1), there(b + 2), there(b + 3), there(b), there(b - 1)
                if n:
                    if nn:
                        pe.wait_ge(bs["turnk"], b + 3)
                        pe.wait_ge(bs["v"], b + 3)
                    else:
                        kT_there(b, 1)
                    b_tq(b + 1, 1 - p, 0)
                b_router(b, 0, (7,), router_first)
                if l:
                    waits(pe, bs["x"], b - 1)
                    b_values(b - 1, 1 - p, 3)
                b_router(b, 0, (6,), router_first)
                if n: b_tk(b + 1, 1 - p, 0)
                if c: b_scoresT(b, p, 0)
                b_router(b, 0, (7,), router_second)
                b_router(b, 0, (5,), router_first)
                if l: b_natural(b - 1, 1 - p, 0)
                b_router(b, 1, (7,), router_first)
                b_router(b, 0, (5, 6), router_second)
                if n and router_at(b, 0) is not None:
                    pe.wait_ge(norm[3]["xnT"], router_at(b, 0))
                    waits(pe, ffn[1]["pos"], router_at(b, 0) - 1)
                if n:
                    b_scores(b + 1, 1 - p, 0)
                    b_tq(b + 1, 1 - p, 1)
                if c: b_scoresT(b, p, 1)
                if n: b_scores(b + 1, 1 - p, 1)
                if c:
                    waits(pe, bs["att"], b * 2 - 1)
                    b_values(b, p, 0)
                if n: b_tk(b + 1, 1 - p, 1)
                if l:
                    if c: pe.wait_ge(bs["ot"], b * 4 + 1)
                    else: pe.wait_ge(bs["att"], b * 2 - 1)
                    b_natural(b - 1, 1 - p, 1)
                b_router(b, 1, (7,), router_second)
                if c: b_scoresT(b, p, 2)
                b_router(b, 2, (7,), router_first)
                if n: b_scores(b + 1, 1 - p, 2)
                if nnn: b_q(b + 3, 1 - p)
                if c:
                    if l: pe.wait_ge(bs["att"], b * 2)
                    else: pe.wait_ge(bs["ot"], b * 4 + 1)
                    b_values(b, p, 1)
                if l:
                    pe.wait_ge(bs["att"], b * 2)
                    if c: pe.wait_ge(bs["ot"], b * 4 + 2)
                    for u in range(2):
                        last = pe.transpose(pb[1][:, u * P:(u + 1) * P], att[:, u, :], ident)
                    last.then_inc(bs["at"], 1)
                b_router(b, 2, (7,), router_second)
                if n: b_scores(b + 1, 1 - p, 3)
                if nnn: b_kv(b + 3)
                if l and c: pe.wait_ge(bs["attT"], b)
                if c:
                    pe.wait_ge(bs["ot"], b * 4 + 2)
                    b_values(b, p, 2)
                    b_scoresT(b, p, 3)
                    pe.wait_ge(bs["ot"], b * 4 + 3)
                b_router(b, 3, (7,), router_first)
                b_router(b, 0, (8,), router_first)
                if l:
                    if not c: pe.wait_ge(bs["attT"], b)
                    for u in range(2):
                        last = pe.matmul(pb[1][:, u * D:(u + 1) * D], attT[:, u, :], wo[:, :], start=True, stop=True)
                    last.then_inc(bs["y"], 1)
                if n:
                    pe.wait_ge(bs["ms"], b + 2)
                    for u in range(2):
                        last = pe.transpose(pb[2][:, 0:P].bitcast(BF16)[:, u * P:(u + 1) * P], ms[:, u, :], identb[:, :])
                    last.then_inc(bs["mt"], 1)
                b_router(b, 3, (7,), router_second)
                b_router(b, 0, (8,), router_second)

            def router_first(h):
                if h in (1, 2):
                    pe.wait_ge(bs["max"], 12 * (h + 5))
                if h in (1, 2, 3):
                    pe.wait_ge(bs["mT"], h + 5)
                if h == 2:
                    pe.wait_ge(pool_const, 6)
                if there(h - 2):
                    waits(pe, ffn[1]["pos"], h - 2)
                    logits(1, h - 2, h % 2, pb[3])
                if there(h - 1):
                    waits(pe, norm[3]["xnT"], h - 1)
                    norm_transpose(3, h - 1, (h - 1) % 2, pb[2])

            def router_second(h):
                if there(h - 2):
                    ranks(1, h - 2, pb[3])

            def b_router(b, point, rounds, what):
                if isinstance(b, int) and b in rounds:
                    what(router_at(b, point))

            pe.wait_ge(b_loaded, 80)
            pe.wait_ge(bs["const"], 3)
            pe.wait_ge(copied, len(copies))
            pe.wait_ge(bs["zero"], 1)
            for c in range(B):
                norm_transpose(2, c, c % 2, pb[2 + c % 2])
                if c == 0: b_q(0, 0)
                if c == 1: b_kv(0)
                if c == 2:
                    pe.wait_ge(bs["turnk"], 1)
                    pe.wait_ge(bs["v"], 1)
                    b_q(1, 1)
                if c == 4:
                    b_kv(1)
            b_rounds(pe, b_round)
            for h in range(B, B + 2):
                router_first(h)
                router_second(h)
            totals(1)
            ffn_tiles(1)


def _constants():
    i = np.arange(P)
    cols = {}
    cols["ident"] = np.eye(P)
    cols["pick"] = np.concatenate([np.eye(P) * ((i // VA) % 2 == jj)[:, None] for jj in range(2)], 1)
    inv = 1.0 / 10000.0 ** (np.arange(0, DB, 2, dtype=np.float32) / DB)
    ang = np.outer(np.arange(T, dtype=np.float32), inv)
    cos, sin = np.repeat(np.cos(ang), 2, 1), np.repeat(np.sin(ang), 2, 1)
    sin[:, 0::2] *= -1
    page = np.arange(T)[:, None] // PAGE
    pages = np.arange(NPG)[None, :]
    zero = np.zeros((T, 8))
    qmask = np.concatenate([np.where(page < pages, MASKED, 0.0), zero], 1)
    kmask = np.concatenate([page == pages, zero], 1)
    for name, c in (("cos", cos), ("sin", sin), ("qmask", qmask), ("kmask", kmask)):
        cols[name] = np.concatenate([c[:P], c[P:]], 1)
    cols["order"] = np.tile(NE - np.arange(NE), (P, 1))
    cols["region"] = np.tile(REGION * np.arange(NE), (P, 1))
    cols["steps"] = np.tile(P * np.arange(NT), (P, 1))
    cols["slots"] = np.tile(np.arange(SLOTS), (P, 1))
    cols["ones"] = np.ones((P, P))
    cols["before"] = np.triu(np.ones((P, P)), 1)
    return cols


def _select():
    s = np.zeros((P, HB, P), np.float32)
    for h in range(HB):
        s[3 * h:3 * h + 3, h, :] = 1.0
    return s.reshape(P, HB * P)


CST, NCST = {}, 0
for _name, _c in _constants().items():
    CST[_name] = (NCST, NCST + _c.shape[1])
    NCST += _c.shape[1]


_INS = ["L0_attn_a_x", "L0_attn_a_Mq", "L0_attn_a_Mk", "L0_attn_a_Mv", "L0_attn_b_wq", "L0_attn_b_w_down",
        "L0_attn_b_wk_up", "L0_attn_b_wv_up", "L0_attn_b_wo", "L0_ffn_w_gate", "L0_ffn_b_gate", "L0_ffn_W1",
        "L0_ffn_b1", "L0_ffn_W2", "L0_ffn_b2"]


def kernel(**inputs):
    import concourse.bacc as _bacc
    from concourse.bass_utils import run_bass_kernel_spmd as _run

    nc = _bacc.Bacc("TRN2", target_bir_lowering=False, num_devices=1)
    arrays = {f"in_{n}": np.ascontiguousarray(inputs[n]) for n in _INS}
    arrays["in_constants"] = np.concatenate(list(_constants().values()), 1).astype(np.float32)
    arrays["in_select"] = _select()
    args = [nc.dram_tensor(n, a.shape, mybir.dt.from_np(a.dtype), kind="ExternalInput").ap()
            for n, a in arrays.items()]
    out = nc.dram_tensor("out_0", (B, T, D), F32, kind="ExternalOutput").ap()
    xs = nc.dram_tensor("slots", (ROWS, D), F32).ap()
    build(nc, *args, out, xs)
    r = _run(nc, [arrays], core_ids=[0])
    return r.results[0]["out_0"]
```
